# Optimizing a Trainium2 kernel written in Bass

```python
import numpy as np
import jax
import jax.numpy as jnp

def _softmax(x, axis=-1):
    return jax.nn.softmax(x, axis=axis)

def _gelu(x):
    return jax.nn.gelu(x, approximate=True)

def _silu(x):
    return jax.nn.silu(x)

def _sigmoid(x):
    return jax.nn.sigmoid(x)

def _layernorm(x, axis=-1, eps=1e-05):
    m = jnp.mean(x, axis=axis, keepdims=True)
    v = jnp.var(x, axis=axis, keepdims=True)
    return (x - m) / jnp.sqrt(v + eps)

def _scatter_add(tgt, idx, src, axis=0):
    return tgt.at[idx].add(src)

def _segment_sum(src, seg, n):
    return jax.ops.segment_sum(src, seg, n)
kernel_name = 'mk_prb_d1_jaxref_r8_73f4d4'

def setup_inputs(seed: int=0):
    np.random.seed(seed)
    _w = jnp.asarray

    def _L0_attn_setup():
        import jax, jax.numpy as jnp
        import numpy as np
        LN_EPS = 1e-05

        def _layernorm(x, g, b):
            mu = jnp.mean(x, axis=-1, keepdims=True)
            var = jnp.var(x, axis=-1, keepdims=True)
            return (x - mu) * jax.lax.rsqrt(var + LN_EPS) * g + b
        key = jax.random.key(seed)
        B, S, D, H = (2, 256, 128, 16)
        dh = D // H
        r = 48
        r_out = 96
        I = 4 * D
        r_mlp = 64
        ks = jax.random.split(key, 24)
        sc = lambda *sh: 0.02
        inp = {'hidden_states': jax.random.normal(ks[0], (B, S, D), jnp.float32), 'ln1_g': jnp.ones((D,), jnp.float32), 'ln1_b': jnp.zeros((D,), jnp.float32), 'ln2_g': jnp.ones((D,), jnp.float32), 'ln2_b': jnp.zeros((D,), jnp.float32), 'q_U': jax.random.normal(ks[1], (D, H, r), jnp.float32) * 0.02, 'q_V': jax.random.normal(ks[2], (H, r, dh), jnp.float32) * 0.02, 'q_b': jax.random.normal(ks[3], (H, dh), jnp.float32) * 0.02, 'k_U': jax.random.normal(ks[4], (D, H, r), jnp.float32) * 0.02, 'k_V': jax.random.normal(ks[5], (H, r, dh), jnp.float32) * 0.02, 'k_b': jax.random.normal(ks[6], (H, dh), jnp.float32) * 0.02, 'v_U': jax.random.normal(ks[7], (D, H, r), jnp.float32) * 0.02, 'v_V': jax.random.normal(ks[8], (H, r, dh), jnp.float32) * 0.02, 'v_b': jax.random.normal(ks[9], (H, dh), jnp.float32) * 0.02, 'out_U': jax.random.normal(ks[10], (D, r_out), jnp.float32) * 0.02, 'out_V': jax.random.normal(ks[11], (r_out, D), jnp.float32) * 0.02, 'out_b': jnp.zeros((D,), jnp.float32), 'fc1_U': jax.random.normal(ks[12], (D, r_mlp), jnp.float32) * 0.02, 'fc1_V': jax.random.normal(ks[13], (r_mlp, I), jnp.float32) * 0.02, 'fc1_b': jnp.zeros((I,), jnp.float32), 'fc2_U': jax.random.normal(ks[14], (I, r_mlp), jnp.float32) * 0.02, 'fc2_V': jax.random.normal(ks[15], (r_mlp, D), jnp.float32) * 0.02, 'fc2_b': jnp.zeros((D,), jnp.float32)}
        return inp
    _L0_attn_in = _L0_attn_setup()

    def _L0_ffn_setup():
        import jax, jax.numpy as jnp
        import numpy as np
        NUM_EXPERTS_TOTAL = 9
        TOP_K = 2
        key = jax.random.key(seed)
        k0, k1, k2, k3, k4 = jax.random.split(key, 5)
        B, S, H, I = (2, 256, 128, 352)
        E = NUM_EXPERTS_TOTAL
        x = jax.random.normal(k0, (B, S, H), dtype=jnp.float32)
        Wr = jax.random.normal(k1, (H, E), dtype=jnp.float32) * 0.02
        Wg = jax.random.normal(k2, (E, H, I), dtype=jnp.float32) * 0.02
        Wu = jax.random.normal(k3, (E, H, I), dtype=jnp.float32) * 0.02
        Wd = jax.random.normal(k4, (E, I, H), dtype=jnp.float32) * 0.02
        return {'x': x, 'Wr': Wr, 'Wg': Wg, 'Wu': Wu, 'Wd': Wd}
    _L0_ffn_in = _L0_ffn_setup()
    _d = {'L0_attn_hidden_states': _L0_attn_in['hidden_states'], 'L0_attn_ln1_g': _L0_attn_in['ln1_g'], 'L0_attn_ln1_b': _L0_attn_in['ln1_b'], 'L0_attn_ln2_g': _L0_attn_in['ln2_g'], 'L0_attn_ln2_b': _L0_attn_in['ln2_b'], 'L0_attn_q_U': _L0_attn_in['q_U'], 'L0_attn_q_V': _L0_attn_in['q_V'], 'L0_attn_q_b': _L0_attn_in['q_b'], 'L0_attn_k_U': _L0_attn_in['k_U'], 'L0_attn_k_V': _L0_attn_in['k_V'], 'L0_attn_k_b': _L0_attn_in['k_b'], 'L0_attn_v_U': _L0_attn_in['v_U'], 'L0_attn_v_V': _L0_attn_in['v_V'], 'L0_attn_v_b': _L0_attn_in['v_b'], 'L0_attn_out_U': _L0_attn_in['out_U'], 'L0_attn_out_V': _L0_attn_in['out_V'], 'L0_attn_out_b': _L0_attn_in['out_b'], 'L0_attn_fc1_U': _L0_attn_in['fc1_U'], 'L0_attn_fc1_V': _L0_attn_in['fc1_V'], 'L0_attn_fc1_b': _L0_attn_in['fc1_b'], 'L0_attn_fc2_U': _L0_attn_in['fc2_U'], 'L0_attn_fc2_V': _L0_attn_in['fc2_V'], 'L0_attn_fc2_b': _L0_attn_in['fc2_b'], 'L0_ffn_Wr': _L0_ffn_in['Wr'], 'L0_ffn_Wg': _L0_ffn_in['Wg'], 'L0_ffn_Wu': _L0_ffn_in['Wu'], 'L0_ffn_Wd': _L0_ffn_in['Wd']}
    _x0 = _d['L0_attn_hidden_states']
    _d['L0_attn_hidden_states'] = jax.random.normal(jax.random.fold_in(jax.random.key(seed), 1), (32, 256, 128), dtype=_x0.dtype)
    del _x0
    return _d

def reference(L0_attn_hidden_states, L0_attn_ln1_g, L0_attn_ln1_b, L0_attn_ln2_g, L0_attn_ln2_b, L0_attn_q_U, L0_attn_q_V, L0_attn_q_b, L0_attn_k_U, L0_attn_k_V, L0_attn_k_b, L0_attn_v_U, L0_attn_v_V, L0_attn_v_b, L0_attn_out_U, L0_attn_out_V, L0_attn_out_b, L0_attn_fc1_U, L0_attn_fc1_V, L0_attn_fc1_b, L0_attn_fc2_U, L0_attn_fc2_V, L0_attn_fc2_b, L0_ffn_Wr, L0_ffn_Wg, L0_ffn_Wu, L0_ffn_Wd):

    def _L0_attn_ref(hidden_states, ln1_g, ln1_b, ln2_g, ln2_b, q_U, q_V, q_b, k_U, k_V, k_b, v_U, v_V, v_b, out_U, out_V, out_b, fc1_U, fc1_V, fc1_b, fc2_U, fc2_V, fc2_b):
        import jax, jax.numpy as jnp
        import numpy as np
        LN_EPS = 1e-05

        def _layernorm(x, g, b):
            mu = jnp.mean(x, axis=-1, keepdims=True)
            var = jnp.var(x, axis=-1, keepdims=True)
            return (x - mu) * jax.lax.rsqrt(var + LN_EPS) * g + b
        B, S, D = hidden_states.shape
        H, dh = (q_V.shape[0], q_V.shape[2])
        x = _layernorm(hidden_states, ln1_g, ln1_b)
        Q = jnp.einsum('bsd,dhr,hre->bhse', x, q_U, q_V) + q_b[None, :, None, :]
        Pk = jnp.einsum('bsd,dhr->bhsr', x, k_U)
        Pv = jnp.einsum('bsd,dhr->bhsr', x, v_U)
        K = jnp.einsum('bhsr,hrd->bhsd', Pk, k_V) + k_b[None, :, None, :]
        V = jnp.einsum('bhsr,hrd->bhsd', Pv, v_V) + v_b[None, :, None, :]
        scale = 1.0 / jnp.sqrt(jnp.asarray(dh, x.dtype))
        scores = jnp.einsum('bhse,bhte->bhst', Q, K) * scale
        causal = jnp.tril(jnp.ones((S, S), bool))
        scores = jnp.where(causal[None, None], scores, jnp.asarray(-1000000000.0, scores.dtype))
        attn = jax.nn.softmax(scores, axis=-1)
        ctx = jnp.einsum('bhst,bhtd->bhsd', attn, V)
        ctx = ctx.transpose(0, 2, 1, 3).reshape(B, S, D)
        attn_out = ctx @ out_U @ out_V + out_b
        h = hidden_states + attn_out
        x2 = _layernorm(h, ln2_g, ln2_b)
        hmid = jax.nn.gelu(x2 @ fc1_U @ fc1_V + fc1_b, approximate=True)
        mlp_out = hmid @ fc2_U @ fc2_V + fc2_b
        return h + mlp_out

    def _L0_ffn_ref(x, Wr, Wg, Wu, Wd):
        import jax, jax.numpy as jnp
        import numpy as np
        NUM_EXPERTS_TOTAL = 9
        TOP_K = 2
        B, S, H = x.shape
        E = NUM_EXPERTS_TOTAL
        T = B * S
        logits = jnp.einsum('bsh,he->bse', x, Wr)
        probs = jax.nn.softmax(logits, axis=-1)
        topk_w, topk_idx = jax.lax.top_k(probs, TOP_K)
        topk_w = topk_w / jnp.sum(topk_w, axis=-1, keepdims=True)
        xf = x.reshape(T, H)
        wf = topk_w.reshape(T, TOP_K)
        idxf = topk_idx.reshape(T, TOP_K)
        cw = jnp.zeros((T, E), dtype=x.dtype).at[jnp.arange(T)[:, None], idxf].add(wf)
        gate = jax.nn.silu(jnp.einsum('th,ehi->tei', xf, Wg))
        hidden = gate * jnp.einsum('th,ehi->tei', xf, Wu)
        out = jnp.einsum('tei,eih,te->th', hidden, Wd, cw)
        return out.reshape(B, S, H)
    x = L0_attn_hidden_states
    xn = _layernorm(x, axis=-1)
    x = x + _L0_attn_ref(xn, L0_attn_ln1_g, L0_attn_ln1_b, L0_attn_ln2_g, L0_attn_ln2_b, L0_attn_q_U, L0_attn_q_V, L0_attn_q_b, L0_attn_k_U, L0_attn_k_V, L0_attn_k_b, L0_attn_v_U, L0_attn_v_V, L0_attn_v_b, L0_attn_out_U, L0_attn_out_V, L0_attn_out_b, L0_attn_fc1_U, L0_attn_fc1_V, L0_attn_fc1_b, L0_attn_fc2_U, L0_attn_fc2_V, L0_attn_fc2_b) + _L0_ffn_ref(xn, L0_ffn_Wr, L0_ffn_Wg, L0_ffn_Wu, L0_ffn_Wd)
    return x

_drawn_inputs = setup_inputs


def setup_inputs(seed=0):
    import zlib

    import numpy as np

    out = dict(_drawn_inputs(seed))
    spreads = {'L0_attn_ln1_g': (1.0, 0.6),
     'L0_attn_ln1_b': (0.0, 0.8),
     'L0_attn_ln2_g': (1.0, 0.6),
     'L0_attn_ln2_b': (0.0, 0.8),
     'L0_attn_out_b': (0.0, 0.784),
     'L0_attn_fc1_b': (0.0, 0.8),
     'L0_attn_fc2_b': (0.0, 0.8)}
    factors = {'L0_attn_q_U': 8.0,
     'L0_attn_q_V': 8.0,
     'L0_attn_q_b': 8.0,
     'L0_attn_k_U': 8.0,
     'L0_attn_k_V': 8.0,
     'L0_attn_k_b': 64.0,
     'L0_attn_v_U': 8.0,
     'L0_attn_v_V': 8.0,
     'L0_attn_v_b': 8.0,
     'L0_attn_out_U': 8.0,
     'L0_attn_out_V': 8.0,
     'L0_attn_fc1_U': 8.0,
     'L0_attn_fc1_V': 8.0,
     'L0_attn_fc2_U': 8.0,
     'L0_attn_fc2_V': 8.0,
     'L0_ffn_Wr': 8.0,
     'L0_ffn_Wg': 8.0,
     'L0_ffn_Wu': 8.0,
     'L0_ffn_Wd': 8.0}
    for name, (base, spread) in spreads.items():
        noise = np.random.default_rng([zlib.crc32(name.encode()), seed]).standard_normal(out[name].shape)
        drawn = base * np.exp(spread * noise) if base else spread * noise
        out[name] = jnp.asarray(drawn.astype(out[name].dtype))
    for name, factor in factors.items():
        out[name] = (out[name] * factor).astype(out[name].dtype)
    return out
```

```python
from collections import namedtuple
from contextlib import ExitStack

import concourse.bass as bass
from concourse import mybir

F32 = mybir.dt.float32
F32R = mybir.dt.float32r
BF16 = mybir.dt.bfloat16
I32 = mybir.dt.int32
U32 = mybir.dt.uint32
ALU = mybir.AluOpType
ACT = mybir.ActivationFunctionType
AX = mybir.AxisListType
ds = bass.ds

P = 128
SEQ = 256
CHUNK = 512
TPC = CHUNK // P
HEADS, DH = 16, 8
LANES = 4
GROUPS = HEADS // LANES
ROWS = 24
LN_EPS = 1e-5
MASKED = -1e30
EXPERTS, FF = 9, 352
FF_CHUNKS = ((0, 128), (128, 128), (256, 96))
HID = 512
HCH = HID // P
RANK_QKV, RANK_OUT, RANK_MLP = 48, 96, 64

Step = namedtuple("Step", "index parity turn")


def at(half, d):
    return Step(2 * half + d, d % 2, half + d // 2)


def layer_kernel(nc, x_in, w, out):
    tokens = x_in.shape[0] * x_in.shape[1]
    tiles = tokens // P
    chunks = tokens // CHUNK
    slot_tiles = (2 * tokens + EXPERTS * (P - 1)) // P
    slots = slot_tiles * P

    x_rows = x_in.rearrange("b s d -> (b s) d")
    out_rows = out.rearrange("b s d -> (b s) d")
    x_tiles = x_rows.rearrange("(n p) d -> p n d", p=P)
    out_tiles = out_rows.rearrange("(n p) d -> p n d", p=P)

    xn_dram = nc.dram_tensor("xn_scratch", [tokens, P], F32, kind="Internal").ap()
    xt_dram = nc.dram_tensor("xt_scratch", [chunks * P, CHUNK], F32, kind="Internal").ap()
    slot_x = nc.dram_tensor("slot_x", [slots, P], F32, kind="Internal").ap()
    slot_y = nc.dram_tensor("slot_y", [slots, P], F32, kind="Internal").ap()
    xn_tiles = xn_dram.rearrange("(n p) d -> p n d", p=P)

    whole = ExitStack()

    def keep(name, shape, dtype=F32):
        return whole.enter_context(nc.sbuf_tensor(name, shape, dtype))

    with whole:
        ident = keep("ident", [P, P])
        wq = keep("wq", [P, P])
        wk = keep("wk", [P, P])
        wv = keep("wv", [P, P])
        wo = keep("wo", [P, P])
        w1 = keep("w1", [P, HID])
        w2 = keep("w2", [P, HCH, P])
        q_bias = keep("q_bias", [P, 1])
        k_bias = keep("k_bias", [P, 1])
        v_bias = keep("v_bias", [P, TPC, P])
        mlp_bias = keep("mlp_bias", [P, HCH])
        out_bias = keep("out_bias", [P, TPC, P])
        fc2_bias = keep("fc2_bias", [P, TPC, P])
        w_gate_up = keep("w_gate_up", [P, EXPERTS, 2 * FF])
        w_down = keep("w_down", [P, EXPERTS, len(FF_CHUNKS), P])
        mix = keep("mix", [P, tiles, 2])
        slot_of = keep("slot_of", [P, tiles * 2], U32)
        tile_expert = keep("tile_expert", [1, slot_tiles], I32)
        h_all = keep("h_all", [P, tiles * P])
        ln2_stats = keep("ln2_stats", [P, tiles * 6])

        prepare(nc, locals())
        attention(nc, locals())
        experts(nc, locals())
        mlp_and_combine(nc, locals())


class Scope:

    def __init__(self, nc, stack, prefix):
        self.nc, self.stack, self.prefix = nc, stack, prefix

    def sb(self, name, shape, dtype=F32):
        return self.stack.enter_context(self.nc.sbuf_tensor(f"{self.prefix}_{name}", shape, dtype))

    def two(self, name, shape, dtype=F32):
        return [self.sb(f"{name}{k}", shape, dtype) for k in range(2)]

    def ps(self, name, shape):
        return self.stack.enter_context(self.nc.psum_tensor(f"{self.prefix}_{name}", shape, F32))

    def sem(self, name):
        return self.stack.enter_context(self.nc.semaphore(f"{self.prefix}_{name}"))

    def two_sems(self, name):
        return [self.sem(f"{name}{k}") for k in range(2)]


def prepare(nc, env):
    w = env["w"]
    tiles, chunks, slot_tiles, slots = env["tiles"], env["chunks"], env["slot_tiles"], env["slots"]
    ident, wq, wk, wv, wo = env["ident"], env["wq"], env["wk"], env["wv"], env["wo"]
    w1, w2, w_gate_up, w_down = env["w1"], env["w2"], env["w_gate_up"], env["w_down"]
    q_bias, k_bias, v_bias, mlp_bias = env["q_bias"], env["k_bias"], env["v_bias"], env["mlp_bias"]
    out_bias, fc2_bias = env["out_bias"], env["fc2_bias"]
    mix, slot_of, tile_expert = env["mix"], env["slot_of"], env["tile_expert"]
    PAIRS = HEADS // 2
    PR = 2 * RANK_QKV
    cols = tiles * EXPERTS
    half = cols // 2

    with ExitStack() as stack:
        s = Scope(nc, stack, "prep")
        x_all = s.sb("x_all", [P, tiles, P])
        u_in = [s.sb(f"u_{n}", [P, HEADS * RANK_QKV]) for n in "qkv"]
        v_in = [s.sb(f"v_{n}", [PR, PAIRS, 2 * DH]) for n in "qkv"]
        out_u, out_v = s.sb("out_u", [P, RANK_OUT]), s.sb("out_v", [RANK_OUT, P])
        fc1_u, fc1_v = s.sb("fc1_u", [P, RANK_MLP]), s.sb("fc1_v", [RANK_MLP, HID])
        fc2_u, fc2_v = s.sb("fc2_u", [P, HCH, RANK_MLP]), s.sb("fc2_v", [RANK_MLP, P])
        w_router = s.sb("w_router", [P, EXPERTS])
        ln1_g, ln1_b = s.sb("ln1_g", [P, 1]), s.sb("ln1_b", [P, 1])
        ln2_g, ln2_b = s.sb("ln2_g", [P, 1]), s.sb("ln2_b", [P, 1])
        q_b, k_b, fc1_b = s.sb("q_b", [P, 1]), s.sb("k_b", [P, 1]), s.sb("fc1_b", [P, HCH])
        v_b = s.sb("v_b", [P, P])
        zeros = s.sb("zeros", [P, 1024])
        ones = s.sb("ones", [P, P])
        before = s.sb("before", [P, P])
        rev_e = s.sb("rev_e", [P, tiles, EXPERTS])
        tile_no_i, tile_no = s.sb("tile_no_i", [1, slot_tiles], I32), s.sb("tile_no", [1, slot_tiles])
        power = s.sb("power", [P, 2, tiles])
        ut = s.sb("ut", [P, 6, 4 * P])
        ut_small = s.sb("ut_small", [P, 2 * P])
        ut_fc2 = s.sb("ut_fc2", [RANK_MLP, HCH * P])
        raw_qkv, raw_w1 = s.sb("raw_qkv", [P, 3, P]), s.sb("raw_w1", [P, HID])
        g_q = s.sb("g_q", [P, 1])
        b_rows = s.sb("b_rows", [P, P])
        stats = s.sb("stats", [P, tiles, 6])
        mean, var, tmp = s.sb("mean", [P, tiles]), s.sb("var", [P, tiles]), s.sb("tmp", [P, tiles])
        rstd, rstd2, std2 = s.sb("rstd", [P, tiles]), s.sb("rstd2", [P, tiles]), s.sb("std2", [P, tiles])
        xn = s.two("xn", [P, TPC, P])
        xnr = s.two("xnr", [P, TPC, P])
        xt = s.two("xt", [P, CHUNK])
        logits = s.sb("logits", [P, tiles, EXPERTS])
        work = s.sb("work", [P, tiles, EXPERTS])
        pick = [s.sb(f"pick{k}", [P, tiles, EXPERTS]) for k in range(2)]
        top = [s.sb(f"top{k}", [P, tiles]) for k in range(2)]
        key = s.sb("key", [P, tiles])
        chosen, scan_a, scan_b = (s.sb(n, [P, tiles, EXPERTS]) for n in ("chosen", "scan_a", "scan_b"))
        gap, gap_exp, gap_sum = s.sb("gap", [P, tiles]), s.sb("gap_exp", [P, tiles]), s.sb("gap_sum", [P, tiles])
        count_f, count_i = s.sb("count_f", [P, EXPERTS]), s.sb("count_i", [P, EXPERTS], I32)
        run_tiles, end_a, end_b, base = (s.sb(n, [P, EXPERTS]) for n in ("run_tiles", "end_a", "end_b", "base"))
        past = s.sb("past", [1, slot_tiles, EXPERTS])
        expert_f = s.sb("expert_f", [1, slot_tiles])
        slot_f = s.sb("slot_f", [P, tiles, 2])

        XL = 4
        x_loaded = [s.sem(f"x_loaded{k}") for k in range(XL)]
        bank = [s.ps(f"bank{k}", [P, 512]) for k in range(8)]

        small_loaded, diag_loaded, experts_loaded = s.sem("small_loaded"), s.sem("diag_loaded"), s.sem("experts_loaded")
        zero_filled = s.sem("zero_filled")
        const_ready, diag_cleared = s.sem("const_ready"), s.sem("diag_cleared")
        fold_pe, fold_act = s.sem("fold_pe"), s.sem("fold_act")
        stats_done, var_ready, pow_done = s.sem("stats_done"), s.sem("var_ready"), s.sem("pow_done")
        ln_step = s.sem("ln_step")
        xn_ready, xnr_ready, xt_turned, xt_ready = s.sem("xn_ready"), s.sem("xnr_ready"), s.sem("xt_turned"), s.sem("xt_ready")
        xn_stored, xt_stored = s.two_sems("xn_stored"), s.two_sems("xt_stored")
        logits_ready, logits_copied = s.sem("logits_ready"), s.sem("logits_copied")
        route, gap_ready, gap_exped, counted = (s.sem(n) for n in ("route", "gap_ready", "gap_exped", "counted"))

        N_SMALL = 3 + 4 + 2 * LANES + 2 + 2 * TPC + 7
        N_DIAG = 6
        N_CONST = 9 + 8
        with nc.Block() as block:

            @block.sync
            def _(sp):
                n = tiles // XL
                for k in range(XL):
                    sp.dma_start(x_all[:, k * n:(k + 1) * n, :], env["x_tiles"][:, k * n:(k + 1) * n, :]).then_inc(x_loaded[k], 16)
                sp.wait_ge(const_ready, N_CONST)
                rows = slots * P // (P * 1024)
                flat = env["slot_x"].rearrange("(p n) d -> p (n d)", p=P)
                for k in range(rows):
                    sp.dma_start(flat[:, k * 1024:(k + 1) * 1024], zeros[:]).then_inc(zero_filled, 16)
                assert rows * 1024 * P == slots * P

                def store(c):
                    sp.wait_ge(xn_ready, c.index + 1)
                    sp.dma_start(env["xn_tiles"][:, ds(c.index * TPC, TPC), :], xn[c.parity][:]).then_inc(xn_stored[c.parity], 16)
                    sp.wait_ge(xt_ready, c.index + 1)
                    sp.dma_start(env["xt_dram"][ds(c.index * P, P), :], xt[c.parity][:]).then_inc(xt_stored[c.parity], 16)

                with sp.Fori(0, chunks // 2) as q:
                    store(at(q, 0))
                    store(at(q, 1))
                sp.wait_ge(zero_filled, 16 * rows)
                for k in range(2):
                    sp.wait_ge(xn_stored[k], 16 * chunks // 2)
                    sp.wait_ge(xt_stored[k], 16 * chunks // 2)
                sp.wait_ge(experts_loaded, 16 * (2 + len(FF_CHUNKS)))

            @block.gpsimd
            def _(pool):
                for k in range(3):
                    pool.memset(v_in[k][:], 0.0).then_inc(diag_cleared, 1)
                pool.memset(ident[:], 0.0).then_inc(const_ready, 1)
                pool.memset(ones[:], 1.0).then_inc(const_ready, 1)
                pool.wait_ge(const_ready, 2)
                pool.affine_select(out=ident[:], in_=ident[:], compare_op=ALU.not_equal, fill=1.0, base=0,
                                   pattern=[[-1, P]], channel_multiplier=1).then_inc(const_ready, 1)
                pool.affine_select(out=before[:], in_=ones[:], compare_op=ALU.is_ge, fill=0.0, base=-1,
                                   pattern=[[1, P]], channel_multiplier=-1).then_inc(const_ready, 1)
                pool.memset(zeros[:], 0.0).then_inc(const_ready, 1)
                pool.memset(power[:, 0, :], -0.5).then_inc(const_ready, 1)
                pool.memset(power[:, 1, :], 0.5).then_inc(const_ready, 1)
                for e in range(EXPERTS):
                    pool.memset(rev_e[:, :, e], float(EXPERTS - e)).then_inc(const_ready, 1)
                pool.iota(tile_no_i[:], pattern=[[1, slot_tiles]], base=0, channel_multiplier=0).then_inc(const_ready, 1)
                pool.wait_ge(const_ready, N_CONST)
                pool.wait_ge(var_ready, 1)
                pool.tensor_tensor(rstd[:], var[:], power[:, 0, :], ALU.pow).then_inc(pow_done, 1)
                pool.wait_ge(var_ready, 2)
                pool.tensor_tensor(rstd2[:], tmp[:], power[:, 0, :], ALU.pow).then_inc(pow_done, 1)
                pool.tensor_tensor(std2[:], tmp[:], power[:, 1, :], ALU.pow).then_inc(pow_done, 1)

            @block.scalar
            def _(act):
                small = [0]

                def load(dst, src, columns=False):
                    act.dma_start(dst, src, allow_slow_non_contiguous=columns).then_inc(small_loaded, 16)
                    small[0] += 16

                for k, n in enumerate("qkv"):
                    load(u_in[k][:], w[f"{n}_U"].rearrange("d h r -> d (h r)"))
                act.wait_ge(diag_cleared, 3)
                for k, n in enumerate("qkv"):
                    by_pair = w[f"{n}_V"].rearrange("(j two) r e -> two r j e", two=2)
                    for b in range(2):
                        act.dma_start(v_in[k][b * RANK_QKV:(b + 1) * RANK_QKV, :, b * DH:(b + 1) * DH],
                                      by_pair[b]).then_inc(diag_loaded, 16)
                for dst, name in ((ln1_g, "ln1_g"), (ln1_b, "ln1_b"), (ln2_g, "ln2_g"), (ln2_b, "ln2_b")):
                    load(dst[:], w[name].rearrange("(p o) -> p o", o=1), True)
                for dst, name in ((q_b, "q_b"), (k_b, "k_b")):
                    by_lane = w[name].rearrange("(g i) (e o) -> i e g o", i=LANES, o=1)
                    for i in range(LANES):
                        load(dst[32 * i:32 * i + 32, :], by_lane[i], True)
                load(fc1_b[:], w["fc1_b"].rearrange("(c p) -> p c", p=P), True)
                load(v_b[:], w["v_b"].rearrange("h e -> (h e)").partition_broadcast(P))
                for t in range(TPC):
                    load(out_bias[:, t, :], w["out_b"].partition_broadcast(P))
                    load(fc2_bias[:, t, :], w["fc2_b"].partition_broadcast(P))
                load(out_u[:], w["out_U"])
                load(out_v[:], w["out_V"])
                load(fc1_u[:], w["fc1_U"])
                load(fc1_v[:], w["fc1_V"])
                load(fc2_u[:], w["fc2_U"].rearrange("(c p) r -> p c r", p=P))
                load(fc2_v[:], w["fc2_V"])
                load(w_router[:], w["Wr"])
                act.dma_start(w_gate_up[:, :, 0:FF], w["Wg"].rearrange("e d i -> d e i")).then_inc(experts_loaded, 16)
                act.dma_start(w_gate_up[:, :, FF:2 * FF], w["Wu"].rearrange("e d i -> d e i")).then_inc(experts_loaded, 16)
                for c, (at_row, n) in enumerate(FF_CHUNKS):
                    act.dma_start(w_down[0:n, :, c, :], w["Wd"][:, at_row:at_row + n, :].rearrange("e p d -> p e d")).then_inc(experts_loaded, 16)

                for r in range(6):
                    act.wait_ge(fold_pe, r + 1)
                    act.copy(ut[0:PR, r, :], bank[r][0:PR, :]).then_inc(fold_act, 1)
                act.wait_ge(fold_pe, 7)
                act.copy(ut_small[0:RANK_OUT, 0:P], bank[7][0:RANK_OUT, 0:P]).then_inc(fold_act, 1)
                act.copy(ut_small[0:RANK_MLP, P:2 * P], bank[7][0:RANK_MLP, P:2 * P]).then_inc(fold_act, 1)
                act.wait_ge(fold_pe, 8)
                act.copy(ut_fc2[:], bank[0][0:RANK_MLP, :]).then_inc(fold_act, 1)
                assert small[0] == 16 * N_SMALL
                act.wait_ge(small_loaded, 16 * N_SMALL)
                act.wait_ge(fold_pe, 9)
                for k in range(2):
                    act.copy(raw_qkv[:, k, :].rearrange("p (i e g) -> p g i e", i=LANES, e=DH),
                             bank[6][:, k * P:(k + 1) * P].rearrange("p (g i e) -> p g i e", i=LANES, e=DH)).then_inc(fold_act, 1)
                act.copy(raw_qkv[:, 2, :], bank[6][:, 2 * P:3 * P]).then_inc(fold_act, 1)
                act.mul(g_q[:], ln1_g[:], float(DH) ** -0.5).then_inc(fold_act, 1)
                act.wait_ge(fold_pe, 10)
                act.copy(wo[:], bank[1][:, 0:P]).then_inc(fold_act, 1)
                act.wait_ge(fold_pe, 11)
                act.copy(raw_w1[:], bank[2][:]).then_inc(fold_act, 1)
                act.wait_ge(fold_pe, 12)
                act.copy(w2[:].rearrange("p c d -> p (c d)"), bank[3][:]).then_inc(fold_act, 1)
                act.wait_ge(fold_act, 16)
                act.activation(wq[:], raw_qkv[:, 0, :], ACT.Identity, scale=g_q[:]).then_inc(fold_act, 1)
                act.activation(wk[:], raw_qkv[:, 1, :], ACT.Identity, scale=ln1_g[:]).then_inc(fold_act, 1)
                act.activation(wv[:], raw_qkv[:, 2, :], ACT.Identity, scale=ln1_g[:]).then_inc(fold_act, 1)
                act.activation(w1[:], raw_w1[:], ACT.Identity, scale=ln2_g[:]).then_inc(fold_act, 1)
                act.wait_ge(const_ready, N_CONST)
                act.activation(b_rows[:], ones[:], ACT.Identity, scale=ln1_b[:]).then_inc(fold_act, 1)

                def copy_xt(c, first):
                    act.wait_ge(xt_turned, c.index + 1)
                    if not first:
                        act.wait_ge(xt_stored[c.parity], 16 * c.turn)
                    act.copy(xt[c.parity][:], bank[c.parity][:]).then_inc(xt_ready, 1)

                copy_xt(at(0, 0), True)
                copy_xt(at(0, 1), True)
                with act.Fori(1, chunks // 2) as q:
                    copy_xt(at(q, 0), False)
                    copy_xt(at(q, 1), False)
                act.wait_ge(gap_ready, 1)
                act.activation(gap_exp[:], gap[:], ACT.Exp).then_inc(gap_exped, 1)

            @block.tensor
            def _(pe):
                pe.wait_ge(const_ready, N_CONST)
                pe.wait_ge(small_loaded, 16 * N_SMALL)
                pe.wait_ge(diag_loaded, 16 * N_DIAG)
                for r in range(6):
                    for j in range(4):
                        pair = 4 * (r % 2) + j
                        last = pe.transpose(bank[r][0:PR, j * P:(j + 1) * P], u_in[r // 2][:, pair * PR:(pair + 1) * PR], ident[:])
                    last.then_inc(fold_pe, 1)
                pe.transpose(bank[7][0:RANK_OUT, 0:P], out_u[:], ident[:])
                pe.transpose(bank[7][0:RANK_MLP, P:2 * P], fc1_u[:], ident[:]).then_inc(fold_pe, 1)
                pe.wait_ge(fold_act, 1)
                for c in range(HCH):
                    last = pe.transpose(bank[0][0:RANK_MLP, c * P:(c + 1) * P], fc2_u[:, c, :], ident[:])
                last.then_inc(fold_pe, 1)
                for r in range(6):
                    pe.wait_ge(fold_act, r + 1)
                    for j in range(4):
                        pair = 4 * (r % 2) + j
                        col = (r // 2) * P + pair * 2 * DH
                        last = pe.matmul(bank[6][:, col:col + 2 * DH], ut[0:PR, r, j * P:(j + 1) * P],
                                         v_in[r // 2][:, pair, :], start=True, stop=True)
                last.then_inc(fold_pe, 1)
                pe.wait_ge(fold_act, 8)
                pe.matmul(bank[1][:, 0:P], ut_small[0:RANK_OUT, 0:P], out_v[:], start=True, stop=True).then_inc(fold_pe, 1)
                pe.matmul(bank[2][:], ut_small[0:RANK_MLP, P:2 * P], fc1_v[:], start=True, stop=True).then_inc(fold_pe, 1)
                pe.wait_ge(fold_act, 9)
                for c in range(HCH):
                    last = pe.matmul(bank[3][:, c * P:(c + 1) * P], ut_fc2[:, c * P:(c + 1) * P], fc2_v[:], start=True, stop=True)
                last.then_inc(fold_pe, 1)
                pe.wait_ge(fold_act, 21)
                pe.matmul(bank[4][:, 0:1], raw_qkv[:, 0, :], ln1_b[:], start=True, stop=True)
                pe.matmul(bank[4][:, 1:2], raw_qkv[:, 1, :], ln1_b[:], start=True, stop=True)
                for c in range(HCH):
                    pe.matmul(bank[4][:, 2 + c:3 + c], raw_w1[:, c * P:(c + 1) * P], ln2_b[:], start=True, stop=True)
                pe.matmul(bank[5][:, 0:P], b_rows[:], raw_qkv[:, 2, :], start=True, stop=True).then_inc(fold_pe, 1)

                def turn(c, first):
                    pe.wait_ge(xnr_ready, c.index + 1)
                    if not first:
                        pe.wait_ge(xt_ready, c.index - 1)
                    for t in range(TPC):
                        last = pe.transpose(bank[c.parity][:, t * P:(t + 1) * P], xnr[c.parity][:, t, :], ident[:])
                    last.then_inc(xt_turned, 1)

                def score(c, first):
                    pe.wait_ge(xt_ready, c.index + 1)
                    if not first:
                        pe.wait_ge(logits_copied, c.index - 1)
                    for t in range(TPC):
                        last = pe.matmul(bank[2 + c.parity][:, t * EXPERTS:(t + 1) * EXPERTS], xt[c.parity][:, t * P:(t + 1) * P],
                                         w_router[:], start=True, stop=True)
                    last.then_inc(logits_ready, 1)

                turn(at(0, 0), True)
                turn(at(0, 1), True)
                score(at(0, 0), True)
                turn(at(0, 2), False)
                score(at(0, 1), True)
                with pe.Fori(1, chunks // 2 - 1) as q:
                    turn(at(q, 1), False)
                    score(at(q, 0), False)
                    turn(at(q, 2), False)
                    score(at(q, 1), False)
                q = chunks // 2 - 1
                turn(at(q, 1), False)
                score(at(q, 0), False)
                score(at(q, 1), False)
                pe.wait_ge(gap_ready, 1)
                flat = chosen[:].rearrange("p t e -> p (t e)")
                for k in range(2):
                    pe.matmul(bank[4 + k][:, 0:half], before[:], flat[:, k * half:(k + 1) * half], start=True, stop=True)
                    last = pe.matmul(bank[6 + k][:, 0:half], ones[:], flat[:, k * half:(k + 1) * half], start=True, stop=True)
                last.then_inc(counted, 1)

            @block.vector
            def _(dve):
                n = tiles // XL
                for k in range(XL):
                    dve.wait_ge(x_loaded[k], 16)
                    with dve.Fori(k * n, (k + 1) * n) as t:
                        dve.bn_stats(stats[:].rearrange("p t c -> p (t c)")[:, ds(t * 6, 6)],
                                     x_all[:].rearrange("p t d -> p (t d)")[:, ds(t * P, P)]).then_inc(stats_done, 1)
                dve.wait_ge(stats_done, tiles)
                steps = [0]

                def step(ins):
                    steps[0] += 1
                    ins.then_inc(ln_step, 1)
                    dve.wait_ge(ln_step, steps[0])

                step(dve.tensor_tensor(mean[:], stats[:, :, 1], stats[:, :, 4], ALU.add))
                step(dve.tensor_tensor(tmp[:], stats[:, :, 1], stats[:, :, 4], ALU.subtract))
                step(dve.tensor_tensor(var[:], stats[:, :, 2], stats[:, :, 5], ALU.add))
                step(dve.tensor_tensor(tmp[:], tmp[:], tmp[:], ALU.mult))
                step(dve.tensor_scalar(var[:], var[:], 1.0 / P, None, ALU.mult))
                step(dve.scalar_tensor_tensor(out=var[:], in0=tmp[:], scalar=0.25, in1=var[:], op0=ALU.mult, op1=ALU.add))
                step(dve.tensor_scalar(mean[:], mean[:], 0.5, None, ALU.mult))
                step(dve.tensor_scalar(std2[:], var[:], 1.0, None, ALU.mult))
                dve.tensor_scalar(var[:], var[:], LN_EPS, None, ALU.add).then_inc(var_ready, 1)
                dve.wait_ge(pow_done, 1)
                step(dve.tensor_tensor(tmp[:], rstd[:], rstd[:], ALU.mult))
                step(dve.tensor_tensor(tmp[:], tmp[:], std2[:], ALU.mult))
                dve.tensor_scalar(tmp[:], tmp[:], LN_EPS, None, ALU.add).then_inc(var_ready, 1)
                dve.wait_ge(pow_done, 3)

                def normalise(c, first):
                    if not first:
                        dve.wait_ge(xn_stored[c.parity], 16 * c.turn)
                        dve.wait_ge(xt_turned, c.index - 1)
                    for t in range(TPC):
                        col = ds(c.index * TPC + t, 1)
                        last = dve.tensor_scalar(xn[c.parity][:, t, :], x_all[:].rearrange("p t d -> p (t d)")[:, ds((c.index * TPC + t) * P, P)],
                                                 mean[:, col], rstd[:, col], ALU.subtract, ALU.mult)
                    last.then_inc(xn_ready, 1)
                    dve.wait_ge(xn_ready, c.index + 1)
                    for t in range(TPC):
                        last = dve.tensor_scalar(xnr[c.parity][:, t, :], xn[c.parity][:, t, :], rstd2[:, ds(c.index * TPC + t, 1)], None, ALU.mult)
                    last.then_inc(xnr_ready, 1)

                def copy_logits(c):
                    dve.wait_ge(logits_ready, c.index + 1)
                    dve.tensor_tensor(logits[:].rearrange("p t e -> p (t e)")[:, ds(c.index * TPC * EXPERTS, TPC * EXPERTS)].rearrange("p (t e) -> p t e", e=EXPERTS),
                                      bank[2 + c.parity][:, 0:TPC * EXPERTS].rearrange("p (t e) -> p t e", e=EXPERTS),
                                      std2[:, ds(c.index * TPC, TPC)].unsqueeze(2).to_broadcast([P, TPC, EXPERTS]), ALU.mult).then_inc(logits_copied, 1)

                normalise(at(0, 0), True)
                normalise(at(0, 1), True)
                with dve.Fori(1, chunks // 2) as q:
                    normalise(at(q, 0), False)
                    copy_logits(at(q, -2))
                    normalise(at(q, 1), False)
                    copy_logits(at(q, -1))
                copy_logits(at(chunks // 2, -2))
                copy_logits(at(chunks // 2, -1))
                dve.wait_ge(logits_copied, chunks)

                dve.wait_ge(fold_pe, 13)
                dve.tensor_scalar(q_bias[:], bank[4][:, 0:1], q_b[:], float(DH) ** -0.5, ALU.add, ALU.mult)
                dve.tensor_tensor(k_bias[:], bank[4][:, 1:2], k_b[:], ALU.add)
                dve.tensor_tensor(mlp_bias[:], bank[4][:, 2:2 + HCH], fc1_b[:], ALU.add)
                for t in range(TPC):
                    dve.tensor_tensor(v_bias[:, t, :], bank[5][:, 0:P], v_b[:], ALU.add)

                routed = [0]

                def link(ins):
                    routed[0] += 1
                    ins.then_inc(route, 1)
                    dve.wait_ge(route, routed[0])

                def over_experts(a):
                    return a.unsqueeze(2).to_broadcast([P, tiles, EXPERTS])

                left = logits
                for k in range(2):
                    link(dve.tensor_reduce(top[k][:], left[:], AX.X, ALU.max))
                    link(dve.tensor_tensor(work[:], left[:], over_experts(top[k][:]), ALU.is_equal))
                    link(dve.tensor_tensor(work[:], work[:], rev_e[:], ALU.mult))
                    link(dve.tensor_reduce(key[:], work[:], AX.X, ALU.max))
                    link(dve.tensor_tensor(pick[k][:], rev_e[:], over_experts(key[:]), ALU.is_equal))
                    if k == 0:
                        link(dve.scalar_tensor_tensor(out=scan_a[:], in0=pick[0][:], scalar=-3e38, in1=logits[:], op0=ALU.mult, op1=ALU.add))
                        left = scan_a
                link(dve.tensor_tensor(chosen[:], pick[0][:], pick[1][:], ALU.add))
                dve.tensor_tensor(gap[:], top[1][:], top[0][:], ALU.subtract).then_inc(gap_ready, 1)
                dve.wait_ge(gap_exped, 1)
                link(dve.tensor_scalar(gap_sum[:], gap_exp[:], 1.0, None, ALU.add))
                link(dve.reciprocal(mix[:, :, 0], gap_sum[:]))
                link(dve.tensor_tensor(mix[:, :, 1], mix[:, :, 0], gap_exp[:], ALU.mult))
                dve.wait_ge(counted, 1)
                for k in range(2):
                    link(dve.tensor_copy(work[:].rearrange("p t e -> p (t e)")[:, k * half:(k + 1) * half], bank[6 + k][:, 0:half]))
                src, dst, far = work, scan_a, 1
                while far < tiles:
                    dve.tensor_copy(dst[:, 0:far, :], src[:, 0:far, :])
                    link(dve.tensor_tensor(dst[:, far:, :], src[:, far:, :], src[:, 0:tiles - far, :], ALU.add))
                    src, dst, far = dst, scan_b if dst is scan_a else scan_a, 2 * far
                link(dve.tensor_scalar(count_f[:], src[:, tiles - 1, :], float(P - 1), None, ALU.add))
                link(dve.tensor_copy(count_i[:], count_f[:]))
                link(dve.tensor_scalar(count_i[:], count_i[:], 7, None, ALU.arith_shift_right))
                link(dve.tensor_copy(run_tiles[:], count_i[:]))
                e_src, e_dst, far = run_tiles, end_a, 1
                while far < EXPERTS:
                    dve.tensor_copy(e_dst[:, 0:far], e_src[:, 0:far])
                    link(dve.tensor_tensor(e_dst[:, far:], e_src[:, far:], e_src[:, 0:EXPERTS - far], ALU.add))
                    e_src, e_dst, far = e_dst, end_b if e_dst is end_a else end_a, 2 * far
                link(dve.tensor_tensor(base[:], e_src[:], run_tiles[:], ALU.subtract))
                link(dve.tensor_scalar(base[:], base[:], float(P), None, ALU.mult))
                link(dve.tensor_tensor(work[:], src[:], work[:], ALU.subtract))
                link(dve.tensor_tensor(work[:], work[:], base[:].unsqueeze(1).to_broadcast([P, tiles, EXPERTS]), ALU.add))
                for k in range(2):
                    part = work[:].rearrange("p t e -> p (t e)")[:, k * half:(k + 1) * half]
                    link(dve.tensor_tensor(part, bank[4 + k][:, 0:half], part, ALU.add))
                for k in range(2):
                    link(dve.tensor_tensor(pick[k][:], pick[k][:], work[:], ALU.mult))
                    link(dve.tensor_reduce(slot_f[:, :, k], pick[k][:], AX.X, ALU.add))
                dve.tensor_copy(slot_of[:], slot_f[:].rearrange("p t k -> p (t k)"))
                link(dve.tensor_copy(tile_no[:], tile_no_i[:]))
                link(dve.tensor_tensor(past[:], tile_no[:].unsqueeze(2).to_broadcast([1, slot_tiles, EXPERTS]),
                                       e_src[0:1, :].unsqueeze(1).to_broadcast([1, slot_tiles, EXPERTS]), ALU.is_ge))
                link(dve.tensor_reduce(expert_f[:], past[:], AX.X, ALU.add))
                link(dve.tensor_scalar(expert_f[:], expert_f[:], float(EXPERTS - 1), None, ALU.min))
                link(dve.tensor_copy(tile_expert[:], expert_f[:]))


def attention(nc, env):
    chunks, slots = env["chunks"], env["slots"]
    ident, wq, wk, wv, wo = env["ident"], env["wq"], env["wk"], env["wv"], env["wo"]
    q_bias, k_bias, v_bias, out_bias = env["q_bias"], env["k_bias"], env["v_bias"], env["out_bias"]
    h_all, ln2_stats, slot_of = env["h_all"], env["ln2_stats"], env["slot_of"]
    UNITS = 12
    PT = 8

    with ExitStack() as stack:
        s = Scope(nc, stack, "att")
        ident_b = s.sb("ident_b", [P, P], BF16)
        mask_st = s.sb("mask_st", [P, LANES, P], BF16)
        mask_ts = s.sb("mask_ts", [P, LANES, P], BF16)
        ones = s.sb("ones", [P, CHUNK])
        xt = s.two("xt", [P, CHUNK])
        xn = s.two("xn", [P, TPC, P])
        x_out = s.two("x_out", [P, TPC, P])
        slot_now = s.two("slot_now", [P, 2 * TPC], U32)
        q_hi, q_lo, k_hi, k_lo = (s.sb(n, [P, CHUNK], F32R) for n in ("q_hi", "q_lo", "k_hi", "k_lo"))
        q_stack = s.two("q_stack", [P, GROUPS, CHUNK], F32R)
        k_stack = s.two("k_stack", [P, GROUPS, CHUNK], F32R)
        v_ones = s.two("v_ones", [P, TPC, HEADS, 32])
        row_max = s.two("row_max", [P, 2, HEADS])
        neg_max = [s.sb(f"neg_max{b}", [HEADS, SEQ], F32R) for b in range(2)]
        probs = s.sb("probs", [P, PT, CHUNK])
        ctx_t = s.sb("ctx_t", [P, GROUPS * SEQ])
        ctx_inv = s.sb("ctx_inv", [P, 2, HEADS])
        ctx = s.sb("ctx", [P, 2, P])
        ctx_turned = s.sb("ctx_turned", [P, SEQ])

        t_ps = [s.ps(f"t_ps{k}", [P, CHUNK]) for k in range(2)]
        m_ps = [s.ps(f"m_ps{k}", [P, CHUNK]) for k in range(2)]
        pv_ps = s.ps("pv_ps", [P, GROUPS * SEQ])
        free_ps = [s.ps(f"free_ps{k}", [P, CHUNK]) for k in range(2)]

        const_ready, rows_loaded = s.sem("const_ready"), s.sem("rows_loaded")
        v_cleared = s.sem("v_cleared")
        xt_loaded, xn_loaded = s.two_sems("xt_loaded"), s.two_sems("xn_loaded")
        q_done, k_done, v_done = s.sem("q_done"), s.sem("k_done"), s.sem("v_done")
        q_hi_ready, k_hi_ready = s.sem("q_hi_ready"), s.sem("k_hi_ready")
        q_split, k_split, v_ready = s.sem("q_split"), s.sem("k_split"), s.sem("v_ready")
        stack_free, stacked = s.sem("stack_free"), s.two_sems("stacked")
        max_scores, max_taken = s.sem("max_scores"), s.sem("max_taken")
        max_turned, max_copied = s.sem("max_turned"), s.sem("max_copied")
        max_stacked = s.two_sems("max_stacked")
        scores_done, exp_done = s.sem("scores_done"), s.sem("exp_done")
        pv_done, ctx_copied = s.sem("pv_done"), s.sem("ctx_copied")
        ctx_back, inv_ready, ctx_ready = s.sem("ctx_back"), s.sem("inv_ready"), s.sem("ctx_ready")
        ctx_again, ctx_turned_ready = s.sem("ctx_again"), s.sem("ctx_turned_ready")
        out_done, h_done = s.sem("out_done"), s.sem("h_done")
        x_out_ready, slot_ready = s.sem("x_out_ready"), s.sem("slot_ready")
        scatter_started, scattered = s.sem("scatter_started"), s.two_sems("scattered")

        MAX_SLOTS = {}
        unit = 0
        for slot, n in zip(range(7, 24), (1, 2, 1, 2, 1, 2, 1, 2, 1, 1, 2, 1, 1, 2, 1, 1, 2)):
            MAX_SLOTS[slot] = range(unit, unit + n)
            unit += n
        assert unit == 2 * UNITS

        last_chunk = chunks - 1

        with nc.Block() as block:

            @block.sync
            def _(sp):
                def load_xt(c):
                    sp.dma_start(xt[c.parity][:], env["xt_dram"][ds(c.index * P, P), :]).then_inc(xt_loaded[c.parity], 16)

                def load_xn(c):
                    sp.dma_start(xn[c.parity][:], env["xn_tiles"][:, ds(c.index * TPC, TPC), :]).then_inc(xn_loaded[c.parity], 16)

                def stack_parts(c):
                    sp.wait_ge(q_split, c.index + 1)
                    sp.wait_ge(k_split, c.index + 1)
                    for i in range(LANES):
                        for part, (q, k) in enumerate(((q_hi, k_hi), (q_hi, k_lo), (q_lo, k_hi))):
                            to = slice(32 * i + DH * part, 32 * i + DH * (part + 1))
                            src = slice(32 * i, 32 * i + 32)
                            sp.dma_start(q_stack[c.parity][to, :, :].bitcast(F32), q[src, :].bitcast(F32)).then_inc(stacked[c.parity], 16)
                            sp.dma_start(k_stack[c.parity][to, :, :].bitcast(F32), k[src, :].bitcast(F32)).then_inc(stacked[c.parity], 16)

                def stack_max(c, b):
                    sp.wait_ge(max_copied, 2 * c.index + b + 1)
                    for i in range(LANES):
                        sp.dma_start(q_stack[c.parity][32 * i + ROWS:32 * i + ROWS + 1, :, b * SEQ:(b + 1) * SEQ].bitcast(F32),
                                     neg_max[b][GROUPS * i:GROUPS * (i + 1), :].bitcast(F32)).then_inc(max_stacked[b], 16)

                def step(half, d):
                    p = at(half, d)
                    first, last = (isinstance(p.index, int) and p.index == k for k in (0, last_chunk))
                    one_left = isinstance(p.index, int) and p.index >= last_chunk - 2
                    two_left = isinstance(p.index, int) and p.index >= last_chunk - 1
                    if not first and not last:
                        sp.wait_ge(scores_done, 2 * UNITS * p.index)
                        sp.sem_inc(stack_free, 1)
                        stack_parts(at(half, d + 1))
                    stack_max(p, 1)
                    if not one_left:
                        sp.wait_ge(v_done, p.index + 2)
                        load_xt(at(half, d + 3))
                    if not last:
                        stack_max(at(half, d + 1), 0)
                    if not two_left:
                        sp.wait_ge(x_out_ready, p.index + 1)
                        sp.wait_ge(scattered[p.parity], 16 * 2 * TPC * (p.turn + 1))
                        load_xn(at(half, d + 2))

                load_xt(at(0, 0))
                load_xt(at(0, 1))
                load_xn(at(0, 0))
                load_xn(at(0, 1))
                sp.wait_ge(const_ready, 6)
                for k in range(2):
                    for i in range(LANES):
                        row = k_stack[k][32 * i + ROWS:32 * i + ROWS + 1, :, :].bitcast(F32)
                        sp.dma_start(row, ones[0:GROUPS, :]).then_inc(rows_loaded, 16)
                sp.wait_ge(v_done, 1)
                load_xt(at(0, 2))
                stack_parts(at(0, 0))
                stack_parts(at(0, 1))
                stack_max(at(0, 0), 0)
                step(0, 0)
                with sp.Fori(0, chunks // 2 - 2) as half:
                    step(half, 1)
                    step(half, 2)
                step(chunks // 2 - 2, 1)
                step(chunks // 2 - 1, 0)
                step(chunks // 2 - 1, 1)

            @block.gpsimd
            def _(pool):
                for k in range(2):
                    pool.memset(v_ones[k][:], 1.0).then_inc(v_cleared, 1)
                pool.memset(mask_st[:], 0.0).then_inc(const_ready, 1)
                pool.memset(mask_ts[:], 0.0).then_inc(const_ready, 1)
                pool.memset(ones[:], 1.0).then_inc(const_ready, 1)
                pool.tensor_copy(ident_b[:], ident[:]).then_inc(const_ready, 1)
                pool.wait_ge(const_ready, 2)
                pool.affine_select(out=mask_st[:], in_=mask_st[:], compare_op=ALU.is_ge, fill=MASKED, base=0,
                                   pattern=[[0, LANES], [-1, P]], channel_multiplier=1).then_inc(const_ready, 1)
                pool.affine_select(out=mask_ts[:], in_=mask_ts[:], compare_op=ALU.is_ge, fill=MASKED, base=0,
                                   pattern=[[0, LANES], [1, P]], channel_multiplier=-1).then_inc(const_ready, 1)

                def residual_and_scatter(c, again):
                    pool.wait_ge(xn_loaded[c.parity], 16 * (c.turn + 1))
                    if again:
                        pool.wait_ge(h_done, 2 * c.index - 2)
                        pool.wait_ge(scattered[c.parity], 16 * 2 * TPC * c.turn)
                    pool.tensor_tensor(x_out[c.parity][:], xn[c.parity][:], out_bias[:], ALU.add).then_inc(x_out_ready, 1)
                    pool.tensor_copy(slot_now[c.parity][:], slot_of[:, ds(c.index * 2 * TPC, 2 * TPC)]).then_inc(slot_ready, 1)
                    pool.wait_ge(slot_ready, c.index + 1)
                    pool.sem_inc(scatter_started, 1)
                    for t in range(TPC):
                        for k in range(2):
                            col = 2 * t + k
                            pool.indirect_dma_start(env["slot_x"][:], bass.IndirectOffsetOnAxis(ap=slot_now[c.parity][:, col:col + 1], axis=0),
                                                    xn[c.parity][:, t, :], None).then_inc(scattered[c.parity], 16)

                residual_and_scatter(at(0, 0), False)
                residual_and_scatter(at(0, 1), False)
                with pool.Fori(1, chunks // 2) as half:
                    residual_and_scatter(at(half, 0), True)
                    residual_and_scatter(at(half, 1), True)
                for k in range(2):
                    pool.wait_ge(scattered[k], 16 * 2 * TPC * (chunks // 2))

            @block.tensor
            def _(pe):
                def project_q(c, bank, free, n):
                    pe.wait_ge(xt_loaded[c.parity], 16 * (c.turn + 1))
                    pe.wait_ge(free, n) if n is not None else None
                    pe.matmul(free_ps[bank][:], wq[:], xt[c.parity][:], start=True, stop=True).then_inc(q_done, 1)

                def project_k(c, bank, free, n):
                    pe.wait_ge(free, n) if n is not None else None
                    pe.matmul(free_ps[bank][:], wk[:], xt[c.parity][:], start=True, stop=True).then_inc(k_done, 1)

                def project_v(c, bank, free, n):
                    pe.wait_ge(free, n)
                    for t in range(TPC):
                        last = pe.matmul(free_ps[bank][:, t * P:(t + 1) * P], xt[c.parity][:, t * P:(t + 1) * P], wv[:], start=True, stop=True)
                    last.then_inc(v_done, 1)

                def max_unit(c, m):
                    b, u = divmod(m, UNITS)
                    wide, i = divmod(u, LANES)
                    r = slice(32 * i, 32 * i + ROWS)
                    ps, q, k = m_ps[m % 2], q_stack[c.parity], k_stack[c.parity]
                    lo, hi = b * SEQ, b * SEQ + P
                    if m == 0:
                        pe.wait_ge(stacked[c.parity], 16 * 2 * 3 * LANES * (c.turn + 1))
                    if not (isinstance(c.index, int) and c.index == 0 and m < 2):
                        pe.wait_ge(max_taken, 2 * UNITS * c.index + m - 1)
                    if wide < 2:
                        for n in range(2):
                            g = 2 * wide + n
                            pe.matmul(ps[:, n * SEQ:(n + 1) * SEQ], q[r, g, hi:hi + P], k[r, g, lo:lo + SEQ],
                                      start=(n == 0), stop=False, skip_group_check=True)
                        last = pe.matmul(ps[:].rearrange("p (n t) -> p n t", n=2)[:, :, P:SEQ], ident_b[:], mask_st[:, 0:2, :],
                                         start=False, stop=True, skip_group_check=True)
                    else:
                        for g in range(GROUPS):
                            pe.matmul(ps[:, g * P:(g + 1) * P], q[r, g, lo:lo + P], k[r, g, lo:lo + P],
                                      start=(g == 0), stop=False, skip_group_check=True)
                        last = pe.matmul(ps[:], ident_b[:], mask_st[:].rearrange("p g t -> p (g t)"), start=False, stop=True, skip_group_check=True)
                    last.then_inc(max_scores, 1)

                def score_unit(c, m):
                    b, u = divmod(m, UNITS)
                    wide, i = divmod(u, LANES)
                    r = slice(32 * i, 32 * i + ROWS + 1)
                    ps, q, k = t_ps[m % 2], q_stack[c.parity], k_stack[c.parity]
                    lo, hi = b * SEQ, b * SEQ + P
                    if u == 0:
                        pe.wait_ge(max_stacked[b], 16 * LANES * (c.index + 1))
                    if not (isinstance(c.index, int) and c.index == 0 and m < 2):
                        pe.wait_ge(exp_done, 2 * UNITS * c.index + m - 1)
                    if wide < 2:
                        for n in range(2):
                            g = 2 * wide + n
                            pe.matmul(ps[:, n * SEQ:(n + 1) * SEQ], k[r, g, lo:lo + P], q[r, g, lo:lo + SEQ],
                                      start=(n == 0), stop=False, skip_group_check=True)
                        last = pe.matmul(ps[:].rearrange("p (n t) -> p n t", n=2)[:, :, 0:P], ident_b[:], mask_ts[:, 0:2, :],
                                         start=False, stop=True, skip_group_check=True)
                    else:
                        for g in range(GROUPS):
                            pe.matmul(ps[:, g * P:(g + 1) * P], k[r, g, hi:hi + P], q[r, g, hi:hi + P],
                                      start=(g == 0), stop=False, skip_group_check=True)
                        last = pe.matmul(ps[:], ident_b[:], mask_ts[:].rearrange("p g t -> p (g t)"), start=False, stop=True, skip_group_check=True)
                    last.then_inc(scores_done, 1)

                def probs_times_v(c, n):
                    b, wide = divmod(n, 3)
                    pe.wait_ge(exp_done, 2 * UNITS * c.index + 4 * (n + 1))
                    if n == 0:
                        pe.wait_ge(v_ready, c.index + 1)
                    if wide == 0 and not (isinstance(c.index, int) and c.index == 0 and b == 0):
                        pe.wait_ge(ctx_copied, 2 * c.index + b)
                    for n_g in range(2 if wide < 2 else GROUPS):
                        for i in range(LANES):
                            pt = probs[:, (4 * n + i) % PT, :]
                            if wide < 2:
                                g = 2 * wide + n_g
                                last = pe.matmul(pv_ps[32 * i:32 * i + 32, g * SEQ:(g + 1) * SEQ], v_ones[c.parity][:, 2 * b, g * LANES + i, :],
                                                 pt[:, n_g * SEQ:(n_g + 1) * SEQ], start=(n_g == 0), stop=False, skip_group_check=True)
                            else:
                                g = n_g
                                last = pe.matmul(pv_ps[32 * i:32 * i + 32, g * SEQ + P:(g + 1) * SEQ], v_ones[c.parity][:, 2 * b + 1, g * LANES + i, :],
                                                 pt[:, g * P:(g + 1) * P], start=False, stop=(g % 2 == 1), skip_group_check=True)
                    last.then_inc(pv_done, 1)

                def turn_max(c, b, bank, free, n):
                    pe.wait_ge(max_taken, UNITS * (2 * c.index + b + 1))
                    pe.wait_ge(free, n)
                    for t in range(2):
                        last = pe.transpose(free_ps[bank][0:HEADS, t * P:(t + 1) * P], row_max[b][:, t, :], ident[:])
                    last.then_inc(max_turned, 1)

                def context_back(seq, t, bank, free, n):
                    pe.wait_ge(ctx_copied, seq + 1)
                    pe.wait_ge(free, n)
                    for g in range(GROUPS):
                        last = pe.transpose(free_ps[bank][:, g * P:(g + 1) * P], ctx_t[:, g * SEQ + t * P:g * SEQ + (t + 1) * P], ident[:])
                    last.then_inc(ctx_back, 1)

                def context_again(seq, bank, free, n):
                    pe.wait_ge(ctx_ready, 2 * seq + 2)
                    pe.wait_ge(free, n)
                    for t in range(2):
                        last = pe.transpose(free_ps[bank][:, t * P:(t + 1) * P], ctx[:, t, :], ident[:])
                    last.then_inc(ctx_again, 1)

                def project_out(seq, bank, free, n):
                    pe.wait_ge(ctx_turned_ready, seq + 1)
                    pe.wait_ge(free, n)
                    for t in range(2):
                        last = pe.matmul(free_ps[bank][:, t * P:(t + 1) * P], ctx_turned[:, t * P:(t + 1) * P], wo[:], start=True, stop=True)
                    last.then_inc(out_done, 1)

                def step(half, d):
                    p, nxt, far = at(half, d), at(half, d + 1), at(half, d + 2)
                    x = p.index
                    first, last = (isinstance(x, int) and x == k for k in (0, last_chunk))
                    two_left = isinstance(x, int) and x >= last_chunk - 1
                    before, here = 2 * x - 1, 2 * x
                    for slot in range(2 * UNITS):
                        score_unit(p, slot)
                        if slot == 0:
                            if first:
                                turn_max(p, 1, 0, max_copied, 1)
                            else:
                                turn_max(p, 1, 0, h_done, before)
                        if slot == 1 and not first:
                            probs_times_v(at(half, d - 1), 5)
                        if slot == 3 and not last:
                            if first:
                                project_v(nxt, 1, k_split, 2)
                            else:
                                project_v(nxt, 1, ctx_turned_ready, before)
                        if slot == 4 and not first:
                            context_back(before, 0, 0, max_copied, 2 * x + 2)
                        if slot == 5:
                            probs_times_v(p, 0)
                            if last:
                                context_back(before, 1, 1, ctx_turned_ready, before)
                            elif not first:
                                context_back(before, 1, 1, v_ready, x + 2)
                        if slot == 8 and not first:
                            context_again(before, 0, ctx_ready, 2 * before + 1)
                        if slot == 9:
                            probs_times_v(p, 1)
                        if slot == 10 and not first:
                            project_out(before, 1, ctx_ready, 2 * before + 2)
                        if slot == 13:
                            probs_times_v(p, 2)
                        if slot == 16 and not last:
                            if first:
                                turn_max(nxt, 0, 0, max_copied, 2)
                            else:
                                turn_max(nxt, 0, 0, ctx_turned_ready, 2 * x)
                        if slot == 17:
                            probs_times_v(p, 3)
                            if first:
                                context_back(here, 0, 1, v_ready, 2)
                            else:
                                context_back(here, 0, 1, h_done, 2 * x)
                        if slot == 18:
                            if last:
                                context_back(here, 1, 0, ctx_turned_ready, 2 * x)
                            else:
                                context_back(here, 1, 0, max_copied, 2 * x + 3)
                        if slot == 19 and not two_left:
                            project_q(far, 1, ctx_ready, 2 * here + 1)
                        if slot == 20 and not two_left:
                            project_k(far, 0, ctx_ready, 2 * here + 2)
                        if slot == 21:
                            probs_times_v(p, 4)
                            if two_left:
                                context_again(here, 1, ctx_ready, 2 * here + 1)
                            else:
                                context_again(here, 1, q_split, x + 3)
                        if slot == 23:
                            if two_left:
                                project_out(here, 0, ctx_ready, 2 * here + 2)
                            else:
                                project_out(here, 0, k_split, x + 3)
                        if not last:
                            for m in MAX_SLOTS.get(slot, ()):
                                max_unit(nxt, m)

                pe.wait_ge(const_ready, 6)
                pe.wait_ge(v_cleared, 2)
                project_q(at(0, 0), 1, None, None)
                project_k(at(0, 0), 0, None, None)
                project_v(at(0, 0), 1, q_split, 1)
                project_q(at(0, 1), 0, k_split, 1)
                project_k(at(0, 1), 1, v_ready, 1)
                pe.wait_ge(rows_loaded, 16 * 2 * LANES)
                for m in range(2 * UNITS):
                    max_unit(at(0, 0), m)
                    if m == 2 * UNITS - 1:
                        turn_max(at(0, 0), 0, 0, q_split, 2)
                step(0, 0)
                with pe.Fori(0, chunks // 2 - 2) as half:
                    step(half, 1)
                    step(half, 2)
                step(chunks // 2 - 2, 1)
                step(chunks // 2 - 1, 0)
                step(chunks // 2 - 1, 1)
                probs_times_v(at(chunks // 2 - 1, 1), 5)
                end = 2 * chunks - 1
                context_back(end, 0, 0, h_done, end)
                context_back(end, 1, 1, ctx_turned_ready, end)
                context_again(end, 0, ctx_ready, 2 * end + 1)
                project_out(end, 1, ctx_ready, 2 * end + 2)

            @block.scalar
            def _(act):
                def high_q(c, bank):
                    act.wait_ge(q_done, c.index + 1)
                    if not (isinstance(c.index, int) and c.index == 0):
                        prev = (1 - c.parity, c.turn if c.parity else c.turn - 1)
                        act.wait_ge(stacked[prev[0]], 16 * 2 * 3 * LANES * (prev[1] + 1))
                    act.activation(q_hi[:], free_ps[bank][:], ACT.Identity, bias=q_bias[:]).then_inc(q_hi_ready, 1)

                def high_k(c, bank):
                    act.wait_ge(k_done, c.index + 1)
                    act.activation(k_hi[:], free_ps[bank][:], ACT.Identity, bias=k_bias[:]).then_inc(k_hi_ready, 1)

                def exp_unit(c, m):
                    act.wait_ge(scores_done, 2 * UNITS * c.index + m + 1)
                    if m % 4 == 0 and not (isinstance(c.index, int) and c.index == 0 and m < PT):
                        act.wait_ge(pv_done, 6 * c.index + m // 4 - 1)
                    act.activation(probs[:, m % PT, :], t_ps[m % 2][:], ACT.Exp).then_inc(exp_done, 1)

                def copy_context(seq):
                    act.wait_ge(pv_done, 3 * (seq + 1))
                    if not (isinstance(seq, int) and seq == 0):
                        act.wait_ge(ctx_back, 2 * seq)
                    act.copy(ctx_t[:], pv_ps[:]).then_inc(ctx_copied, 1)

                def copy_turned(seq, bank):
                    act.wait_ge(ctx_again, seq + 1)
                    if not (isinstance(seq, int) and seq == 0):
                        act.wait_ge(out_done, seq)
                    act.copy(ctx_turned[:], free_ps[bank][:, 0:SEQ]).then_inc(ctx_turned_ready, 1)

                def step(half, d):
                    p, far = at(half, d), at(half, d + 2)
                    x = p.index
                    first = isinstance(x, int) and x == 0
                    two_left = isinstance(x, int) and x >= last_chunk - 1
                    for slot in range(2 * UNITS):
                        exp_unit(p, slot)
                        if slot == 1 and not first:
                            copy_context(2 * x - 1)
                        if slot == 8 and not first:
                            copy_turned(2 * x - 1, 0)
                        if slot == 13:
                            copy_context(2 * x)
                        if slot == 19 and not two_left:
                            high_q(far, 1)
                        if slot == 20 and not two_left:
                            high_k(far, 0)
                        if slot == 21:
                            copy_turned(2 * x, 1)

                high_q(at(0, 0), 1)
                high_k(at(0, 0), 0)
                high_q(at(0, 1), 0)
                high_k(at(0, 1), 1)
                step(0, 0)
                with act.Fori(0, chunks // 2 - 2) as half:
                    step(half, 1)
                    step(half, 2)
                step(chunks // 2 - 2, 1)
                step(chunks // 2 - 1, 0)
                step(chunks // 2 - 1, 1)
                copy_context(2 * chunks - 1)
                copy_turned(2 * chunks - 1, 0)

            @block.vector
            def _(dve):
                def low_q(c, bank):
                    dve.wait_ge(q_hi_ready, c.index + 1)
                    dve.scalar_tensor_tensor(out=q_lo[:], in0=free_ps[bank][:], scalar=q_bias[:], in1=q_hi[:].bitcast(F32),
                                             op0=ALU.add, op1=ALU.subtract).then_inc(q_split, 1)

                def low_k(c, bank):
                    dve.wait_ge(k_hi_ready, c.index + 1)
                    dve.scalar_tensor_tensor(out=k_lo[:], in0=free_ps[bank][:], scalar=k_bias[:], in1=k_hi[:].bitcast(F32),
                                             op0=ALU.add, op1=ALU.subtract).then_inc(k_split, 1)

                def copy_v(c, bank):
                    dve.wait_ge(v_done, c.index + 1)
                    dve.tensor_tensor(v_ones[c.parity][:, :, :, 0:DH], free_ps[bank][:].rearrange("p (t h e) -> p t h e", t=TPC, e=DH),
                                      v_bias[:].rearrange("p t (h e) -> p t h e", e=DH), ALU.add).then_inc(v_ready, 1)

                def take_max(c, m):
                    b, u = divmod(m, UNITS)
                    wide, i = divmod(u, LANES)
                    dve.wait_ge(max_scores, 2 * UNITS * c.index + m + 1)
                    if u == 0 and not (isinstance(c.index, int) and c.index == 0):
                        dve.wait_ge(max_turned, 2 * c.index + b - 1)
                    n, t = (2, 1) if wide < 2 else (GROUPS, 0)
                    col = GROUPS * i + (2 * wide if wide < 2 else 0)
                    dve.tensor_reduce(row_max[b][:, t, col:col + n], m_ps[m % 2][:].rearrange("p (n t) -> p n t", n=n), AX.X, ALU.max).then_inc(max_taken, 1)

                def copy_max(c, b):
                    dve.wait_ge(max_turned, 2 * c.index + b + 1)
                    if not (isinstance(c.index, int) and c.index == 0):
                        dve.wait_ge(max_stacked[b], 16 * LANES * c.index)
                    dve.tensor_scalar(neg_max[b][:], free_ps[0][0:HEADS, 0:SEQ], -1.0, None, ALU.mult).then_inc(max_copied, 1)

                def normalise(seq, t, bank):
                    n = 2 * seq + t
                    dve.wait_ge(ctx_back, n + 1)
                    if t == 0 and not (isinstance(seq, int) and seq == 0):
                        dve.wait_ge(ctx_again, seq)
                    rows = free_ps[bank][:].rearrange("p (h c) -> p h c", c=32)
                    dve.reciprocal(ctx_inv[:, t, :], rows[:, :, DH]).then_inc(inv_ready, 1)
                    dve.wait_ge(inv_ready, n + 1)
                    dve.tensor_tensor(ctx[:, t, :].rearrange("p (h e) -> p h e", e=DH), rows[:, :, 0:DH],
                                      ctx_inv[:, t, :].unsqueeze(2).to_broadcast([P, HEADS, DH]), ALU.mult).then_inc(ctx_ready, 1)

                def add_residual(seq, c, b, bank):
                    dve.wait_ge(out_done, seq + 1)
                    dve.wait_ge(x_out_ready, c.index + 1)
                    rows = h_all[:, ds(seq * SEQ, SEQ)]
                    dve.tensor_tensor(rows, free_ps[bank][:, 0:SEQ], x_out[c.parity][:, 2 * b:2 * b + 2, :].rearrange("p t d -> p (t d)"), ALU.add).then_inc(h_done, 1)
                    dve.wait_ge(h_done, seq + 1)
                    for t in range(2):
                        dve.bn_stats(ln2_stats[:, ds((seq * 2 + t) * 6, 6)], h_all[:, ds(seq * SEQ + t * P, P)])

                def step(half, d):
                    p, prev, nxt, far = at(half, d), at(half, d - 1), at(half, d + 1), at(half, d + 2)
                    x = p.index
                    first, last = (isinstance(x, int) and x == k for k in (0, last_chunk))
                    two_left = isinstance(x, int) and x >= last_chunk - 1
                    for slot in range(2 * UNITS):
                        if slot == 0:
                            copy_max(p, 1)
                        if slot == 3 and not last:
                            copy_v(nxt, 1)
                        if slot == 4 and not first:
                            normalise(2 * x - 1, 0, 0)
                        if slot == 5 and not first:
                            normalise(2 * x - 1, 1, 1)
                        if slot == 10 and not first:
                            add_residual(2 * x - 1, prev, 1, 1)
                        if slot == 16 and not last:
                            copy_max(nxt, 0)
                        if slot == 17:
                            normalise(2 * x, 0, 1)
                        if slot == 18:
                            normalise(2 * x, 1, 0)
                        if slot == 19 and not two_left:
                            low_q(far, 1)
                        if slot == 20 and not two_left:
                            low_k(far, 0)
                        if slot == 23:
                            add_residual(2 * x, p, 0, 0)
                        if not last:
                            for m in MAX_SLOTS.get(slot, ()):
                                take_max(nxt, m)

                dve.wait_ge(v_cleared, 2)
                low_q(at(0, 0), 1)
                low_k(at(0, 0), 0)
                copy_v(at(0, 0), 1)
                low_q(at(0, 1), 0)
                low_k(at(0, 1), 1)
                for m in range(2 * UNITS):
                    take_max(at(0, 0), m)
                copy_max(at(0, 0), 0)
                step(0, 0)
                with dve.Fori(0, chunks // 2 - 2) as half:
                    step(half, 1)
                    step(half, 2)
                step(chunks // 2 - 2, 1)
                step(chunks // 2 - 1, 0)
                step(chunks // 2 - 1, 1)
                normalise(2 * chunks - 1, 0, 0)
                normalise(2 * chunks - 1, 1, 1)
                add_residual(2 * chunks - 1, at(chunks // 2 - 1, 1), 1, 1)


def experts(nc, env):
    slot_tiles = env["slot_tiles"]
    ident, w_gate_up, w_down, tile_expert = env["ident"], env["w_gate_up"], env["w_down"], env["tile_expert"]
    gate_up_cols = w_gate_up[:].rearrange("p e f -> p (e f)")
    down_cols = w_down[:].rearrange("p e c d -> p (e c d)")
    NCH = len(FF_CHUNKS)

    with ExitStack() as stack:
        s = Scope(nc, stack, "moe")
        x = s.two("x", [P, P])
        x_t = s.two("x_t", [P, P])
        gate = s.two("gate", [P, FF])
        hidden = s.two("hidden", [P, FF])
        hidden_t = s.two("hidden_t", [P, NCH * P])
        y = s.two("y", [P, P])
        x_ps = [s.ps(f"x_ps{k}", [P, 512]) for k in range(2)]
        gate_ps = [s.ps(f"gate_ps{k}", [P, 512]) for k in range(2)]
        up_ps = [s.ps(f"up_ps{k}", [P, 512]) for k in range(2)]
        hidden_ps, y_ps = s.ps("hidden_ps", [P, 512]), s.ps("y_ps", [P, 512])

        x_loaded, y_stored = s.two_sems("x_loaded"), s.two_sems("y_stored")
        x_turned, x_copied, gate_up_done = s.sem("x_turned"), s.sem("x_copied"), s.sem("gate_up_done")
        gate_done, hidden_done, hidden_turned = s.sem("gate_done"), s.sem("hidden_done"), s.sem("hidden_turned")
        hidden_copied, down_done, y_copied = s.sem("hidden_copied"), s.sem("down_done"), s.sem("y_copied")

        def run(eng, first_step, step):
            end = (slot_tiles - 4) // 2
            first_step()
            step(0, 1, 3)
            step(0, 2, 3)
            with eng.Fori(1, end) as half:
                step(half, 1, 3)
                step(half, 2, 3)
            for j in range(2 * end + 1, slot_tiles):
                step(j // 2, j % 2, min(3, slot_tiles - j))

        with nc.Block() as block:

            @block.sync
            def _(sp):
                def load(c, early=False):
                    if not early:
                        sp.wait_ge(x_turned, c.index - 1)
                    sp.dma_start(x[c.parity][:], env["slot_x"][ds(c.index * P, P), :]).then_inc(x_loaded[c.parity], 16)

                load(at(0, 0), True)
                load(at(0, 1), True)
                with sp.Fori(1, slot_tiles // 2) as half:
                    load(at(half, 0))
                    load(at(half, 1))

            @block.gpsimd
            def _(pool):
                def store(c):
                    pool.wait_ge(y_copied, c.index + 1)
                    pool.dma_start(env["slot_y"][ds(c.index * P, P), :], y[c.parity][:]).then_inc(y_stored[c.parity], 16)

                with pool.Fori(0, slot_tiles // 2) as half:
                    store(at(half, 0))
                    store(at(half, 1))
                for k in range(2):
                    pool.wait_ge(y_stored[k], 16 * (slot_tiles // 2))

            @block.tensor
            def _(pe):
                def turn_x(c, early=False):
                    pe.wait_ge(x_loaded[c.parity], 16 * (c.turn + 1))
                    if not early:
                        pe.wait_ge(x_copied, c.index - 1)
                    pe.transpose(x_ps[c.parity][:, 0:P], x[c.parity][:], ident[:]).then_inc(x_turned, 1)

                def gate_up(c, early=False):
                    e = pe.value_load(tile_expert[0:1, ds(c.index, 1)], min_val=0, max_val=EXPERTS - 1)
                    pe.wait_ge(x_copied, c.index + 1)
                    if not early:
                        pe.wait_ge(hidden_done, c.index - 1)
                    pe.matmul(gate_ps[c.parity][:, 0:FF], x_t[c.parity][:], gate_up_cols[:, ds(e * (2 * FF), FF)], start=True, stop=True)
                    pe.matmul(up_ps[c.parity][:, 0:FF], x_t[c.parity][:], gate_up_cols[:, ds(e * (2 * FF) + FF, FF)], start=True, stop=True).then_inc(gate_up_done, 1)

                def turn_hidden(c, early=False):
                    pe.wait_ge(hidden_done, c.index + 1)
                    if not early:
                        pe.wait_ge(hidden_copied, c.index)
                    for k, (col, n) in enumerate(FF_CHUNKS):
                        last = pe.transpose(hidden_ps[0:n, k * P:(k + 1) * P], hidden[c.parity][:, col:col + n], ident[:])
                    last.then_inc(hidden_turned, 1)

                def down(c, early=False):
                    e = pe.value_load(tile_expert[0:1, ds(c.index, 1)], min_val=0, max_val=EXPERTS - 1)
                    pe.wait_ge(hidden_copied, c.index + 1)
                    if not early:
                        pe.wait_ge(y_copied, c.index)
                    for k, (col, n) in enumerate(FF_CHUNKS):
                        last = pe.matmul(y_ps[:, 0:P], hidden_t[c.parity][0:n, k * P:(k + 1) * P],
                                         down_cols[0:n, ds(e * (NCH * P) + k * P, P)], start=(k == 0), stop=(k == NCH - 1))
                    last.then_inc(down_done, 1)

                def first_step():
                    turn_x(at(0, 0), True)
                    turn_x(at(0, 1), True)
                    gate_up(at(0, 0), True)
                    turn_x(at(0, 2))
                    gate_up(at(0, 1), True)
                    turn_hidden(at(0, 0), True)

                def step(half, d, left):
                    if left > 2:
                        turn_x(at(half, d + 2))
                    if left > 1:
                        gate_up(at(half, d + 1))
                    turn_hidden(at(half, d))
                    c = at(half, d - 1)
                    down(c, isinstance(c.index, int) and c.index == 0)

                run(pe, first_step, step)
                down(at(slot_tiles // 2, -1))

            @block.scalar
            def _(act):
                def silu(c, early=False):
                    act.wait_ge(gate_up_done, c.index + 1)
                    if not early:
                        act.wait_ge(hidden_done, c.index - 1)
                    act.activation(gate[c.parity][:], gate_ps[c.parity][:, 0:FF], ACT.Silu).then_inc(gate_done, 1)

                def copy_hidden(c, early=False):
                    act.wait_ge(hidden_turned, c.index + 1)
                    if not early and not (isinstance(c.index, int) and c.index == 1):
                        act.wait_ge(down_done, c.index - 1)
                    whole = FF_CHUNKS[-1][0]
                    rest = FF_CHUNKS[-1][1]
                    act.copy(hidden_t[c.parity][:, 0:whole], hidden_ps[:, 0:whole])
                    act.copy(hidden_t[c.parity][0:rest, whole:whole + P], hidden_ps[0:rest, whole:whole + P]).then_inc(hidden_copied, 1)

                def first_step():
                    silu(at(0, 0), True)
                    silu(at(0, 1), True)
                    copy_hidden(at(0, 0), True)

                def step(half, d, left):
                    if left > 1:
                        silu(at(half, d + 1))
                    copy_hidden(at(half, d))

                run(act, first_step, step)

            @block.vector
            def _(dve):
                def copy_x(c, early=False):
                    dve.wait_ge(x_turned, c.index + 1)
                    if not early:
                        dve.wait_ge(gate_up_done, c.index - 1)
                    dve.tensor_copy(x_t[c.parity][:], x_ps[c.parity][:, 0:P]).then_inc(x_copied, 1)

                def gated(c, early=False):
                    dve.wait_ge(gate_done, c.index + 1)
                    if not early:
                        dve.wait_ge(hidden_turned, c.index - 1)
                    dve.tensor_tensor(hidden[c.parity][:], gate[c.parity][:], up_ps[c.parity][:, 0:FF], ALU.mult).then_inc(hidden_done, 1)

                def copy_y(c):
                    dve.wait_ge(down_done, c.index + 1)
                    if not (isinstance(c.turn, int) and c.turn == 0):
                        dve.wait_ge(y_stored[c.parity], 16 * c.turn)
                    dve.tensor_copy(y[c.parity][:], y_ps[:, 0:P]).then_inc(y_copied, 1)

                def first_step():
                    copy_x(at(0, 0), True)
                    copy_x(at(0, 1), True)
                    gated(at(0, 0), True)
                    copy_x(at(0, 2))
                    gated(at(0, 1), True)

                def step(half, d, left):
                    if left > 2:
                        copy_x(at(half, d + 2))
                    if left > 1:
                        gated(at(half, d + 1))
                    copy_y(at(half, d - 1))

                run(dve, first_step, step)
                copy_y(at(slot_tiles // 2, -1))


def mlp_and_combine(nc, env):
    chunks, tiles = env["chunks"], env["tiles"]
    ident, w1, w2, mlp_bias, fc2_bias = env["ident"], env["w1"], env["w2"], env["mlp_bias"], env["fc2_bias"]
    mix, slot_of, h_all, ln2_stats = env["mix"], env["slot_of"], env["h_all"], env["ln2_stats"]
    mix_cols = mix[:].rearrange("p t k -> p (t k)")

    with ExitStack() as stack:
        s = Scope(nc, stack, "mlp")
        mean, var, tmp, rstd, power = (s.sb(n, [P, tiles]) for n in ("mean", "var", "tmp", "rstd", "power"))
        hn = s.two("hn", [P, TPC, P])
        hn_t = s.two("hn_t", [P, CHUNK])
        mid = s.two("mid", [P, HCH, CHUNK])
        x = s.two("x", [P, TPC, P])
        total = s.two("total", [P, TPC, P])
        slot_now = s.two("slot_now", [P, 2 * TPC], U32)
        rows = s.two("rows", [P, 2 * TPC, P])
        t_ps = s.ps("t_ps", [P, CHUNK])
        f_ps = [s.ps(f"f_ps{k}", [P, CHUNK]) for k in range(HCH)]
        o_ps = [s.ps(f"o_ps{k}", [P, CHUNK]) for k in range(2)]

        power_ready, var_ready, rstd_ready, ln_step = (s.sem(n) for n in ("power_ready", "var_ready", "rstd_ready", "ln_step"))
        hn_ready, hn_turned, hn_copied = s.sem("hn_ready"), s.sem("hn_turned"), s.sem("hn_copied")
        fc1_done, mid_ready, fc2_done = s.sem("fc1_done"), s.sem("mid_ready"), s.sem("fc2_done")
        gather_started = s.sem("gather_started")
        x_loaded, gathered, stored = s.two_sems("x_loaded"), s.two_sems("gathered"), s.two_sems("stored")
        slot_ready, sum_step, total_ready = s.sem("slot_ready"), s.sem("sum_step"), s.sem("total_ready")
        SUMS = 3 + 2

        def run(eng, step):
            with eng.Fori(0, chunks // 2 - 1) as half:
                step(half, 0, 3)
                step(half, 1, 3)
            step(chunks // 2 - 1, 0, 2)
            step(chunks // 2 - 1, 1, 1)

        with nc.Block() as block:

            @block.sync
            def _(sp):
                def load(c):
                    sp.dma_start(x[c.parity][:], env["x_tiles"][:, ds(c.index * TPC, TPC), :]).then_inc(x_loaded[c.parity], 16)

                def step(half, d, left):
                    c = at(half, d)
                    sp.wait_ge(total_ready, c.index + 1)
                    sp.dma_start(env["out_tiles"][:, ds(c.index * TPC, TPC), :], total[c.parity][:]).then_inc(stored[c.parity], 16)
                    if left > 2:
                        load(at(half, d + 2))

                load(at(0, 0))
                load(at(0, 1))
                run(sp, step)
                for k in range(2):
                    sp.wait_ge(stored[k], 16 * (chunks // 2))

            @block.gpsimd
            def _(pool):
                pool.memset(power[:], -0.5).then_inc(power_ready, 1)
                pool.wait_ge(power_ready, 1)
                pool.wait_ge(var_ready, 1)
                pool.tensor_tensor(rstd[:], var[:], power[:], ALU.pow).then_inc(rstd_ready, 1)

                def gather(c, again):
                    if again:
                        pool.wait_ge(total_ready, c.index - 1)
                    pool.tensor_copy(slot_now[c.parity][:], slot_of[:, ds(c.index * 2 * TPC, 2 * TPC)]).then_inc(slot_ready, 1)
                    pool.wait_ge(slot_ready, c.index + 1)
                    pool.sem_inc(gather_started, 1)
                    for col in range(2 * TPC):
                        pool.indirect_dma_start(rows[c.parity][:, col, :], None, env["slot_y"][:],
                                                bass.IndirectOffsetOnAxis(ap=slot_now[c.parity][:, col:col + 1], axis=0)).then_inc(gathered[c.parity], 16)

                gather(at(0, 0), False)
                gather(at(0, 1), False)
                with pool.Fori(1, chunks // 2) as half:
                    gather(at(half, 0), True)
                    gather(at(half, 1), True)

            @block.tensor
            def _(pe):
                def turn(c, early=False):
                    pe.wait_ge(hn_ready, c.index + 1)
                    if not early:
                        pe.wait_ge(hn_copied, c.index)
                    for t in range(TPC):
                        last = pe.transpose(t_ps[:, t * P:(t + 1) * P], hn[c.parity][:, t, :], ident[:])
                    last.then_inc(hn_turned, 1)

                def fc1(c, k, early=False):
                    pe.wait_ge(hn_copied, c.index + 1)
                    if not early:
                        pe.wait_ge(mid_ready, HCH * (c.index - 1) + k + 1)
                    pe.matmul(f_ps[k][:], w1[:, k * P:(k + 1) * P], hn_t[c.parity][:], start=True, stop=True).then_inc(fc1_done, 1)

                def fc2(c, t):
                    if t == 0:
                        pe.wait_ge(mid_ready, HCH * (c.index + 1))
                        if not (isinstance(c.index, int) and c.index < 2):
                            pe.wait_ge(total_ready, c.index - 1)
                    for k in range(HCH):
                        last = pe.matmul(o_ps[c.parity][:, t * P:(t + 1) * P], mid[c.parity][:, k, t * P:(t + 1) * P], w2[:, k, :],
                                         start=(k == 0), stop=(k == HCH - 1))
                    if t == TPC - 1:
                        last.then_inc(fc2_done, 1)

                def step(half, d, left):
                    if left > 2:
                        turn(at(half, d + 2))
                    for k in range(HCH):
                        if left > 1:
                            fc1(at(half, d + 1), k)
                        fc2(at(half, d), k)

                turn(at(0, 0), True)
                turn(at(0, 1))
                for k in range(HCH):
                    fc1(at(0, 0), k, True)
                step(0, 0, 3)
                step(0, 1, 3)
                with pe.Fori(1, chunks // 2 - 1) as half:
                    step(half, 0, 3)
                    step(half, 1, 3)
                step(chunks // 2 - 1, 0, 2)
                step(chunks // 2 - 1, 1, 1)

            @block.scalar
            def _(act):
                def copy_turned(c, early=False):
                    act.wait_ge(hn_turned, c.index + 1)
                    if not early:
                        act.wait_ge(fc1_done, HCH * (c.index - 1))
                    act.copy(hn_t[c.parity][:], t_ps[:]).then_inc(hn_copied, 1)

                def gelu(c, k, early=False):
                    act.wait_ge(fc1_done, HCH * c.index + k + 1)
                    if not early and k == 0:
                        act.wait_ge(fc2_done, c.index - 1)
                    act.activation(mid[c.parity][:, k, :], f_ps[k][:], ACT.Gelu_apprx_tanh, bias=mlp_bias[:, k:k + 1]).then_inc(mid_ready, 1)

                def step(half, d, left, early=False):
                    if left > 2:
                        copy_turned(at(half, d + 2))
                    if left > 1:
                        for k in range(HCH):
                            gelu(at(half, d + 1), k, early)

                copy_turned(at(0, 0), True)
                copy_turned(at(0, 1), True)
                for k in range(HCH):
                    gelu(at(0, 0), k, True)
                step(0, 0, 3, True)
                step(0, 1, 3)
                with act.Fori(1, chunks // 2 - 1) as half:
                    step(half, 0, 3)
                    step(half, 1, 3)
                step(chunks // 2 - 1, 0, 2)

            @block.vector
            def _(dve):
                steps = [0]

                def step_of(ins):
                    steps[0] += 1
                    ins.then_inc(ln_step, 1)
                    dve.wait_ge(ln_step, steps[0])

                parts = ln2_stats[:].rearrange("p (t c) -> p t c", c=6)
                step_of(dve.tensor_tensor(mean[:], parts[:, :, 1], parts[:, :, 4], ALU.add))
                step_of(dve.tensor_tensor(tmp[:], parts[:, :, 1], parts[:, :, 4], ALU.subtract))
                step_of(dve.tensor_tensor(var[:], parts[:, :, 2], parts[:, :, 5], ALU.add))
                step_of(dve.tensor_tensor(tmp[:], tmp[:], tmp[:], ALU.mult))
                step_of(dve.tensor_scalar(var[:], var[:], 1.0 / P, LN_EPS, ALU.mult, ALU.add))
                step_of(dve.tensor_scalar(mean[:], mean[:], 0.5, None, ALU.mult))
                dve.scalar_tensor_tensor(out=var[:], in0=tmp[:], scalar=0.25, in1=var[:], op0=ALU.mult, op1=ALU.add).then_inc(var_ready, 1)
                dve.wait_ge(rstd_ready, 1)

                def normalise(c, early=False):
                    if not early:
                        dve.wait_ge(hn_turned, c.index - 1)
                    for t in range(TPC):
                        tile = c.index * TPC + t
                        last = dve.tensor_scalar(hn[c.parity][:, t, :], h_all[:, ds(tile * P, P)], mean[:, ds(tile, 1)], rstd[:, ds(tile, 1)],
                                                 ALU.subtract, ALU.mult)
                    last.then_inc(hn_ready, 1)

                def add_up(c):
                    sums = total[c.parity]
                    dve.wait_ge(x_loaded[c.parity], 16 * (c.turn + 1))
                    if not (isinstance(c.turn, int) and c.turn == 0):
                        dve.wait_ge(stored[c.parity], 16 * c.turn)
                    done = SUMS * c.index
                    dve.tensor_tensor(sums[:].rearrange("p t d -> p (t d)"), x[c.parity][:].rearrange("p t d -> p (t d)"),
                                      h_all[:, ds(c.index * CHUNK, CHUNK)], ALU.add).then_inc(sum_step, 1)
                    dve.wait_ge(sum_step, done + 1)
                    dve.tensor_tensor(sums[:], sums[:], fc2_bias[:], ALU.add).then_inc(sum_step, 1)
                    dve.wait_ge(sum_step, done + 2)
                    dve.wait_ge(fc2_done, c.index + 1)
                    dve.tensor_tensor(sums[:], o_ps[c.parity][:].rearrange("p (t d) -> p t d", d=P), sums[:], ALU.add).then_inc(sum_step, 1)
                    dve.wait_ge(sum_step, done + 3)
                    dve.wait_ge(gathered[c.parity], 16 * 2 * TPC * (c.turn + 1))
                    for k in range(2):
                        for t in range(TPC):
                            last = dve.scalar_tensor_tensor(out=sums[:, t, :], in0=rows[c.parity][:, 2 * t + k, :], scalar=mix_cols[:, ds(c.index * 2 * TPC + 2 * t + k, 1)],
                                                            in1=sums[:, t, :], op0=ALU.mult, op1=ALU.add)
                        last.then_inc(sum_step, 1)
                        dve.wait_ge(sum_step, done + 4 + k)
                    dve.sem_inc(total_ready, 1)

                def step(half, d, left):
                    if left > 2:
                        normalise(at(half, d + 2))
                    add_up(at(half, d))

                normalise(at(0, 0), True)
                normalise(at(0, 1), True)
                step(0, 0, 3)
                step(0, 1, 3)
                with dve.Fori(1, chunks // 2 - 1) as half:
                    step(half, 0, 3)
                    step(half, 1, 3)
                step(chunks // 2 - 1, 0, 2)
                step(chunks // 2 - 1, 1, 1)


_ATTN = ("ln1_g", "ln1_b", "ln2_g", "ln2_b", "q_U", "q_V", "q_b", "k_U", "k_V", "k_b", "v_U", "v_V", "v_b",
         "out_U", "out_V", "out_b", "fc1_U", "fc1_V", "fc1_b", "fc2_U", "fc2_V", "fc2_b")
_FFN = ("Wr", "Wg", "Wu", "Wd")


def kernel(**inputs):
    import numpy as _np
    import concourse.bacc as _bacc
    from concourse import mybir as _mybir
    from concourse.bass_utils import run_bass_kernel_spmd as _run

    nc = _bacc.Bacc("TRN2", target_bir_lowering=False, num_devices=1)
    arrays = {}

    def given(name):
        a = _np.ascontiguousarray(inputs[name])
        arrays[f"in_{name}"] = a
        return nc.dram_tensor(f"in_{name}", a.shape, _mybir.dt.from_np(a.dtype), kind="ExternalInput").ap()

    x = given("L0_attn_hidden_states")
    w = {n: given(f"L0_attn_{n}") for n in _ATTN} | {n: given(f"L0_ffn_{n}") for n in _FFN}
    out = nc.dram_tensor("out", arrays["in_L0_attn_hidden_states"].shape, F32, kind="ExternalOutput").ap()
    layer_kernel(nc, x, w, out)
    r = _run(nc, [arrays], core_ids=[0])
    return r.results[0]["out"]
```

```python
from collections import namedtuple
from contextlib import ExitStack

import concourse.bass as bass
from concourse import mybir

F32 = mybir.dt.float32
F32R = mybir.dt.float32r
BF16 = mybir.dt.bfloat16
I32 = mybir.dt.int32
U32 = mybir.dt.uint32
ALU = mybir.AluOpType
ACT = mybir.ActivationFunctionType
AX = mybir.AxisListType
ds = bass.ds

P = 128
SEQ = 256
CHUNK = 512
TPC = CHUNK // P
HEADS, DH = 16, 8
LANES = 4
GROUPS = HEADS // LANES
PARTS = 3
ROWS = PARTS * LANES * DH
LN_EPS = 1e-5
MASKED = -1e30
EXPERTS, FF = 9, 352
FF_CHUNKS = ((0, 128), (128, 128), (256, 96))
HID = 512
HCH = HID // P
RANK_QKV, RANK_OUT, RANK_MLP = 48, 96, 64

Step = namedtuple("Step", "index parity turn")


def at(half, d):
    return Step(2 * half + d, d % 2, half + d // 2)


def layer_kernel(nc, x_in, w, out):
    tokens = x_in.shape[0] * x_in.shape[1]
    tiles = tokens // P
    chunks = tokens // CHUNK
    slot_tiles = (2 * tokens + EXPERTS * (P - 1)) // P
    slots = slot_tiles * P

    x_rows = x_in.rearrange("b s d -> (b s) d")
    out_rows = out.rearrange("b s d -> (b s) d")
    x_tiles = x_rows.rearrange("(n p) d -> p n d", p=P)
    out_tiles = out_rows.rearrange("(n p) d -> p n d", p=P)

    xn_dram = nc.dram_tensor("xn_scratch", [tokens, P], F32, kind="Internal").ap()
    xt_dram = nc.dram_tensor("xt_scratch", [chunks * P, CHUNK], F32, kind="Internal").ap()
    slot_x = nc.dram_tensor("slot_x", [slots, P], F32, kind="Internal").ap()
    slot_y = nc.dram_tensor("slot_y", [slots, P], F32, kind="Internal").ap()
    h_dram = nc.dram_tensor("h_scratch", [tokens, P], F32, kind="Internal").ap()
    xn_tiles = xn_dram.rearrange("(n p) d -> p n d", p=P)
    h_tiles = h_dram.rearrange("(n p) d -> p n d", p=P)

    whole = ExitStack()

    def keep(name, shape, dtype=F32):
        return whole.enter_context(nc.sbuf_tensor(name, shape, dtype))

    with whole:
        ident = keep("ident", [P, P])
        wq = keep("wq", [P, P])
        wk = keep("wk", [P, P])
        wv = keep("wv", [P, P])
        wo = keep("wo", [P, P])
        w1 = keep("w1", [P, HID])
        w2 = keep("w2", [P, HCH, P])
        q_bias = keep("q_bias", [P, 1])
        k_bias = keep("k_bias", [P, 1])
        v_bias = keep("v_bias", [P, P])
        mlp_bias = keep("mlp_bias", [P, HCH])
        out_bias = keep("out_bias", [P, P])
        fc2_bias = keep("fc2_bias", [P, P])
        w_gate_up = keep("w_gate_up", [P, EXPERTS, 2 * FF])
        w_down = keep("w_down", [P, EXPERTS, len(FF_CHUNKS), P])
        mix = keep("mix", [P, tiles, 2])
        slot_of = keep("slot_of", [P, tiles * 2], U32)
        tile_expert = keep("tile_expert", [1, slot_tiles], I32)
        ln2_stats = keep("ln2_stats", [P, tiles * 6])

        prepare(nc, locals())
        attention(nc, locals())
        experts(nc, locals())
        mlp_and_combine(nc, locals())


class Scope:

    def __init__(self, nc, stack, prefix):
        self.nc, self.stack, self.prefix = nc, stack, prefix

    def sb(self, name, shape, dtype=F32):
        return self.stack.enter_context(self.nc.sbuf_tensor(f"{self.prefix}_{name}", shape, dtype))

    def two(self, name, shape, dtype=F32):
        return [self.sb(f"{name}{k}", shape, dtype) for k in range(2)]

    def ps(self, name, shape):
        return self.stack.enter_context(self.nc.psum_tensor(f"{self.prefix}_{name}", shape, F32))

    def sem(self, name):
        return self.stack.enter_context(self.nc.semaphore(f"{self.prefix}_{name}"))

    def two_sems(self, name):
        return [self.sem(f"{name}{k}") for k in range(2)]


def prepare(nc, env):
    w = env["w"]
    tiles, chunks, slot_tiles, slots = env["tiles"], env["chunks"], env["slot_tiles"], env["slots"]
    ident, wq, wk, wv, wo = env["ident"], env["wq"], env["wk"], env["wv"], env["wo"]
    w1, w2, w_gate_up, w_down = env["w1"], env["w2"], env["w_gate_up"], env["w_down"]
    q_bias, k_bias, v_bias, mlp_bias = env["q_bias"], env["k_bias"], env["v_bias"], env["mlp_bias"]
    out_bias, fc2_bias = env["out_bias"], env["fc2_bias"]
    mix, slot_of, tile_expert = env["mix"], env["slot_of"], env["tile_expert"]
    PAIRS = HEADS // 2
    PR = 2 * RANK_QKV
    cols = tiles * EXPERTS
    half = cols // 2

    with ExitStack() as stack:
        s = Scope(nc, stack, "prep")
        x_all = s.sb("x_all", [P, tiles, P])
        u_in = [s.sb(f"u_{n}", [P, HEADS * RANK_QKV]) for n in "qkv"]
        v_in = [s.sb(f"v_{n}", [PR, PAIRS, 2 * DH]) for n in "qkv"]
        out_u, out_v = s.sb("out_u", [P, RANK_OUT]), s.sb("out_v", [RANK_OUT, P])
        fc1_u, fc1_v = s.sb("fc1_u", [P, RANK_MLP]), s.sb("fc1_v", [RANK_MLP, HID])
        fc2_u, fc2_v = s.sb("fc2_u", [P, HCH, RANK_MLP]), s.sb("fc2_v", [RANK_MLP, P])
        w_router = s.sb("w_router", [P, EXPERTS])
        ln1_g, ln1_b = s.sb("ln1_g", [P, 1]), s.sb("ln1_b", [P, 1])
        ln2_g, ln2_b = s.sb("ln2_g", [P, 1]), s.sb("ln2_b", [P, 1])
        q_b, k_b, fc1_b = s.sb("q_b", [P, 1]), s.sb("k_b", [P, 1]), s.sb("fc1_b", [P, HCH])
        v_b = s.sb("v_b", [P, P])
        zeros = s.sb("zeros", [P, 1024])
        ones = s.sb("ones", [P, P])
        before = s.sb("before", [P, P])
        rev_e = s.sb("rev_e", [P, tiles, EXPERTS])
        tile_no_i, tile_no = s.sb("tile_no_i", [1, slot_tiles], I32), s.sb("tile_no", [1, slot_tiles])
        power = s.sb("power", [P, 2, tiles])
        ut = s.sb("ut", [P, 6, 4 * P])
        ut_small = s.sb("ut_small", [P, 2 * P])
        ut_fc2 = s.sb("ut_fc2", [RANK_MLP, HCH * P])
        raw_qkv, raw_w1 = s.sb("raw_qkv", [P, 3, P]), s.sb("raw_w1", [P, HID])
        g_q = s.sb("g_q", [P, 1])
        b_rows = s.sb("b_rows", [P, P])
        stats = s.sb("stats", [P, tiles, 6])
        mean, var, tmp = s.sb("mean", [P, tiles]), s.sb("var", [P, tiles]), s.sb("tmp", [P, tiles])
        rstd, rstd2, std2 = s.sb("rstd", [P, tiles]), s.sb("rstd2", [P, tiles]), s.sb("std2", [P, tiles])
        xn = s.two("xn", [P, TPC, P])
        xnr = s.two("xnr", [P, TPC, P])
        xt = s.two("xt", [P, CHUNK])
        logits = s.sb("logits", [P, tiles, EXPERTS])
        work = s.sb("work", [P, tiles, EXPERTS])
        pick = [s.sb(f"pick{k}", [P, tiles, EXPERTS]) for k in range(2)]
        top = [s.sb(f"top{k}", [P, tiles]) for k in range(2)]
        key = s.sb("key", [P, tiles])
        chosen, scan_a, scan_b = (s.sb(n, [P, tiles, EXPERTS]) for n in ("chosen", "scan_a", "scan_b"))
        gap, gap_exp, gap_sum = s.sb("gap", [P, tiles]), s.sb("gap_exp", [P, tiles]), s.sb("gap_sum", [P, tiles])
        count_f, count_i = s.sb("count_f", [P, EXPERTS]), s.sb("count_i", [P, EXPERTS], I32)
        run_tiles, end_a, end_b, base = (s.sb(n, [P, EXPERTS]) for n in ("run_tiles", "end_a", "end_b", "base"))
        past = s.sb("past", [1, slot_tiles, EXPERTS])
        expert_f = s.sb("expert_f", [1, slot_tiles])
        slot_f = s.sb("slot_f", [P, tiles, 2])

        XL = 4
        x_loaded = [s.sem(f"x_loaded{k}") for k in range(XL)]
        bank = [s.ps(f"bank{k}", [P, 512]) for k in range(8)]

        small_loaded, diag_loaded, experts_loaded = s.sem("small_loaded"), s.sem("diag_loaded"), s.sem("experts_loaded")
        zero_filled = s.sem("zero_filled")
        const_ready, diag_cleared = s.sem("const_ready"), s.sem("diag_cleared")
        fold_pe, fold_act = s.sem("fold_pe"), s.sem("fold_act")
        stats_done, var_ready, pow_done = s.sem("stats_done"), s.sem("var_ready"), s.sem("pow_done")
        ln_step = s.sem("ln_step")
        xn_ready, xnr_ready, xt_turned, xt_ready = s.sem("xn_ready"), s.sem("xnr_ready"), s.sem("xt_turned"), s.sem("xt_ready")
        xn_stored, xt_stored = s.two_sems("xn_stored"), s.two_sems("xt_stored")
        logits_ready, logits_copied = s.sem("logits_ready"), s.sem("logits_copied")
        route, gap_ready, gap_exped, counted = (s.sem(n) for n in ("route", "gap_ready", "gap_exped", "counted"))

        N_SMALL = 3 + 4 + 2 * LANES + 2 + 2 + 7
        N_DIAG = 6
        N_CONST = 9 + 8
        with nc.Block() as block:

            @block.sync
            def _(sp):
                n = tiles // XL
                for k in range(XL):
                    sp.dma_start(x_all[:, k * n:(k + 1) * n, :], env["x_tiles"][:, k * n:(k + 1) * n, :]).then_inc(x_loaded[k], 16)
                sp.wait_ge(const_ready, N_CONST)
                rows = slots * P // (P * 1024)
                flat = env["slot_x"].rearrange("(p n) d -> p (n d)", p=P)
                for k in range(rows):
                    sp.dma_start(flat[:, k * 1024:(k + 1) * 1024], zeros[:]).then_inc(zero_filled, 16)
                assert rows * 1024 * P == slots * P

                def store(c):
                    sp.wait_ge(xn_ready, c.index + 1)
                    sp.dma_start(env["xn_tiles"][:, ds(c.index * TPC, TPC), :], xn[c.parity][:]).then_inc(xn_stored[c.parity], 16)
                    sp.wait_ge(xt_ready, c.index + 1)
                    sp.dma_start(env["xt_dram"][ds(c.index * P, P), :], xt[c.parity][:]).then_inc(xt_stored[c.parity], 16)

                with sp.Fori(0, chunks // 2) as q:
                    store(at(q, 0))
                    store(at(q, 1))
                sp.wait_ge(zero_filled, 16 * rows)
                for k in range(2):
                    sp.wait_ge(xn_stored[k], 16 * chunks // 2)
                    sp.wait_ge(xt_stored[k], 16 * chunks // 2)
                sp.wait_ge(experts_loaded, 16 * (2 + len(FF_CHUNKS)))

            @block.gpsimd
            def _(pool):
                for k in range(3):
                    pool.memset(v_in[k][:], 0.0).then_inc(diag_cleared, 1)
                pool.memset(ident[:], 0.0).then_inc(const_ready, 1)
                pool.memset(ones[:], 1.0).then_inc(const_ready, 1)
                pool.wait_ge(const_ready, 2)
                pool.affine_select(out=ident[:], in_=ident[:], compare_op=ALU.not_equal, fill=1.0, base=0,
                                   pattern=[[-1, P]], channel_multiplier=1).then_inc(const_ready, 1)
                pool.affine_select(out=before[:], in_=ones[:], compare_op=ALU.is_ge, fill=0.0, base=-1,
                                   pattern=[[1, P]], channel_multiplier=-1).then_inc(const_ready, 1)
                pool.memset(zeros[:], 0.0).then_inc(const_ready, 1)
                pool.memset(power[:, 0, :], -0.5).then_inc(const_ready, 1)
                pool.memset(power[:, 1, :], 0.5).then_inc(const_ready, 1)
                for e in range(EXPERTS):
                    pool.memset(rev_e[:, :, e], float(EXPERTS - e)).then_inc(const_ready, 1)
                pool.iota(tile_no_i[:], pattern=[[1, slot_tiles]], base=0, channel_multiplier=0).then_inc(const_ready, 1)
                pool.wait_ge(const_ready, N_CONST)
                pool.wait_ge(var_ready, 1)
                pool.tensor_tensor(rstd[:], var[:], power[:, 0, :], ALU.pow).then_inc(pow_done, 1)
                pool.wait_ge(var_ready, 2)
                pool.tensor_tensor(rstd2[:], tmp[:], power[:, 0, :], ALU.pow).then_inc(pow_done, 1)
                pool.tensor_tensor(std2[:], tmp[:], power[:, 1, :], ALU.pow).then_inc(pow_done, 1)

            @block.scalar
            def _(act):
                small = [0]

                def load(dst, src, columns=False):
                    act.dma_start(dst, src, allow_slow_non_contiguous=columns).then_inc(small_loaded, 16)
                    small[0] += 16

                for k, n in enumerate("qkv"):
                    load(u_in[k][:], w[f"{n}_U"].rearrange("d h r -> d (h r)"))
                act.wait_ge(diag_cleared, 3)
                for k, n in enumerate("qkv"):
                    by_pair = w[f"{n}_V"].rearrange("(j two) r e -> two r j e", two=2)
                    for b in range(2):
                        act.dma_start(v_in[k][b * RANK_QKV:(b + 1) * RANK_QKV, :, b * DH:(b + 1) * DH],
                                      by_pair[b]).then_inc(diag_loaded, 16)
                for dst, name in ((ln1_g, "ln1_g"), (ln1_b, "ln1_b"), (ln2_g, "ln2_g"), (ln2_b, "ln2_b")):
                    load(dst[:], w[name].rearrange("(p o) -> p o", o=1), True)
                for dst, name in ((q_b, "q_b"), (k_b, "k_b")):
                    by_lane = w[name].rearrange("(g i) (e o) -> i e g o", i=LANES, o=1)
                    for i in range(LANES):
                        load(dst[32 * i:32 * i + 32, :], by_lane[i], True)
                load(fc1_b[:], w["fc1_b"].rearrange("(c p) -> p c", p=P), True)
                load(v_b[:], w["v_b"].rearrange("h e -> (h e)").partition_broadcast(P))
                load(out_bias[:], w["out_b"].partition_broadcast(P))
                load(fc2_bias[:], w["fc2_b"].partition_broadcast(P))
                load(out_u[:], w["out_U"])
                load(out_v[:], w["out_V"])
                load(fc1_u[:], w["fc1_U"])
                load(fc1_v[:], w["fc1_V"])
                load(fc2_u[:], w["fc2_U"].rearrange("(c p) r -> p c r", p=P))
                load(fc2_v[:], w["fc2_V"])
                load(w_router[:], w["Wr"])
                act.dma_start(w_gate_up[:, :, 0:FF], w["Wg"].rearrange("e d i -> d e i")).then_inc(experts_loaded, 16)
                act.dma_start(w_gate_up[:, :, FF:2 * FF], w["Wu"].rearrange("e d i -> d e i")).then_inc(experts_loaded, 16)
                for c, (at_row, n) in enumerate(FF_CHUNKS):
                    act.dma_start(w_down[0:n, :, c, :], w["Wd"][:, at_row:at_row + n, :].rearrange("e p d -> p e d")).then_inc(experts_loaded, 16)

                for r in range(6):
                    act.wait_ge(fold_pe, r + 1)
                    act.copy(ut[0:PR, r, :], bank[r][0:PR, :]).then_inc(fold_act, 1)
                act.wait_ge(fold_pe, 7)
                act.copy(ut_small[0:RANK_OUT, 0:P], bank[7][0:RANK_OUT, 0:P]).then_inc(fold_act, 1)
                act.copy(ut_small[0:RANK_MLP, P:2 * P], bank[7][0:RANK_MLP, P:2 * P]).then_inc(fold_act, 1)
                act.wait_ge(fold_pe, 8)
                act.copy(ut_fc2[:], bank[0][0:RANK_MLP, :]).then_inc(fold_act, 1)
                assert small[0] == 16 * N_SMALL
                act.wait_ge(small_loaded, 16 * N_SMALL)
                act.wait_ge(fold_pe, 9)
                for k in range(2):
                    act.copy(raw_qkv[:, k, :].rearrange("p (i e g) -> p g i e", i=LANES, e=DH),
                             bank[6][:, k * P:(k + 1) * P].rearrange("p (g i e) -> p g i e", i=LANES, e=DH)).then_inc(fold_act, 1)
                act.copy(raw_qkv[:, 2, :], bank[6][:, 2 * P:3 * P]).then_inc(fold_act, 1)
                act.mul(g_q[:], ln1_g[:], float(DH) ** -0.5).then_inc(fold_act, 1)
                act.wait_ge(fold_pe, 10)
                act.copy(wo[:], bank[1][:, 0:P]).then_inc(fold_act, 1)
                act.wait_ge(fold_pe, 11)
                act.copy(raw_w1[:], bank[2][:]).then_inc(fold_act, 1)
                act.wait_ge(fold_pe, 12)
                act.copy(w2[:].rearrange("p c d -> p (c d)"), bank[3][:]).then_inc(fold_act, 1)
                act.wait_ge(fold_act, 16)
                act.activation(wq[:], raw_qkv[:, 0, :], ACT.Identity, scale=g_q[:]).then_inc(fold_act, 1)
                act.activation(wk[:], raw_qkv[:, 1, :], ACT.Identity, scale=ln1_g[:]).then_inc(fold_act, 1)
                act.activation(wv[:], raw_qkv[:, 2, :], ACT.Identity, scale=ln1_g[:]).then_inc(fold_act, 1)
                act.activation(w1[:], raw_w1[:], ACT.Identity, scale=ln2_g[:]).then_inc(fold_act, 1)
                act.wait_ge(const_ready, N_CONST)
                act.activation(b_rows[:], ones[:], ACT.Identity, scale=ln1_b[:]).then_inc(fold_act, 1)

                def copy_xt(c, first):
                    act.wait_ge(xt_turned, c.index + 1)
                    if not first:
                        act.wait_ge(xt_stored[c.parity], 16 * c.turn)
                    act.copy(xt[c.parity][:], bank[c.parity][:]).then_inc(xt_ready, 1)

                copy_xt(at(0, 0), True)
                copy_xt(at(0, 1), True)
                with act.Fori(1, chunks // 2) as q:
                    copy_xt(at(q, 0), False)
                    copy_xt(at(q, 1), False)
                act.wait_ge(gap_ready, 1)
                act.activation(gap_exp[:], gap[:], ACT.Exp).then_inc(gap_exped, 1)

            @block.tensor
            def _(pe):
                pe.wait_ge(const_ready, N_CONST)
                pe.wait_ge(small_loaded, 16 * N_SMALL)
                pe.wait_ge(diag_loaded, 16 * N_DIAG)
                for r in range(6):
                    for j in range(4):
                        pair = 4 * (r % 2) + j
                        last = pe.transpose(bank[r][0:PR, j * P:(j + 1) * P], u_in[r // 2][:, pair * PR:(pair + 1) * PR], ident[:])
                    last.then_inc(fold_pe, 1)
                pe.transpose(bank[7][0:RANK_OUT, 0:P], out_u[:], ident[:])
                pe.transpose(bank[7][0:RANK_MLP, P:2 * P], fc1_u[:], ident[:]).then_inc(fold_pe, 1)
                pe.wait_ge(fold_act, 1)
                for c in range(HCH):
                    last = pe.transpose(bank[0][0:RANK_MLP, c * P:(c + 1) * P], fc2_u[:, c, :], ident[:])
                last.then_inc(fold_pe, 1)
                for r in range(6):
                    pe.wait_ge(fold_act, r + 1)
                    for j in range(4):
                        pair = 4 * (r % 2) + j
                        col = (r // 2) * P + pair * 2 * DH
                        last = pe.matmul(bank[6][:, col:col + 2 * DH], ut[0:PR, r, j * P:(j + 1) * P],
                                         v_in[r // 2][:, pair, :], start=True, stop=True)
                last.then_inc(fold_pe, 1)
                pe.wait_ge(fold_act, 8)
                pe.matmul(bank[1][:, 0:P], ut_small[0:RANK_OUT, 0:P], out_v[:], start=True, stop=True).then_inc(fold_pe, 1)
                pe.matmul(bank[2][:], ut_small[0:RANK_MLP, P:2 * P], fc1_v[:], start=True, stop=True).then_inc(fold_pe, 1)
                pe.wait_ge(fold_act, 9)
                for c in range(HCH):
                    last = pe.matmul(bank[3][:, c * P:(c + 1) * P], ut_fc2[:, c * P:(c + 1) * P], fc2_v[:], start=True, stop=True)
                last.then_inc(fold_pe, 1)
                pe.wait_ge(fold_act, 21)
                pe.matmul(bank[4][:, 0:1], raw_qkv[:, 0, :], ln1_b[:], start=True, stop=True)
                pe.matmul(bank[4][:, 1:2], raw_qkv[:, 1, :], ln1_b[:], start=True, stop=True)
                for c in range(HCH):
                    pe.matmul(bank[4][:, 2 + c:3 + c], raw_w1[:, c * P:(c + 1) * P], ln2_b[:], start=True, stop=True)
                pe.matmul(bank[5][:, 0:P], b_rows[:], raw_qkv[:, 2, :], start=True, stop=True).then_inc(fold_pe, 1)

                def turn(c, first):
                    pe.wait_ge(xnr_ready, c.index + 1)
                    if not first:
                        pe.wait_ge(xt_ready, c.index - 1)
                    for t in range(TPC):
                        last = pe.transpose(bank[c.parity][:, t * P:(t + 1) * P], xnr[c.parity][:, t, :], ident[:])
                    last.then_inc(xt_turned, 1)

                def score(c, first):
                    pe.wait_ge(xt_ready, c.index + 1)
                    if not first:
                        pe.wait_ge(logits_copied, c.index - 1)
                    for t in range(TPC):
                        last = pe.matmul(bank[2 + c.parity][:, t * EXPERTS:(t + 1) * EXPERTS], xt[c.parity][:, t * P:(t + 1) * P],
                                         w_router[:], start=True, stop=True)
                    last.then_inc(logits_ready, 1)

                turn(at(0, 0), True)
                turn(at(0, 1), True)
                score(at(0, 0), True)
                turn(at(0, 2), False)
                score(at(0, 1), True)
                with pe.Fori(1, chunks // 2 - 1) as q:
                    turn(at(q, 1), False)
                    score(at(q, 0), False)
                    turn(at(q, 2), False)
                    score(at(q, 1), False)
                q = chunks // 2 - 1
                turn(at(q, 1), False)
                score(at(q, 0), False)
                score(at(q, 1), False)
                pe.wait_ge(gap_ready, 1)
                flat = chosen[:].rearrange("p t e -> p (t e)")
                for k in range(2):
                    pe.matmul(bank[4 + k][:, 0:half], before[:], flat[:, k * half:(k + 1) * half], start=True, stop=True)
                    last = pe.matmul(bank[6 + k][:, 0:half], ones[:], flat[:, k * half:(k + 1) * half], start=True, stop=True)
                last.then_inc(counted, 1)

            @block.vector
            def _(dve):
                n = tiles // XL
                for k in range(XL):
                    dve.wait_ge(x_loaded[k], 16)
                    with dve.Fori(k * n, (k + 1) * n) as t:
                        dve.bn_stats(stats[:].rearrange("p t c -> p (t c)")[:, ds(t * 6, 6)],
                                     x_all[:].rearrange("p t d -> p (t d)")[:, ds(t * P, P)]).then_inc(stats_done, 1)
                dve.wait_ge(stats_done, tiles)
                steps = [0]

                def step(ins):
                    steps[0] += 1
                    ins.then_inc(ln_step, 1)
                    dve.wait_ge(ln_step, steps[0])

                step(dve.tensor_tensor(mean[:], stats[:, :, 1], stats[:, :, 4], ALU.add))
                step(dve.tensor_tensor(tmp[:], stats[:, :, 1], stats[:, :, 4], ALU.subtract))
                step(dve.tensor_tensor(var[:], stats[:, :, 2], stats[:, :, 5], ALU.add))
                step(dve.tensor_tensor(tmp[:], tmp[:], tmp[:], ALU.mult))
                step(dve.tensor_scalar(var[:], var[:], 1.0 / P, None, ALU.mult))
                step(dve.scalar_tensor_tensor(out=var[:], in0=tmp[:], scalar=0.25, in1=var[:], op0=ALU.mult, op1=ALU.add))
                step(dve.tensor_scalar(mean[:], mean[:], 0.5, None, ALU.mult))
                step(dve.tensor_scalar(std2[:], var[:], 1.0, None, ALU.mult))
                dve.tensor_scalar(var[:], var[:], LN_EPS, None, ALU.add).then_inc(var_ready, 1)
                dve.wait_ge(pow_done, 1)
                step(dve.tensor_tensor(tmp[:], rstd[:], rstd[:], ALU.mult))
                step(dve.tensor_tensor(tmp[:], tmp[:], std2[:], ALU.mult))
                dve.tensor_scalar(tmp[:], tmp[:], LN_EPS, None, ALU.add).then_inc(var_ready, 1)
                dve.wait_ge(pow_done, 3)

                def normalise(c, first):
                    if not first:
                        dve.wait_ge(xn_stored[c.parity], 16 * c.turn)
                        dve.wait_ge(xt_turned, c.index - 1)
                    for t in range(TPC):
                        col = ds(c.index * TPC + t, 1)
                        last = dve.tensor_scalar(xn[c.parity][:, t, :], x_all[:].rearrange("p t d -> p (t d)")[:, ds((c.index * TPC + t) * P, P)],
                                                 mean[:, col], rstd[:, col], ALU.subtract, ALU.mult)
                    last.then_inc(xn_ready, 1)
                    dve.wait_ge(xn_ready, c.index + 1)
                    for t in range(TPC):
                        last = dve.tensor_scalar(xnr[c.parity][:, t, :], xn[c.parity][:, t, :], rstd2[:, ds(c.index * TPC + t, 1)], None, ALU.mult)
                    last.then_inc(xnr_ready, 1)

                def copy_logits(c):
                    dve.wait_ge(logits_ready, c.index + 1)
                    dve.tensor_tensor(logits[:].rearrange("p t e -> p (t e)")[:, ds(c.index * TPC * EXPERTS, TPC * EXPERTS)].rearrange("p (t e) -> p t e", e=EXPERTS),
                                      bank[2 + c.parity][:, 0:TPC * EXPERTS].rearrange("p (t e) -> p t e", e=EXPERTS),
                                      std2[:, ds(c.index * TPC, TPC)].unsqueeze(2).to_broadcast([P, TPC, EXPERTS]), ALU.mult).then_inc(logits_copied, 1)

                normalise(at(0, 0), True)
                normalise(at(0, 1), True)
                with dve.Fori(1, chunks // 2) as q:
                    normalise(at(q, 0), False)
                    copy_logits(at(q, -2))
                    normalise(at(q, 1), False)
                    copy_logits(at(q, -1))
                copy_logits(at(chunks // 2, -2))
                copy_logits(at(chunks // 2, -1))
                dve.wait_ge(logits_copied, chunks)

                dve.wait_ge(fold_pe, 13)
                dve.tensor_scalar(q_bias[:], bank[4][:, 0:1], q_b[:], float(DH) ** -0.5, ALU.add, ALU.mult)
                dve.tensor_tensor(k_bias[:], bank[4][:, 1:2], k_b[:], ALU.add)
                dve.tensor_tensor(mlp_bias[:], bank[4][:, 2:2 + HCH], fc1_b[:], ALU.add)
                dve.tensor_tensor(v_bias[:], bank[5][:, 0:P], v_b[:], ALU.add)

                routed = [0]

                def link(ins):
                    routed[0] += 1
                    ins.then_inc(route, 1)
                    dve.wait_ge(route, routed[0])

                def over_experts(a):
                    return a.unsqueeze(2).to_broadcast([P, tiles, EXPERTS])

                left = logits
                for k in range(2):
                    link(dve.tensor_reduce(top[k][:], left[:], AX.X, ALU.max))
                    link(dve.tensor_tensor(work[:], left[:], over_experts(top[k][:]), ALU.is_equal))
                    link(dve.tensor_tensor(work[:], work[:], rev_e[:], ALU.mult))
                    link(dve.tensor_reduce(key[:], work[:], AX.X, ALU.max))
                    link(dve.tensor_tensor(pick[k][:], rev_e[:], over_experts(key[:]), ALU.is_equal))
                    if k == 0:
                        link(dve.scalar_tensor_tensor(out=scan_a[:], in0=pick[0][:], scalar=-3e38, in1=logits[:], op0=ALU.mult, op1=ALU.add))
                        left = scan_a
                link(dve.tensor_tensor(chosen[:], pick[0][:], pick[1][:], ALU.add))
                dve.tensor_tensor(gap[:], top[1][:], top[0][:], ALU.subtract).then_inc(gap_ready, 1)
                dve.wait_ge(gap_exped, 1)
                link(dve.tensor_scalar(gap_sum[:], gap_exp[:], 1.0, None, ALU.add))
                link(dve.reciprocal(mix[:, :, 0], gap_sum[:]))
                link(dve.tensor_tensor(mix[:, :, 1], mix[:, :, 0], gap_exp[:], ALU.mult))
                dve.wait_ge(counted, 1)
                for k in range(2):
                    link(dve.tensor_copy(work[:].rearrange("p t e -> p (t e)")[:, k * half:(k + 1) * half], bank[6 + k][:, 0:half]))
                src, dst, far = work, scan_a, 1
                while far < tiles:
                    dve.tensor_copy(dst[:, 0:far, :], src[:, 0:far, :])
                    link(dve.tensor_tensor(dst[:, far:, :], src[:, far:, :], src[:, 0:tiles - far, :], ALU.add))
                    src, dst, far = dst, scan_b if dst is scan_a else scan_a, 2 * far
                link(dve.tensor_scalar(count_f[:], src[:, tiles - 1, :], float(P - 1), None, ALU.add))
                link(dve.tensor_copy(count_i[:], count_f[:]))
                link(dve.tensor_scalar(count_i[:], count_i[:], 7, None, ALU.arith_shift_right))
                link(dve.tensor_copy(run_tiles[:], count_i[:]))
                e_src, e_dst, far = run_tiles, end_a, 1
                while far < EXPERTS:
                    dve.tensor_copy(e_dst[:, 0:far], e_src[:, 0:far])
                    link(dve.tensor_tensor(e_dst[:, far:], e_src[:, far:], e_src[:, 0:EXPERTS - far], ALU.add))
                    e_src, e_dst, far = e_dst, end_b if e_dst is end_a else end_a, 2 * far
                link(dve.tensor_tensor(base[:], e_src[:], run_tiles[:], ALU.subtract))
                link(dve.tensor_scalar(base[:], base[:], float(P), None, ALU.mult))
                link(dve.tensor_tensor(work[:], src[:], work[:], ALU.subtract))
                link(dve.tensor_tensor(work[:], work[:], base[:].unsqueeze(1).to_broadcast([P, tiles, EXPERTS]), ALU.add))
                for k in range(2):
                    part = work[:].rearrange("p t e -> p (t e)")[:, k * half:(k + 1) * half]
                    link(dve.tensor_tensor(part, bank[4 + k][:, 0:half], part, ALU.add))
                for k in range(2):
                    link(dve.tensor_tensor(pick[k][:], pick[k][:], work[:], ALU.mult))
                    link(dve.tensor_reduce(slot_f[:, :, k], pick[k][:], AX.X, ALU.add))
                dve.tensor_copy(slot_of[:], slot_f[:].rearrange("p t k -> p (t k)"))
                link(dve.tensor_copy(tile_no[:], tile_no_i[:]))
                link(dve.tensor_tensor(past[:], tile_no[:].unsqueeze(2).to_broadcast([1, slot_tiles, EXPERTS]),
                                       e_src[0:1, :].unsqueeze(1).to_broadcast([1, slot_tiles, EXPERTS]), ALU.is_ge))
                link(dve.tensor_reduce(expert_f[:], past[:], AX.X, ALU.add))
                link(dve.tensor_scalar(expert_f[:], expert_f[:], float(EXPERTS - 1), None, ALU.min))
                link(dve.tensor_copy(tile_expert[:], expert_f[:]))


def attention(nc, env):
    chunks, slots = env["chunks"], env["slots"]
    ident, wq, wk, wv, wo = env["ident"], env["wq"], env["wk"], env["wv"], env["wo"]
    q_bias, k_bias, v_bias, out_bias = env["q_bias"], env["k_bias"], env["v_bias"], env["out_bias"]
    ln2_stats, slot_of = env["ln2_stats"], env["slot_of"]
    UNITS = 12
    STACKS = PARTS * (1 + LANES)
    PT = 8

    with ExitStack() as stack:
        s = Scope(nc, stack, "att")
        ident_b = s.sb("ident_b", [P, P], BF16)
        mask_st = s.sb("mask_st", [P, LANES, P], BF16)
        mask_ts = s.sb("mask_ts", [P, LANES, P], BF16)
        xt = s.two("xt", [P, CHUNK])
        xn = s.two("xn", [P, TPC, P])
        slot_now = s.two("slot_now", [P, 2 * TPC], U32)
        q_hi, q_lo, k_hi, k_lo = (s.sb(n, [P, CHUNK], F32R) for n in ("q_hi", "q_lo", "k_hi", "k_lo"))
        q_stack = s.two("q_stack", [P, GROUPS, LANES, CHUNK], F32R)
        k_stack = s.two("k_stack", [P, GROUPS, CHUNK], F32R)
        v_ones = s.two("v_ones", [P, TPC, HEADS, 32])
        row_max = s.two("row_max", [P, 2, HEADS])
        neg_max = [s.sb(f"neg_max{b}", [HEADS, SEQ], F32R) for b in range(2)]
        probs = s.sb("probs", [P, PT, CHUNK])
        ctx_t = s.sb("ctx_t", [P, GROUPS * SEQ])
        ctx_inv = s.sb("ctx_inv", [P, 2, HEADS])
        ctx = s.sb("ctx", [P, 2, P])
        ctx_turned = s.sb("ctx_turned", [P, SEQ])
        h = s.two("h", [P, SEQ])

        t_ps = [s.ps(f"t_ps{k}", [P, CHUNK]) for k in range(2)]
        m_ps = [s.ps(f"m_ps{k}", [P, CHUNK]) for k in range(2)]
        pv_ps = s.ps("pv_ps", [P, GROUPS * SEQ])
        free_ps = [s.ps(f"free_ps{k}", [P, CHUNK]) for k in range(2)]

        const_ready, cleared = s.sem("const_ready"), s.sem("cleared")
        xt_loaded, xn_loaded = s.two_sems("xt_loaded"), s.two_sems("xn_loaded")
        q_done, k_done, v_done = s.sem("q_done"), s.sem("k_done"), s.sem("v_done")
        q_hi_ready, k_hi_ready = s.sem("q_hi_ready"), s.sem("k_hi_ready")
        q_split, k_split, v_ready = s.sem("q_split"), s.sem("k_split"), s.sem("v_ready")
        stack_free, stacked = s.sem("stack_free"), s.two_sems("stacked")
        max_scores, max_taken = s.sem("max_scores"), s.sem("max_taken")
        max_turned, max_copied = s.sem("max_turned"), s.sem("max_copied")
        max_stacked = s.two_sems("max_stacked")
        scores_done, exp_done = s.sem("scores_done"), s.sem("exp_done")
        pv_done, ctx_copied = s.sem("pv_done"), s.sem("ctx_copied")
        ctx_back, inv_ready, ctx_ready = s.sem("ctx_back"), s.sem("inv_ready"), s.sem("ctx_ready")
        ctx_again, ctx_turned_ready = s.sem("ctx_again"), s.sem("ctx_turned_ready")
        out_done, h_done, h_stored = s.sem("out_done"), s.sem("h_done"), s.two_sems("h_stored")
        x_out_ready, slot_ready = s.sem("x_out_ready"), s.sem("slot_ready")
        scatter_started, scattered = s.sem("scatter_started"), s.two_sems("scattered")

        EARLY = UNITS + 3
        MAX_SLOTS, m = {}, 0
        for slot, n in [(s_, 2 if s_ % 3 == 2 else 1) for s_ in range(12, 21)] + [(21, 1), (22, 1), (23, 1), (0, 2)] + [(s_, 1) for s_ in range(1, 8)]:
            MAX_SLOTS[slot] = [(int(m < EARLY), u) for u in range(m, m + n)]
            m += n
        assert m == 2 * UNITS

        last_chunk = chunks - 1

        with nc.Block() as block:

            @block.sync
            def _(sp):
                def load_xt(c):
                    sp.dma_start(xt[c.parity][:], env["xt_dram"][ds(c.index * P, P), :]).then_inc(xt_loaded[c.parity], 16)

                def load_xn(c):
                    sp.dma_start(xn[c.parity][:], env["xn_tiles"][:, ds(c.index * TPC, TPC), :]).then_inc(xn_loaded[c.parity], 16)

                def stack_parts(c):
                    sp.wait_ge(q_split, c.index + 1)
                    sp.wait_ge(k_split, c.index + 1)
                    for part, k in enumerate((k_hi, k_lo, k_hi)):
                        sp.dma_start(k_stack[c.parity][32 * part:32 * part + 32, :, :].bitcast(F32), k[:].bitcast(F32)).then_inc(stacked[c.parity], 16)
                    for part, q in enumerate((q_hi, q_hi, q_lo)):
                        for i in range(LANES):
                            to = 32 * part + DH * i
                            sp.dma_start(q_stack[c.parity][to:to + DH, :, i, :].bitcast(F32),
                                         q[32 * i:32 * i + 32, :].bitcast(F32)).then_inc(stacked[c.parity], 16)

                def stack_max(c, b):
                    sp.wait_ge(max_copied, 2 * c.index + b + 1)
                    sp.dma_start(q_stack[c.parity][ROWS:ROWS + 1, :, :, b * SEQ:(b + 1) * SEQ].bitcast(F32),
                                 neg_max[b][:].bitcast(F32)).then_inc(max_stacked[b], 16)

                def store_h(c, b):
                    seq = 2 * c.index + b
                    sp.wait_ge(h_done, seq + 1)
                    sp.dma_start(env["h_tiles"][:, ds(2 * seq, 2), :], h[b][:].rearrange("p (t d) -> p t d", d=P)).then_inc(h_stored[b], 16)

                def step(half, d):
                    p = at(half, d)
                    first, last = (isinstance(p.index, int) and p.index == k for k in (0, last_chunk))
                    three_ahead = not (isinstance(p.index, int) and p.index >= last_chunk - 2)
                    if not first and not last:
                        sp.wait_ge(scores_done, 2 * UNITS * p.index)
                        sp.sem_inc(stack_free, 1)
                        stack_parts(at(half, d + 1))
                    if not first:
                        store_h(at(half, d - 1), 0)
                    if three_ahead:
                        sp.wait_ge(v_done, p.index + 2)
                        load_xt(at(half, d + 3))
                    stack_max(p, 1)
                    if not first:
                        store_h(at(half, d - 1), 1)
                        if not last:
                            load_xn(at(half, d + 1))
                    if not last:
                        stack_max(at(half, d + 1), 0)

                load_xt(at(0, 0))
                load_xt(at(0, 1))
                load_xn(at(0, 0))
                load_xn(at(0, 1))
                sp.wait_ge(cleared, 6)
                sp.wait_ge(v_done, 1)
                load_xt(at(0, 2))
                stack_parts(at(0, 0))
                stack_parts(at(0, 1))
                stack_max(at(0, 0), 0)
                step(0, 0)
                with sp.Fori(0, chunks // 2 - 2) as half:
                    step(half, 1)
                    step(half, 2)
                step(chunks // 2 - 2, 1)
                step(chunks // 2 - 1, 0)
                step(chunks // 2 - 1, 1)
                for b in range(2):
                    store_h(at(chunks // 2 - 1, 1), b)
                    sp.wait_ge(h_stored[b], 16 * chunks)

            @block.gpsimd
            def _(pool):
                pool.memset(mask_st[:], 0.0).then_inc(const_ready, 1)
                pool.memset(mask_ts[:], 0.0).then_inc(const_ready, 1)
                pool.tensor_copy(ident_b[:], ident[:]).then_inc(const_ready, 1)
                pool.wait_ge(const_ready, 2)
                pool.affine_select(out=mask_st[:], in_=mask_st[:], compare_op=ALU.is_ge, fill=MASKED, base=0,
                                   pattern=[[0, LANES], [-1, P]], channel_multiplier=1).then_inc(const_ready, 1)
                pool.affine_select(out=mask_ts[:], in_=mask_ts[:], compare_op=ALU.is_ge, fill=MASKED, base=0,
                                   pattern=[[0, LANES], [1, P]], channel_multiplier=-1).then_inc(const_ready, 1)
                pool.memset(v_ones[0][:], 1.0).then_inc(cleared, 1)
                pool.memset(q_stack[1][:].bitcast(F32), 0.0).then_inc(cleared, 1)
                pool.memset(v_ones[1][:], 1.0).then_inc(cleared, 1)

                def scatter(c, col):
                    t, k = divmod(col, 2)
                    pool.indirect_dma_start(env["slot_x"][:], bass.IndirectOffsetOnAxis(ap=slot_now[c.parity][:, col:col + 1], axis=0),
                                            xn[c.parity][:, t, :], None).then_inc(scattered[c.parity], 16)

                def step(half, d):
                    p = at(half, d)
                    pool.tensor_copy(slot_now[p.parity][:], slot_of[:, ds(p.index * 2 * TPC, 2 * TPC)]).then_inc(slot_ready, 1)
                    pool.wait_ge(xn_loaded[p.parity], 16 * (p.turn + 1))
                    pool.wait_ge(slot_ready, p.index + 1)
                    pool.sem_inc(scatter_started, 1)
                    for col in range(2 * TPC):
                        scatter(p, col)
                    pool.wait_ge(scattered[p.parity], 16 * 2 * TPC * (p.turn + 1))
                    pool.tensor_tensor(xn[p.parity][:], xn[p.parity][:], out_bias[:].unsqueeze(1).to_broadcast([P, TPC, P]), ALU.add).then_inc(x_out_ready, 1)

                step(0, 0)
                step(0, 1)
                with pool.Fori(1, chunks // 2) as half:
                    step(half, 0)
                    step(half, 1)

            @block.tensor
            def _(pe):
                def project_q(c, bank, free, n):
                    pe.wait_ge(xt_loaded[c.parity], 16 * (c.turn + 1))
                    pe.wait_ge(free, n) if n is not None else None
                    pe.matmul(free_ps[bank][:], wq[:], xt[c.parity][:], start=True, stop=True).then_inc(q_done, 1)

                def project_k(c, bank, free, n):
                    pe.wait_ge(free, n) if n is not None else None
                    pe.matmul(free_ps[bank][:], wk[:], xt[c.parity][:], start=True, stop=True).then_inc(k_done, 1)

                def project_v(c, bank, free, n):
                    pe.wait_ge(free, n)
                    for t in range(TPC):
                        last = pe.matmul(free_ps[bank][:, t * P:(t + 1) * P], xt[c.parity][:, t * P:(t + 1) * P], wv[:], start=True, stop=True)
                    last.then_inc(v_done, 1)

                def max_unit(c, m):
                    b, u = divmod(m, UNITS)
                    wide, i = divmod(u, LANES)
                    ps, q, k = m_ps[m % 2], q_stack[c.parity], k_stack[c.parity]
                    lo, hi = b * SEQ, b * SEQ + P
                    if m == 0:
                        pe.wait_ge(stacked[c.parity], 16 * STACKS * (c.turn + 1))
                    if not (isinstance(c.index, int) and c.index == 0 and m < 2):
                        pe.wait_ge(max_taken, 2 * UNITS * c.index + m - 1)
                    if wide < 2:
                        for n in range(2):
                            g = 2 * wide + n
                            pe.matmul(ps[:, n * SEQ:(n + 1) * SEQ], q[0:ROWS, g, i, hi:hi + P], k[0:ROWS, g, lo:lo + SEQ],
                                      start=(n == 0), stop=False, skip_group_check=True)
                        last = pe.matmul(ps[:].rearrange("p (n t) -> p n t", n=2)[:, :, P:SEQ], ident_b[:], mask_st[:, 0:2, :],
                                         start=False, stop=True, skip_group_check=True)
                    else:
                        for g in range(GROUPS):
                            pe.matmul(ps[:, g * P:(g + 1) * P], q[0:ROWS, g, i, lo:lo + P], k[0:ROWS, g, lo:lo + P],
                                      start=(g == 0), stop=False, skip_group_check=True)
                        last = pe.matmul(ps[:], ident_b[:], mask_st[:].rearrange("p g t -> p (g t)"), start=False, stop=True, skip_group_check=True)
                    last.then_inc(max_scores, 1)

                def score_unit(c, m):
                    b, u = divmod(m, UNITS)
                    rows = slice(0, ROWS + 1)
                    ps, q, k = t_ps[m % 2], q_stack[c.parity], k_stack[c.parity]
                    lo, hi, end = b * SEQ, b * SEQ + P, (b + 1) * SEQ
                    if u == 0:
                        pe.wait_ge(max_stacked[b], 16 * (c.index + 1))
                    if not (isinstance(c.index, int) and c.index == 0 and m < 2):
                        pe.wait_ge(exp_done, 2 * UNITS * c.index + m - 1)
                    if u < 8:
                        g, pair = divmod(u, 2)
                        keys, queries, lanes = k[rows, g, lo:hi], slice(lo, end), slice(2 * pair, 2 * pair + 2)
                    else:
                        g = u - 8
                        keys, queries, lanes = k[rows, g, hi:end], slice(hi, end), slice(0, LANES)
                    by_lane = ps[:].rearrange("p (i s) -> p i s", s=queries.stop - queries.start)
                    pe.matmul(by_lane, keys, q[rows, g, lanes, queries], start=True, stop=False, skip_group_check=True)
                    pe.matmul(by_lane[:, :, 0:P], ident_b[:], mask_ts[:, lanes, :], start=False, stop=True, skip_group_check=True).then_inc(scores_done, 1)

                def probs_times_v(c, n):
                    b, wide = divmod(n, 3)
                    pe.wait_ge(exp_done, 2 * UNITS * c.index + 4 * (n + 1))
                    if n == 0:
                        pe.wait_ge(v_ready, c.index + 1)
                    if wide == 0 and not (isinstance(c.index, int) and c.index == 0 and b == 0):
                        pe.wait_ge(ctx_copied, 2 * c.index + b)
                    for n_g in range(2 if wide < 2 else GROUPS):
                        for i in range(LANES):
                            if wide < 2:
                                g = 2 * wide + n_g
                                pt = probs[:, (4 * n + 2 * n_g + i // 2) % PT, i % 2 * SEQ:(i % 2 + 1) * SEQ]
                                last = pe.matmul(pv_ps[32 * i:32 * i + 32, g * SEQ:(g + 1) * SEQ], v_ones[c.parity][:, 2 * b, g * LANES + i, :],
                                                 pt, start=(n_g == 0), stop=False, skip_group_check=True)
                            else:
                                g = n_g
                                pt = probs[:, (4 * n + g) % PT, i * P:(i + 1) * P]
                                last = pe.matmul(pv_ps[32 * i:32 * i + 32, g * SEQ + P:(g + 1) * SEQ], v_ones[c.parity][:, 2 * b + 1, g * LANES + i, :],
                                                 pt, start=False, stop=(g % 2 == 1), skip_group_check=True)
                    last.then_inc(pv_done, 1)

                def turn_max(c, b, bank, free, n):
                    pe.wait_ge(max_taken, UNITS * (2 * c.index + b + 1))
                    pe.wait_ge(free, n)
                    for t in range(2):
                        last = pe.transpose(free_ps[bank][0:HEADS, t * P:(t + 1) * P], row_max[b][:, t, :], ident[:])
                    last.then_inc(max_turned, 1)

                def context_back(seq, t, bank, free, n):
                    pe.wait_ge(ctx_copied, seq + 1)
                    pe.wait_ge(free, n)
                    for g in range(GROUPS):
                        last = pe.transpose(free_ps[bank][:, g * P:(g + 1) * P], ctx_t[:, g * SEQ + t * P:g * SEQ + (t + 1) * P], ident[:])
                    last.then_inc(ctx_back, 1)

                def context_again(seq, bank, free, n):
                    pe.wait_ge(ctx_ready, 2 * seq + 2)
                    pe.wait_ge(free, n)
                    for t in range(2):
                        last = pe.transpose(free_ps[bank][:, t * P:(t + 1) * P], ctx[:, t, :], ident[:])
                    last.then_inc(ctx_again, 1)

                def project_out(seq, bank, free, n):
                    pe.wait_ge(ctx_turned_ready, seq + 1)
                    pe.wait_ge(free, n)
                    for t in range(2):
                        last = pe.matmul(free_ps[bank][:, t * P:(t + 1) * P], ctx_turned[:, t * P:(t + 1) * P], wo[:], start=True, stop=True)
                    last.then_inc(out_done, 1)

                def step(half, d):
                    p, nxt, far = at(half, d), at(half, d + 1), at(half, d + 2)
                    x = p.index
                    first, last = (isinstance(x, int) and x == k for k in (0, last_chunk))
                    two_left = isinstance(x, int) and x >= last_chunk - 1
                    before, here = 2 * x - 1, 2 * x
                    for slot in range(2 * UNITS):
                        score_unit(p, slot)
                        if slot == 2 and not first:
                            probs_times_v(at(half, d - 1), 5)
                        if slot == 3 and not last:
                            if first:
                                project_v(nxt, 0, max_copied, 1)
                            else:
                                project_v(nxt, 0, h_done, before)
                        if slot == 4 and not first:
                            context_back(before, 0, 1, ctx_turned_ready, before)
                        if slot == 5 and not first:
                            if last:
                                context_back(before, 1, 0, h_done, before)
                            else:
                                context_back(before, 1, 0, v_ready, x + 2)
                        if slot == 6:
                            probs_times_v(p, 0)
                        if slot == 8 and not first:
                            context_again(before, 1, ctx_ready, 2 * before + 1)
                        if slot == 8:
                            if first:
                                turn_max(p, 1, 0, v_ready, 2)
                            else:
                                turn_max(p, 1, 0, ctx_ready, 2 * before + 2)
                        if slot == 10:
                            probs_times_v(p, 1)
                        if slot == 11 and not first:
                            project_out(before, 1, ctx_turned_ready, before + 1)
                        if slot == 14:
                            probs_times_v(p, 2)
                        if slot == 17:
                            context_back(here, 0, 0, max_copied, 2 * x + 2)
                        if slot == 18:
                            probs_times_v(p, 3)
                            if first:
                                context_back(here, 1, 1, k_split, 2)
                            else:
                                context_back(here, 1, 1, h_done, 2 * x)
                        if slot == 19 and not two_left:
                            project_q(far, 0, ctx_ready, 2 * here + 1)
                        if slot == 20 and not two_left:
                            project_k(far, 1, ctx_ready, 2 * here + 2)
                        if slot == 21 and not last:
                            if two_left:
                                turn_max(nxt, 0, 0, ctx_ready, 2 * here + 1)
                            else:
                                turn_max(nxt, 0, 0, q_split, x + 3)
                        if slot == 22:
                            probs_times_v(p, 4)
                            if two_left:
                                context_again(here, 1, ctx_ready, 2 * here + 2)
                            else:
                                context_again(here, 1, k_split, x + 3)
                        if slot == 23:
                            if last:
                                project_out(here, 0, ctx_ready, 2 * here + 1)
                            else:
                                project_out(here, 0, max_copied, 2 * x + 3)
                        for ahead, m in MAX_SLOTS.get(slot, ()):
                            if not (ahead and last):
                                max_unit(at(half, d + ahead), m)

                pe.wait_ge(const_ready, 5)
                project_q(at(0, 0), 1, None, None)
                project_k(at(0, 0), 0, None, None)
                project_v(at(0, 0), 1, q_split, 1)
                project_q(at(0, 1), 0, k_split, 1)
                project_k(at(0, 1), 1, v_ready, 1)
                pe.wait_ge(cleared, 6)
                for m in range(EARLY):
                    max_unit(at(0, 0), m)
                turn_max(at(0, 0), 0, 0, q_split, 2)
                step(0, 0)
                with pe.Fori(0, chunks // 2 - 2) as half:
                    step(half, 1)
                    step(half, 2)
                step(chunks // 2 - 2, 1)
                step(chunks // 2 - 1, 0)
                step(chunks // 2 - 1, 1)
                probs_times_v(at(chunks // 2 - 1, 1), 5)
                end = 2 * chunks - 1
                context_back(end, 0, 1, ctx_turned_ready, end)
                context_back(end, 1, 0, h_done, end)
                context_again(end, 1, ctx_ready, 2 * end + 1)
                project_out(end, 0, ctx_ready, 2 * end + 2)

            @block.scalar
            def _(act):
                def high_q(c, bank):
                    act.wait_ge(q_done, c.index + 1)
                    if not (isinstance(c.index, int) and c.index == 0):
                        prev = (1 - c.parity, c.turn if c.parity else c.turn - 1)
                        act.wait_ge(stacked[prev[0]], 16 * STACKS * (prev[1] + 1))
                    act.activation(q_hi[:], free_ps[bank][:], ACT.Identity, bias=q_bias[:]).then_inc(q_hi_ready, 1)

                def high_k(c, bank):
                    act.wait_ge(k_done, c.index + 1)
                    act.activation(k_hi[:], free_ps[bank][:], ACT.Identity, bias=k_bias[:]).then_inc(k_hi_ready, 1)

                def exp_unit(c, m):
                    act.wait_ge(scores_done, 2 * UNITS * c.index + m + 1)
                    if m % 4 == 0 and not (isinstance(c.index, int) and c.index == 0 and m < PT):
                        act.wait_ge(pv_done, 6 * c.index + m // 4 - 1)
                    act.activation(probs[:, m % PT, :], t_ps[m % 2][:], ACT.Exp).then_inc(exp_done, 1)

                def copy_context(seq):
                    act.wait_ge(pv_done, 3 * (seq + 1))
                    if not (isinstance(seq, int) and seq == 0):
                        act.wait_ge(ctx_back, 2 * seq)
                    act.copy(ctx_t[:], pv_ps[:]).then_inc(ctx_copied, 1)

                def copy_turned(seq, bank):
                    act.wait_ge(ctx_again, seq + 1)
                    if not (isinstance(seq, int) and seq == 0):
                        act.wait_ge(out_done, seq)
                    act.copy(ctx_turned[:], free_ps[bank][:, 0:SEQ]).then_inc(ctx_turned_ready, 1)

                def step(half, d):
                    p, far = at(half, d), at(half, d + 2)
                    x = p.index
                    first = isinstance(x, int) and x == 0
                    two_left = isinstance(x, int) and x >= last_chunk - 1
                    for slot in range(2 * UNITS):
                        exp_unit(p, slot)
                        if slot == 2 and not first:
                            copy_context(2 * x - 1)
                        if slot == 8 and not first:
                            copy_turned(2 * x - 1, 1)
                        if slot == 14:
                            copy_context(2 * x)
                        if slot == 19 and not two_left:
                            high_q(far, 0)
                        if slot == 20 and not two_left:
                            high_k(far, 1)
                        if slot == 22:
                            copy_turned(2 * x, 1)

                high_q(at(0, 0), 1)
                high_k(at(0, 0), 0)
                high_q(at(0, 1), 0)
                high_k(at(0, 1), 1)
                step(0, 0)
                with act.Fori(0, chunks // 2 - 2) as half:
                    step(half, 1)
                    step(half, 2)
                step(chunks // 2 - 2, 1)
                step(chunks // 2 - 1, 0)
                step(chunks // 2 - 1, 1)
                copy_context(2 * chunks - 1)
                copy_turned(2 * chunks - 1, 1)

            @block.vector
            def _(dve):
                def low_q(c, bank):
                    dve.wait_ge(q_hi_ready, c.index + 1)
                    dve.scalar_tensor_tensor(out=q_lo[:], in0=free_ps[bank][:], scalar=q_bias[:], in1=q_hi[:].bitcast(F32),
                                             op0=ALU.add, op1=ALU.subtract).then_inc(q_split, 1)

                def low_k(c, bank):
                    dve.wait_ge(k_hi_ready, c.index + 1)
                    dve.scalar_tensor_tensor(out=k_lo[:], in0=free_ps[bank][:], scalar=k_bias[:], in1=k_hi[:].bitcast(F32),
                                             op0=ALU.add, op1=ALU.subtract).then_inc(k_split, 1)

                def copy_v(c, bank):
                    dve.wait_ge(v_done, c.index + 1)
                    dve.tensor_tensor(v_ones[c.parity][:, :, :, 0:DH], free_ps[bank][:].rearrange("p (t h e) -> p t h e", t=TPC, e=DH),
                                      v_bias[:].rearrange("p (h e) -> p h e", e=DH).unsqueeze(1).to_broadcast([P, TPC, HEADS, DH]), ALU.add).then_inc(v_ready, 1)

                def take_max(c, m):
                    b, u = divmod(m, UNITS)
                    wide, i = divmod(u, LANES)
                    dve.wait_ge(max_scores, 2 * UNITS * c.index + m + 1)
                    if u == 0 and not (isinstance(c.index, int) and c.index == 0):
                        dve.wait_ge(max_turned, 2 * c.index + b - 1)
                    n, t, g = (2, 1, 2 * wide) if wide < 2 else (GROUPS, 0, 0)
                    heads = row_max[b][:, t, :].rearrange("p (g i) -> p g i", i=LANES)[:, g:g + n, i]
                    dve.tensor_reduce(heads, m_ps[m % 2][:].rearrange("p (n t) -> p n t", n=n), AX.X, ALU.max).then_inc(max_taken, 1)

                def copy_max(c, b):
                    dve.wait_ge(max_turned, 2 * c.index + b + 1)
                    if not (isinstance(c.index, int) and c.index == 0):
                        dve.wait_ge(max_stacked[b], 16 * c.index)
                    dve.tensor_scalar(neg_max[b][:], free_ps[0][0:HEADS, 0:SEQ], -1.0, None, ALU.mult).then_inc(max_copied, 1)

                def normalise(seq, t, bank):
                    n = 2 * seq + t
                    dve.wait_ge(ctx_back, n + 1)
                    if t == 0 and not (isinstance(seq, int) and seq == 0):
                        dve.wait_ge(ctx_again, seq)
                    rows = free_ps[bank][:].rearrange("p (h c) -> p h c", c=32)
                    dve.reciprocal(ctx_inv[:, t, :], rows[:, :, DH]).then_inc(inv_ready, 1)
                    dve.wait_ge(inv_ready, n + 1)
                    dve.tensor_tensor(ctx[:, t, :].rearrange("p (h e) -> p h e", e=DH), rows[:, :, 0:DH],
                                      ctx_inv[:, t, :].unsqueeze(2).to_broadcast([P, HEADS, DH]), ALU.mult).then_inc(ctx_ready, 1)

                def add_residual(seq, c, b, bank):
                    dve.wait_ge(out_done, seq + 1)
                    dve.wait_ge(x_out_ready, c.index + 1)
                    if not (isinstance(c.index, int) and c.index == 0):
                        dve.wait_ge(h_stored[b], 16 * c.index)
                    dve.tensor_tensor(h[b][:], free_ps[bank][:, 0:SEQ], xn[c.parity][:, 2 * b:2 * b + 2, :].rearrange("p t d -> p (t d)"), ALU.add).then_inc(h_done, 1)
                    dve.wait_ge(h_done, seq + 1)
                    for t in range(2):
                        dve.bn_stats(ln2_stats[:, ds((seq * 2 + t) * 6, 6)], h[b][:, t * P:(t + 1) * P])

                def step(half, d):
                    p, prev, nxt, far = at(half, d), at(half, d - 1), at(half, d + 1), at(half, d + 2)
                    x = p.index
                    first, last = (isinstance(x, int) and x == k for k in (0, last_chunk))
                    two_left = isinstance(x, int) and x >= last_chunk - 1
                    for slot in range(2 * UNITS):
                        if slot == 3 and not last:
                            copy_v(nxt, 0)
                        if slot == 4 and not first:
                            normalise(2 * x - 1, 0, 1)
                        if slot == 5 and not first:
                            normalise(2 * x - 1, 1, 0)
                        if slot == 8:
                            copy_max(p, 1)
                        if slot == 11 and not first:
                            add_residual(2 * x - 1, prev, 1, 1)
                        if slot == 17:
                            normalise(2 * x, 0, 0)
                        if slot == 18:
                            normalise(2 * x, 1, 1)
                        if slot == 19 and not two_left:
                            low_q(far, 0)
                        if slot == 20 and not two_left:
                            low_k(far, 1)
                        if slot == 21 and not last:
                            copy_max(nxt, 0)
                        if slot == 23:
                            add_residual(2 * x, p, 0, 0)
                        for ahead, m in MAX_SLOTS.get(slot, ()):
                            if not (ahead and last):
                                take_max(at(half, d + ahead), m)

                dve.memset(q_stack[0][:].bitcast(F32), 0.0).then_inc(cleared, 1)
                for k in range(2):
                    dve.memset(k_stack[k][ROWS:ROWS + 1, :, :].bitcast(F32), 1.0).then_inc(cleared, 1)
                low_q(at(0, 0), 1)
                low_k(at(0, 0), 0)
                dve.wait_ge(cleared, 6)
                copy_v(at(0, 0), 1)
                low_q(at(0, 1), 0)
                low_k(at(0, 1), 1)
                for m in range(EARLY):
                    take_max(at(0, 0), m)
                copy_max(at(0, 0), 0)
                step(0, 0)
                with dve.Fori(0, chunks // 2 - 2) as half:
                    step(half, 1)
                    step(half, 2)
                step(chunks // 2 - 2, 1)
                step(chunks // 2 - 1, 0)
                step(chunks // 2 - 1, 1)
                normalise(2 * chunks - 1, 0, 1)
                normalise(2 * chunks - 1, 1, 0)
                add_residual(2 * chunks - 1, at(chunks // 2 - 1, 1), 1, 0)


def experts(nc, env):
    slot_tiles = env["slot_tiles"]
    ident, w_gate_up, w_down, tile_expert = env["ident"], env["w_gate_up"], env["w_down"], env["tile_expert"]
    gate_up_cols = w_gate_up[:].rearrange("p e f -> p (e f)")
    down_cols = w_down[:].rearrange("p e c d -> p (e c d)")
    NCH = len(FF_CHUNKS)

    with ExitStack() as stack:
        s = Scope(nc, stack, "moe")
        x = s.two("x", [P, P])
        x_t = s.two("x_t", [P, P])
        gate = s.two("gate", [P, FF])
        hidden = s.two("hidden", [P, FF])
        hidden_t = s.two("hidden_t", [P, NCH * P])
        y = s.two("y", [P, P])
        x_ps = [s.ps(f"x_ps{k}", [P, 512]) for k in range(2)]
        gate_ps = [s.ps(f"gate_ps{k}", [P, 512]) for k in range(2)]
        up_ps = [s.ps(f"up_ps{k}", [P, 512]) for k in range(2)]
        hidden_ps, y_ps = s.ps("hidden_ps", [P, 512]), s.ps("y_ps", [P, 512])

        x_loaded, y_stored = s.two_sems("x_loaded"), s.two_sems("y_stored")
        x_turned, x_copied, gate_up_done = s.sem("x_turned"), s.sem("x_copied"), s.sem("gate_up_done")
        gate_done, hidden_done, hidden_turned = s.sem("gate_done"), s.sem("hidden_done"), s.sem("hidden_turned")
        hidden_copied, down_done, y_copied = s.sem("hidden_copied"), s.sem("down_done"), s.sem("y_copied")

        def run(eng, first_step, step):
            end = (slot_tiles - 4) // 2
            first_step()
            step(0, 1, 3)
            step(0, 2, 3)
            with eng.Fori(1, end) as half:
                step(half, 1, 3)
                step(half, 2, 3)
            for j in range(2 * end + 1, slot_tiles):
                step(j // 2, j % 2, min(3, slot_tiles - j))

        with nc.Block() as block:

            @block.sync
            def _(sp):
                def load(c, early=False):
                    if not early:
                        sp.wait_ge(x_turned, c.index - 1)
                    sp.dma_start(x[c.parity][:], env["slot_x"][ds(c.index * P, P), :]).then_inc(x_loaded[c.parity], 16)

                load(at(0, 0), True)
                load(at(0, 1), True)
                with sp.Fori(1, slot_tiles // 2) as half:
                    load(at(half, 0))
                    load(at(half, 1))

            @block.gpsimd
            def _(pool):
                def store(c):
                    pool.wait_ge(y_copied, c.index + 1)
                    pool.dma_start(env["slot_y"][ds(c.index * P, P), :], y[c.parity][:]).then_inc(y_stored[c.parity], 16)

                with pool.Fori(0, slot_tiles // 2) as half:
                    store(at(half, 0))
                    store(at(half, 1))
                for k in range(2):
                    pool.wait_ge(y_stored[k], 16 * (slot_tiles // 2))

            @block.tensor
            def _(pe):
                def turn_x(c, early=False):
                    pe.wait_ge(x_loaded[c.parity], 16 * (c.turn + 1))
                    if not early:
                        pe.wait_ge(x_copied, c.index - 1)
                    pe.transpose(x_ps[c.parity][:, 0:P], x[c.parity][:], ident[:]).then_inc(x_turned, 1)

                def gate_up(c, early=False):
                    e = pe.value_load(tile_expert[0:1, ds(c.index, 1)], min_val=0, max_val=EXPERTS - 1)
                    pe.wait_ge(x_copied, c.index + 1)
                    if not early:
                        pe.wait_ge(hidden_done, c.index - 1)
                    pe.matmul(gate_ps[c.parity][:, 0:FF], x_t[c.parity][:], gate_up_cols[:, ds(e * (2 * FF), FF)], start=True, stop=True)
                    pe.matmul(up_ps[c.parity][:, 0:FF], x_t[c.parity][:], gate_up_cols[:, ds(e * (2 * FF) + FF, FF)], start=True, stop=True).then_inc(gate_up_done, 1)

                def turn_hidden(c, early=False):
                    pe.wait_ge(hidden_done, c.index + 1)
                    if not early:
                        pe.wait_ge(hidden_copied, c.index)
                    for k, (col, n) in enumerate(FF_CHUNKS):
                        last = pe.transpose(hidden_ps[0:n, k * P:(k + 1) * P], hidden[c.parity][:, col:col + n], ident[:])
                    last.then_inc(hidden_turned, 1)

                def down(c, early=False):
                    e = pe.value_load(tile_expert[0:1, ds(c.index, 1)], min_val=0, max_val=EXPERTS - 1)
                    pe.wait_ge(hidden_copied, c.index + 1)
                    if not early:
                        pe.wait_ge(y_copied, c.index)
                    for k, (col, n) in enumerate(FF_CHUNKS):
                        last = pe.matmul(y_ps[:, 0:P], hidden_t[c.parity][0:n, k * P:(k + 1) * P],
                                         down_cols[0:n, ds(e * (NCH * P) + k * P, P)], start=(k == 0), stop=(k == NCH - 1))
                    last.then_inc(down_done, 1)

                def first_step():
                    turn_x(at(0, 0), True)
                    turn_x(at(0, 1), True)
                    gate_up(at(0, 0), True)
                    turn_x(at(0, 2))
                    gate_up(at(0, 1), True)
                    turn_hidden(at(0, 0), True)

                def step(half, d, left):
                    if left > 2:
                        turn_x(at(half, d + 2))
                    if left > 1:
                        gate_up(at(half, d + 1))
                    turn_hidden(at(half, d))
                    c = at(half, d - 1)
                    down(c, isinstance(c.index, int) and c.index == 0)

                run(pe, first_step, step)
                down(at(slot_tiles // 2, -1))

            @block.scalar
            def _(act):
                def silu(c, early=False):
                    act.wait_ge(gate_up_done, c.index + 1)
                    if not early:
                        act.wait_ge(hidden_done, c.index - 1)
                    act.activation(gate[c.parity][:], gate_ps[c.parity][:, 0:FF], ACT.Silu).then_inc(gate_done, 1)

                def copy_hidden(c, early=False):
                    act.wait_ge(hidden_turned, c.index + 1)
                    if not early and not (isinstance(c.index, int) and c.index == 1):
                        act.wait_ge(down_done, c.index - 1)
                    whole = FF_CHUNKS[-1][0]
                    rest = FF_CHUNKS[-1][1]
                    act.copy(hidden_t[c.parity][:, 0:whole], hidden_ps[:, 0:whole])
                    act.copy(hidden_t[c.parity][0:rest, whole:whole + P], hidden_ps[0:rest, whole:whole + P]).then_inc(hidden_copied, 1)

                def first_step():
                    silu(at(0, 0), True)
                    silu(at(0, 1), True)
                    copy_hidden(at(0, 0), True)

                def step(half, d, left):
                    if left > 1:
                        silu(at(half, d + 1))
                    copy_hidden(at(half, d))

                run(act, first_step, step)

            @block.vector
            def _(dve):
                def copy_x(c, early=False):
                    dve.wait_ge(x_turned, c.index + 1)
                    if not early:
                        dve.wait_ge(gate_up_done, c.index - 1)
                    dve.tensor_copy(x_t[c.parity][:], x_ps[c.parity][:, 0:P]).then_inc(x_copied, 1)

                def gated(c, early=False):
                    dve.wait_ge(gate_done, c.index + 1)
                    if not early:
                        dve.wait_ge(hidden_turned, c.index - 1)
                    dve.tensor_tensor(hidden[c.parity][:], gate[c.parity][:], up_ps[c.parity][:, 0:FF], ALU.mult).then_inc(hidden_done, 1)

                def copy_y(c):
                    dve.wait_ge(down_done, c.index + 1)
                    if not (isinstance(c.turn, int) and c.turn == 0):
                        dve.wait_ge(y_stored[c.parity], 16 * c.turn)
                    dve.tensor_copy(y[c.parity][:], y_ps[:, 0:P]).then_inc(y_copied, 1)

                def first_step():
                    copy_x(at(0, 0), True)
                    copy_x(at(0, 1), True)
                    gated(at(0, 0), True)
                    copy_x(at(0, 2))
                    gated(at(0, 1), True)

                def step(half, d, left):
                    if left > 2:
                        copy_x(at(half, d + 2))
                    if left > 1:
                        gated(at(half, d + 1))
                    copy_y(at(half, d - 1))

                run(dve, first_step, step)
                copy_y(at(slot_tiles // 2, -1))


def mlp_and_combine(nc, env):
    chunks, tiles = env["chunks"], env["tiles"]
    ident, w1, w2, mlp_bias, fc2_bias = env["ident"], env["w1"], env["w2"], env["mlp_bias"], env["fc2_bias"]
    mix, slot_of, ln2_stats = env["mix"], env["slot_of"], env["ln2_stats"]
    mix_cols = mix[:].rearrange("p t k -> p (t k)")

    with ExitStack() as stack:
        s = Scope(nc, stack, "mlp")
        mean, var, tmp, rstd, power = (s.sb(n, [P, tiles]) for n in ("mean", "var", "tmp", "rstd", "power"))
        hn = s.two("hn", [P, TPC, P])
        hn_t = s.two("hn_t", [P, CHUNK])
        mid = s.two("mid", [P, HCH, CHUNK])
        h = s.two("h", [P, TPC, P])
        x = s.two("x", [P, TPC, P])
        h_again = s.two("h_again", [P, TPC, P])
        total = s.two("total", [P, TPC, P])
        slot_now = s.two("slot_now", [P, 2 * TPC], U32)
        rows = s.two("rows", [P, 2 * TPC, P])
        t_ps = s.ps("t_ps", [P, CHUNK])
        f_ps = [s.ps(f"f_ps{k}", [P, CHUNK]) for k in range(HCH)]
        o_ps = [s.ps(f"o_ps{k}", [P, CHUNK]) for k in range(2)]

        power_ready, var_ready, rstd_ready, ln_step = (s.sem(n) for n in ("power_ready", "var_ready", "rstd_ready", "ln_step"))
        hn_ready, hn_turned, hn_copied = s.sem("hn_ready"), s.sem("hn_turned"), s.sem("hn_copied")
        fc1_done, mid_ready, fc2_done = s.sem("fc1_done"), s.sem("mid_ready"), s.sem("fc2_done")
        gather_started = s.sem("gather_started")
        h_loaded = s.two_sems("h_loaded")
        x_loaded, gathered, stored = s.two_sems("x_loaded"), s.two_sems("gathered"), s.two_sems("stored")
        slot_ready, sum_step, total_ready = s.sem("slot_ready"), s.sem("sum_step"), s.sem("total_ready")
        SUMS = 3 + 2

        def run(eng, step):
            with eng.Fori(0, chunks // 2 - 1) as half:
                step(half, 0, 3)
                step(half, 1, 3)
            step(chunks // 2 - 1, 0, 2)
            step(chunks // 2 - 1, 1, 1)

        with nc.Block() as block:

            @block.sync
            def _(sp):
                def load_h(c):
                    sp.dma_start(h[c.parity][:], env["h_tiles"][:, ds(c.index * TPC, TPC), :]).then_inc(h_loaded[c.parity], 16)

                def load_residual(c):
                    sp.dma_start(x[c.parity][:], env["x_tiles"][:, ds(c.index * TPC, TPC), :]).then_inc(x_loaded[c.parity], 16)
                    sp.dma_start(h_again[c.parity][:], env["h_tiles"][:, ds(c.index * TPC, TPC), :]).then_inc(x_loaded[c.parity], 16)

                def step(half, d, left):
                    c = at(half, d)
                    if left > 4:
                        sp.wait_ge(hn_ready, c.index + 3)
                        load_h(at(half, d + 4))
                    sp.wait_ge(total_ready, c.index + 1)
                    sp.dma_start(env["out_tiles"][:, ds(c.index * TPC, TPC), :], total[c.parity][:]).then_inc(stored[c.parity], 16)
                    if left > 2:
                        load_residual(at(half, d + 2))

                for d in range(2):
                    load_h(at(0, d))
                for d in range(2):
                    load_residual(at(0, d))
                for d in range(2):
                    sp.wait_ge(hn_ready, d + 1)
                    load_h(at(0, d + 2))
                with sp.Fori(0, chunks // 2 - 2) as half:
                    step(half, 0, 5)
                    step(half, 1, 5)
                for j in range(chunks - 4, chunks):
                    step(j // 2, j % 2, chunks - j)
                for k in range(2):
                    sp.wait_ge(stored[k], 16 * (chunks // 2))

            @block.gpsimd
            def _(pool):
                pool.memset(power[:], -0.5).then_inc(power_ready, 1)
                pool.wait_ge(power_ready, 1)
                pool.wait_ge(var_ready, 1)
                pool.tensor_tensor(rstd[:], var[:], power[:], ALU.pow).then_inc(rstd_ready, 1)

                def gather(c, again):
                    if again:
                        pool.wait_ge(total_ready, c.index - 1)
                    pool.tensor_copy(slot_now[c.parity][:], slot_of[:, ds(c.index * 2 * TPC, 2 * TPC)]).then_inc(slot_ready, 1)
                    pool.wait_ge(slot_ready, c.index + 1)
                    pool.sem_inc(gather_started, 1)
                    for col in range(2 * TPC):
                        pool.indirect_dma_start(rows[c.parity][:, col, :], None, env["slot_y"][:],
                                                bass.IndirectOffsetOnAxis(ap=slot_now[c.parity][:, col:col + 1], axis=0)).then_inc(gathered[c.parity], 16)

                gather(at(0, 0), False)
                gather(at(0, 1), False)
                with pool.Fori(1, chunks // 2) as half:
                    gather(at(half, 0), True)
                    gather(at(half, 1), True)

            @block.tensor
            def _(pe):
                def turn(c, early=False):
                    pe.wait_ge(hn_ready, c.index + 1)
                    if not early:
                        pe.wait_ge(hn_copied, c.index)
                    for t in range(TPC):
                        last = pe.transpose(t_ps[:, t * P:(t + 1) * P], hn[c.parity][:, t, :], ident[:])
                    last.then_inc(hn_turned, 1)

                def fc1(c, k, early=False):
                    pe.wait_ge(hn_copied, c.index + 1)
                    if not early:
                        pe.wait_ge(mid_ready, HCH * (c.index - 1) + k + 1)
                    pe.matmul(f_ps[k][:], w1[:, k * P:(k + 1) * P], hn_t[c.parity][:], start=True, stop=True).then_inc(fc1_done, 1)

                def fc2(c, t):
                    if t == 0:
                        pe.wait_ge(mid_ready, HCH * (c.index + 1))
                        if not (isinstance(c.index, int) and c.index < 2):
                            pe.wait_ge(total_ready, c.index - 1)
                    for k in range(HCH):
                        last = pe.matmul(o_ps[c.parity][:, t * P:(t + 1) * P], mid[c.parity][:, k, t * P:(t + 1) * P], w2[:, k, :],
                                         start=(k == 0), stop=(k == HCH - 1))
                    if t == TPC - 1:
                        last.then_inc(fc2_done, 1)

                def step(half, d, left):
                    if left > 2:
                        turn(at(half, d + 2))
                    for k in range(HCH):
                        if left > 1:
                            fc1(at(half, d + 1), k)
                        fc2(at(half, d), k)

                turn(at(0, 0), True)
                turn(at(0, 1))
                for k in range(HCH):
                    fc1(at(0, 0), k, True)
                step(0, 0, 3)
                step(0, 1, 3)
                with pe.Fori(1, chunks // 2 - 1) as half:
                    step(half, 0, 3)
                    step(half, 1, 3)
                step(chunks // 2 - 1, 0, 2)
                step(chunks // 2 - 1, 1, 1)

            @block.scalar
            def _(act):
                def copy_turned(c, early=False):
                    act.wait_ge(hn_turned, c.index + 1)
                    if not early:
                        act.wait_ge(fc1_done, HCH * (c.index - 1))
                    act.copy(hn_t[c.parity][:], t_ps[:]).then_inc(hn_copied, 1)

                def gelu(c, k, early=False):
                    act.wait_ge(fc1_done, HCH * c.index + k + 1)
                    if not early and k == 0:
                        act.wait_ge(fc2_done, c.index - 1)
                    act.activation(mid[c.parity][:, k, :], f_ps[k][:], ACT.Gelu_apprx_tanh, bias=mlp_bias[:, k:k + 1]).then_inc(mid_ready, 1)

                def step(half, d, left, early=False):
                    if left > 2:
                        copy_turned(at(half, d + 2))
                    if left > 1:
                        for k in range(HCH):
                            gelu(at(half, d + 1), k, early)

                copy_turned(at(0, 0), True)
                copy_turned(at(0, 1), True)
                for k in range(HCH):
                    gelu(at(0, 0), k, True)
                step(0, 0, 3, True)
                step(0, 1, 3)
                with act.Fori(1, chunks // 2 - 1) as half:
                    step(half, 0, 3)
                    step(half, 1, 3)
                step(chunks // 2 - 1, 0, 2)

            @block.vector
            def _(dve):
                steps = [0]

                def step_of(ins):
                    steps[0] += 1
                    ins.then_inc(ln_step, 1)
                    dve.wait_ge(ln_step, steps[0])

                parts = ln2_stats[:].rearrange("p (t c) -> p t c", c=6)
                step_of(dve.tensor_tensor(mean[:], parts[:, :, 1], parts[:, :, 4], ALU.add))
                step_of(dve.tensor_tensor(tmp[:], parts[:, :, 1], parts[:, :, 4], ALU.subtract))
                step_of(dve.tensor_tensor(var[:], parts[:, :, 2], parts[:, :, 5], ALU.add))
                step_of(dve.tensor_tensor(tmp[:], tmp[:], tmp[:], ALU.mult))
                step_of(dve.tensor_scalar(var[:], var[:], 1.0 / P, LN_EPS, ALU.mult, ALU.add))
                step_of(dve.tensor_scalar(mean[:], mean[:], 0.5, None, ALU.mult))
                dve.scalar_tensor_tensor(out=var[:], in0=tmp[:], scalar=0.25, in1=var[:], op0=ALU.mult, op1=ALU.add).then_inc(var_ready, 1)
                dve.wait_ge(rstd_ready, 1)

                def normalise(c, early=False):
                    dve.wait_ge(h_loaded[c.parity], 16 * (c.turn + 1))
                    if not early:
                        dve.wait_ge(hn_turned, c.index - 1)
                    for t in range(TPC):
                        tile = c.index * TPC + t
                        last = dve.tensor_scalar(hn[c.parity][:, t, :], h[c.parity][:, t, :], mean[:, ds(tile, 1)], rstd[:, ds(tile, 1)],
                                                 ALU.subtract, ALU.mult)
                    last.then_inc(hn_ready, 1)

                def add_up(c):
                    sums = total[c.parity]
                    dve.wait_ge(x_loaded[c.parity], 32 * (c.turn + 1))
                    if not (isinstance(c.turn, int) and c.turn == 0):
                        dve.wait_ge(stored[c.parity], 16 * c.turn)
                    done = SUMS * c.index
                    dve.tensor_tensor(sums[:], x[c.parity][:], h_again[c.parity][:], ALU.add).then_inc(sum_step, 1)
                    dve.wait_ge(sum_step, done + 1)
                    dve.tensor_tensor(sums[:], sums[:], fc2_bias[:].unsqueeze(1).to_broadcast([P, TPC, P]), ALU.add).then_inc(sum_step, 1)
                    dve.wait_ge(sum_step, done + 2)
                    dve.wait_ge(fc2_done, c.index + 1)
                    dve.tensor_tensor(sums[:], o_ps[c.parity][:].rearrange("p (t d) -> p t d", d=P), sums[:], ALU.add).then_inc(sum_step, 1)
                    dve.wait_ge(sum_step, done + 3)
                    dve.wait_ge(gathered[c.parity], 16 * 2 * TPC * (c.turn + 1))
                    for k in range(2):
                        for t in range(TPC):
                            last = dve.scalar_tensor_tensor(out=sums[:, t, :], in0=rows[c.parity][:, 2 * t + k, :], scalar=mix_cols[:, ds(c.index * 2 * TPC + 2 * t + k, 1)],
                                                            in1=sums[:, t, :], op0=ALU.mult, op1=ALU.add)
                        last.then_inc(sum_step, 1)
                        dve.wait_ge(sum_step, done + 4 + k)
                    dve.sem_inc(total_ready, 1)

                def step(half, d, left):
                    if left > 2:
                        normalise(at(half, d + 2))
                    add_up(at(half, d))

                normalise(at(0, 0), True)
                normalise(at(0, 1), True)
                step(0, 0, 3)
                step(0, 1, 3)
                with dve.Fori(1, chunks // 2 - 1) as half:
                    step(half, 0, 3)
                    step(half, 1, 3)
                step(chunks // 2 - 1, 0, 2)
                step(chunks // 2 - 1, 1, 1)


_ATTN = ("ln1_g", "ln1_b", "ln2_g", "ln2_b", "q_U", "q_V", "q_b", "k_U", "k_V", "k_b", "v_U", "v_V", "v_b",
         "out_U", "out_V", "out_b", "fc1_U", "fc1_V", "fc1_b", "fc2_U", "fc2_V", "fc2_b")
_FFN = ("Wr", "Wg", "Wu", "Wd")


def kernel(**inputs):
    import numpy as _np
    import concourse.bacc as _bacc
    from concourse import mybir as _mybir
    from concourse.bass_utils import run_bass_kernel_spmd as _run

    nc = _bacc.Bacc("TRN2", target_bir_lowering=False, num_devices=1)
    arrays = {}

    def given(name):
        a = _np.ascontiguousarray(inputs[name])
        arrays[f"in_{name}"] = a
        return nc.dram_tensor(f"in_{name}", a.shape, _mybir.dt.from_np(a.dtype), kind="ExternalInput").ap()

    x = given("L0_attn_hidden_states")
    w = {n: given(f"L0_attn_{n}") for n in _ATTN} | {n: given(f"L0_ffn_{n}") for n in _FFN}
    out = nc.dram_tensor("out", arrays["in_L0_attn_hidden_states"].shape, F32, kind="ExternalOutput").ap()
    layer_kernel(nc, x, w, out)
    r = _run(nc, [arrays], core_ids=[0])
    return r.results[0]["out"]
```

```python
from collections import namedtuple
from contextlib import ExitStack

import concourse.bass as bass
from concourse import mybir

F32 = mybir.dt.float32
F32R = mybir.dt.float32r
BF16 = mybir.dt.bfloat16
I32 = mybir.dt.int32
U32 = mybir.dt.uint32
ALU = mybir.AluOpType
ACT = mybir.ActivationFunctionType
AX = mybir.AxisListType
ds = bass.ds

P = 128
SEQ = 256
CHUNK = 512
TPC = CHUNK // P
HEADS, DH = 16, 8
LANES = 4
GROUPS = HEADS // LANES
PARTS = 3
ROWS = PARTS * LANES * DH
LN_EPS = 1e-5
MASKED, LOWEST = -1e30, -3e38
EXPERTS, FF = 9, 352
FF_CHUNKS = ((0, 128), (128, 128), (256, 96))
HID = 512
HCH = HID // P
RANK_QKV, RANK_OUT, RANK_MLP = 48, 96, 64

Step = namedtuple("Step", "index parity turn")


def at(half, d):
    return Step(2 * half + d, d % 2, half + d // 2)


def layer_kernel(nc, x_in, w, out):
    tokens = x_in.shape[0] * x_in.shape[1]
    tiles = tokens // P
    chunks = tokens // CHUNK
    slot_tiles = (2 * tokens + EXPERTS * (P - 1)) // P
    slots = slot_tiles * P

    x_rows = x_in.rearrange("b s d -> (b s) d")
    out_rows = out.rearrange("b s d -> (b s) d")
    x_tiles = x_rows.rearrange("(n p) d -> p n d", p=P)
    out_tiles = out_rows.rearrange("(n p) d -> p n d", p=P)

    xn_dram = nc.dram_tensor("xn_scratch", [tokens, P], F32, kind="Internal").ap()
    xt_dram = nc.dram_tensor("xt_scratch", [chunks * P, CHUNK], F32, kind="Internal").ap()
    slot_x = nc.dram_tensor("slot_x", [slots, P], F32, kind="Internal").ap()
    slot_row = nc.dram_tensor("slot_row", [slots, 1], F32, kind="Internal").ap()
    y_dram = nc.dram_tensor("y_scratch", [2 * tokens + slots, P], F32, kind="Internal").ap()
    h_dram = nc.dram_tensor("h_scratch", [tokens, P], F32, kind="Internal").ap()
    xn_tiles = xn_dram.rearrange("(n p) d -> p n d", p=P)
    h_tiles = h_dram.rearrange("(n p) d -> p n d", p=P)

    whole = ExitStack()

    def keep(name, shape, dtype=F32):
        return whole.enter_context(nc.sbuf_tensor(name, shape, dtype))

    with whole:
        ident = keep("ident", [P, P])
        wq = keep("wq", [P, P])
        wk = keep("wk", [P, P])
        wv = keep("wv", [P, P])
        wo = keep("wo", [P, P])
        w1 = keep("w1", [P, HID])
        w2 = keep("w2", [P, HCH, P])
        q_bias = keep("q_bias", [P, 1])
        k_bias = keep("k_bias", [P, 1])
        v_bias = keep("v_bias", [P, P])
        mlp_bias = keep("mlp_bias", [P, HCH])
        out_bias = keep("out_bias", [P, P])
        fc2_bias = keep("fc2_bias", [P, P])
        w_gate_up = keep("w_gate_up", [P, EXPERTS, 2 * FF], F32R)
        even_stack = keep("even_stack", [P, GROUPS * LANES * CHUNK], F32R)
        assert EXPERTS * 2 * FF <= GROUPS * LANES * CHUNK
        w_hi = even_stack[:, 0:EXPERTS * 2 * FF].rearrange("p (e f) -> p e f", e=EXPERTS)
        w_down = keep("w_down", [P, EXPERTS, len(FF_CHUNKS), P])
        mix = keep("mix", [P, tiles, 2])
        slot_of = keep("slot_of", [P, tiles * 2], U32)
        tile_expert = keep("tile_expert", [1, slot_tiles], I32)
        ln2_stats = keep("ln2_stats", [P, tiles * 6])

        prepare(nc, locals())
        attention(nc, locals())
        experts(nc, locals())
        mlp_and_combine(nc, locals())


class Scope:

    def __init__(self, nc, stack, prefix):
        self.nc, self.stack, self.prefix = nc, stack, prefix

    def sb(self, name, shape, dtype=F32):
        return self.stack.enter_context(self.nc.sbuf_tensor(f"{self.prefix}_{name}", shape, dtype))

    def two(self, name, shape, dtype=F32):
        return [self.sb(f"{name}{k}", shape, dtype) for k in range(2)]

    def ps(self, name, shape):
        return self.stack.enter_context(self.nc.psum_tensor(f"{self.prefix}_{name}", shape, F32))

    def sem(self, name):
        return self.stack.enter_context(self.nc.semaphore(f"{self.prefix}_{name}"))

    def two_sems(self, name):
        return [self.sem(f"{name}{k}") for k in range(2)]


def inverse_root(dve, step, x, y, bits, tmp):
    step(dve.tensor_scalar(bits, x.bitcast(I32), 1, None, ALU.arith_shift_right))
    step(dve.tensor_scalar(y.bitcast(I32), bits, -1.0, float(0x5F3759DF), ALU.mult, ALU.add))
    for _ in range(3):
        step(dve.tensor_tensor(tmp, y, y, ALU.mult))
        step(dve.scalar_tensor_tensor(out=tmp, in0=tmp, scalar=-0.5, in1=x, op0=ALU.mult, op1=ALU.mult))
        step(dve.scalar_tensor_tensor(out=y, in0=tmp, scalar=1.5, in1=y, op0=ALU.add, op1=ALU.mult))


def prepare(nc, env):
    w = env["w"]
    tiles, chunks, slot_tiles, slots = env["tiles"], env["chunks"], env["slot_tiles"], env["slots"]
    ident, wq, wk, wv, wo = env["ident"], env["wq"], env["wk"], env["wv"], env["wo"]
    w1, w2, w_gate_up, w_down = env["w1"], env["w2"], env["w_gate_up"], env["w_down"]
    q_bias, k_bias, v_bias, mlp_bias = env["q_bias"], env["k_bias"], env["v_bias"], env["mlp_bias"]
    out_bias, fc2_bias = env["out_bias"], env["fc2_bias"]
    mix, slot_of, tile_expert = env["mix"], env["slot_of"], env["tile_expert"]
    PAIRS = HEADS // 2
    PR = 2 * RANK_QKV
    cols = tiles * EXPERTS
    half = cols // 2
    FILL = 8

    with ExitStack() as stack:
        s = Scope(nc, stack, "prep")
        x_all = s.sb("x_all", [P, tiles, P])
        u_in = [s.sb(f"u_{n}", [P, HEADS * RANK_QKV]) for n in "qkv"]
        v_in = [s.sb(f"v_{n}", [PR, PAIRS, 2 * DH]) for n in "qkv"]
        out_u, out_v = s.sb("out_u", [P, RANK_OUT]), s.sb("out_v", [RANK_OUT, P])
        fc1_u, fc1_v = s.sb("fc1_u", [P, RANK_MLP]), s.sb("fc1_v", [RANK_MLP, HID])
        fc2_u, fc2_v = s.sb("fc2_u", [P, HCH, RANK_MLP]), s.sb("fc2_v", [RANK_MLP, P])
        w_router = s.sb("w_router", [P, EXPERTS])
        ln1_g, ln1_b = s.sb("ln1_g", [P, 1]), s.sb("ln1_b", [P, 1])
        ln2_g, ln2_b = s.sb("ln2_g", [P, 1]), s.sb("ln2_b", [P, 1])
        q_b, k_b, fc1_b = s.sb("q_b", [P, 1]), s.sb("k_b", [P, 1]), s.sb("fc1_b", [P, HCH])
        v_b = s.sb("v_b", [P, P])
        zeros = s.sb("zeros", [P, FILL * P])
        spare_i, spare = s.sb("spare_i", [P, slot_tiles], I32), s.sb("spare", [P, slot_tiles])
        ones = s.sb("ones", [P, P])
        before = s.sb("before", [P, P])
        rev_e = s.sb("rev_e", [P, tiles, EXPERTS])
        tile_no_i, tile_no = s.sb("tile_no_i", [1, slot_tiles], I32), s.sb("tile_no", [1, slot_tiles])
        ut = s.sb("ut", [P, 6, 4 * P])
        ut_small = s.sb("ut_small", [P, 2 * P])
        ut_fc2 = s.sb("ut_fc2", [RANK_MLP, HCH * P])
        raw_qkv, raw_w1 = s.sb("raw_qkv", [P, 3, P]), s.sb("raw_w1", [P, HID])
        g_q = s.sb("g_q", [P, 1])
        b_rows = s.sb("b_rows", [P, P])
        stats = s.sb("stats", [P, tiles, 6])
        mean, var, tmp = s.sb("mean", [P, tiles]), s.sb("var", [P, tiles]), s.sb("tmp", [P, tiles])
        root_bits = s.sb("root_bits", [P, tiles], I32)
        rstd, rstd2, std2 = s.sb("rstd", [P, tiles]), s.sb("rstd2", [P, tiles]), s.sb("std2", [P, tiles])
        xn = s.two("xn", [P, TPC, P])
        xnr = s.two("xnr", [P, TPC, P])
        xt = s.two("xt", [P, CHUNK])
        logits = s.sb("logits", [P, tiles, EXPERTS])
        work = s.sb("work", [P, tiles, EXPERTS])
        pick = [s.sb(f"pick{k}", [P, tiles, EXPERTS]) for k in range(2)]
        top = [s.sb(f"top{k}", [P, tiles]) for k in range(2)]
        key = s.sb("key", [P, tiles])
        chosen, left = (s.sb(n, [P, tiles, EXPERTS]) for n in ("chosen", "left"))
        tile_count = s.sb("tile_count", [tiles, EXPERTS])
        earlier = s.sb("earlier", [tiles, tiles, EXPERTS])
        gap, gap_exp, gap_sum = s.sb("gap", [P, tiles]), s.sb("gap_exp", [P, tiles]), s.sb("gap_sum", [P, tiles])
        count_f, count_i = s.sb("count_f", [P, EXPERTS]), s.sb("count_i", [P, EXPERTS], I32)
        run_tiles, end_a, end_b, base = (s.sb(n, [P, EXPERTS]) for n in ("run_tiles", "end_a", "end_b", "base"))
        past = s.sb("past", [1, slot_tiles, EXPERTS])
        expert_f = s.sb("expert_f", [1, slot_tiles])
        slot_f = s.sb("slot_f", [P, tiles, 2])

        XL = 4
        x_loaded = [s.sem(f"x_loaded{k}") for k in range(XL)]
        bank = [s.ps(f"bank{k}", [P, 512]) for k in range(8)]

        small_loaded, diag_loaded, experts_loaded = s.sem("small_loaded"), s.sem("diag_loaded"), s.sem("experts_loaded")
        router_loaded, zero_filled, spare_ready = s.sem("router_loaded"), s.sem("zero_filled"), s.sem("spare_ready")
        const_ready, diag_cleared = s.sem("const_ready"), s.sem("diag_cleared")
        fold_pe, fold_act = s.sem("fold_pe"), s.sem("fold_act")
        stats_done = s.sem("stats_done")
        ln_step = s.sem("ln_step")
        xn_ready, xnr_ready, xt_turned, xt_ready = s.sem("xn_ready"), s.sem("xnr_ready"), s.sem("xt_turned"), s.sem("xt_ready")
        xn_stored, xt_stored = s.two_sems("xn_stored"), s.two_sems("xt_stored")
        logits_ready, logits_copied = s.sem("logits_ready"), s.sem("logits_copied")
        route, gap_ready, gap_exped = (s.sem(n) for n in ("route", "gap_ready", "gap_exped"))
        tile_counted, earlier_ready, counted = (s.sem(n) for n in ("tile_counted", "earlier_ready", "counted"))

        N_SMALL = 3 + 4 + 2 * LANES + 2 + 2 + 6
        N_DIAG = 6
        N_CONST = 7 + 8
        with nc.Block() as block:

            @block.sync
            def _(sp):
                n = tiles // XL
                for k in range(XL):
                    sp.dma_start(x_all[:, k * n:(k + 1) * n, :], env["x_tiles"][:, k * n:(k + 1) * n, :]).then_inc(x_loaded[k], 16)

                def store_xn(c):
                    sp.wait_ge(xn_ready, c.index + 1)
                    sp.dma_start(env["xn_tiles"][:, ds(c.index * TPC, TPC), :], xn[c.parity][:]).then_inc(xn_stored[c.parity], 16)

                def store_xt(c):
                    sp.wait_ge(xt_ready, c.index + 1)
                    sp.dma_start(env["xt_dram"][ds(c.index * P, P), :], xt[c.parity][:]).then_inc(xt_stored[c.parity], 16)

                store_xn(at(0, 0))
                store_xn(at(0, 1))
                with sp.Fori(0, chunks // 2 - 1) as q:
                    store_xt(at(q, 0))
                    store_xn(at(q, 2))
                    store_xt(at(q, 1))
                    store_xn(at(q, 3))
                store_xt(at(chunks // 2 - 1, 0))
                store_xt(at(chunks // 2 - 1, 1))
                sp.wait_ge(zero_filled, 16 * (slots // (FILL * P) + 1))
                for k in range(2):
                    sp.wait_ge(xn_stored[k], 16 * chunks // 2)
                    sp.wait_ge(xt_stored[k], 16 * chunks // 2)
                sp.wait_ge(experts_loaded, 16 * (2 + len(FF_CHUNKS)))

            @block.gpsimd
            def _(pool):
                for k in range(3):
                    pool.memset(v_in[k][:], 0.0).then_inc(diag_cleared, 1)
                pool.memset(ident[:], 0.0).then_inc(const_ready, 1)
                pool.memset(ones[:], 1.0).then_inc(const_ready, 1)
                pool.wait_ge(const_ready, 2)
                pool.affine_select(out=ident[:], in_=ident[:], compare_op=ALU.not_equal, fill=1.0, base=0,
                                   pattern=[[-1, P]], channel_multiplier=1).then_inc(const_ready, 1)
                pool.affine_select(out=before[:], in_=ones[:], compare_op=ALU.is_ge, fill=0.0, base=-1,
                                   pattern=[[1, P]], channel_multiplier=-1).then_inc(const_ready, 1)
                pool.memset(zeros[:], 0.0).then_inc(const_ready, 1)
                for e in range(EXPERTS):
                    pool.memset(rev_e[:, :, e], float(EXPERTS - e)).then_inc(const_ready, 1)
                pool.iota(tile_no_i[:], pattern=[[1, slot_tiles]], base=0, channel_multiplier=0).then_inc(const_ready, 1)
                pool.iota(spare_i[:], pattern=[[1, slot_tiles]], base=2 * env["tokens"], channel_multiplier=slot_tiles).then_inc(spare_ready, 1)
                pool.wait_ge(spare_ready, 1)
                pool.tensor_copy(spare[:], spare_i[:]).then_inc(spare_ready, 1)
                pool.wait_ge(spare_ready, 2)
                pool.dma_start(env["slot_row"].rearrange("(p n) o -> p (n o)", p=P), spare[:]).then_inc(zero_filled, 16)
                pool.wait_ge(const_ready, N_CONST)
                pool.wait_ge(xn_ready, chunks)
                assert slots % (FILL * P) == 0
                for k in range(slots // (FILL * P)):
                    pool.dma_start(env["slot_x"][k * FILL * P:(k + 1) * FILL * P, :].rearrange("(p n) d -> p (n d)", p=P), zeros[:]).then_inc(zero_filled, 16)

            @block.scalar
            def _(act):
                small = [0]

                def load(dst, src, columns=False):
                    act.dma_start(dst, src, allow_slow_non_contiguous=columns).then_inc(small_loaded, 16)
                    small[0] += 16

                for k, n in enumerate("qkv"):
                    load(u_in[k][:], w[f"{n}_U"].rearrange("d h r -> d (h r)"))
                act.wait_ge(diag_cleared, 3)
                for k, n in enumerate("qkv"):
                    by_pair = w[f"{n}_V"].rearrange("(j two) r e -> two r j e", two=2)
                    for b in range(2):
                        act.dma_start(v_in[k][b * RANK_QKV:(b + 1) * RANK_QKV, :, b * DH:(b + 1) * DH],
                                      by_pair[b]).then_inc(diag_loaded, 16)
                for dst, name in ((ln1_g, "ln1_g"), (ln1_b, "ln1_b"), (ln2_g, "ln2_g"), (ln2_b, "ln2_b")):
                    load(dst[:], w[name].rearrange("(p o) -> p o", o=1), True)
                for dst, name in ((q_b, "q_b"), (k_b, "k_b")):
                    by_lane = w[name].rearrange("(g i) (e o) -> i e g o", i=LANES, o=1)
                    for i in range(LANES):
                        load(dst[32 * i:32 * i + 32, :], by_lane[i], True)
                load(fc1_b[:], w["fc1_b"].rearrange("(c p) -> p c", p=P), True)
                load(v_b[:], w["v_b"].rearrange("h e -> (h e)").partition_broadcast(P))
                load(out_bias[:], w["out_b"].partition_broadcast(P))
                load(fc2_bias[:], w["fc2_b"].partition_broadcast(P))
                load(out_u[:], w["out_U"])
                load(out_v[:], w["out_V"])
                load(fc1_u[:], w["fc1_U"])
                load(fc1_v[:], w["fc1_V"])
                load(fc2_u[:], w["fc2_U"].rearrange("(c p) r -> p c r", p=P))
                load(fc2_v[:], w["fc2_V"])
                act.dma_start(w_router[:], w["Wr"]).then_inc(router_loaded, 16)
                act.dma_start(w_gate_up[:, :, 0:FF].bitcast(F32), w["Wg"].rearrange("e d i -> d e i")).then_inc(experts_loaded, 16)
                act.dma_start(w_gate_up[:, :, FF:2 * FF].bitcast(F32), w["Wu"].rearrange("e d i -> d e i")).then_inc(experts_loaded, 16)
                for c, (at_row, n) in enumerate(FF_CHUNKS):
                    act.dma_start(w_down[0:n, :, c, :], w["Wd"][:, at_row:at_row + n, :].rearrange("e p d -> p e d")).then_inc(experts_loaded, 16)

                for r in range(6):
                    act.wait_ge(fold_pe, r + 1)
                    act.copy(ut[0:PR, r, :], bank[r][0:PR, :]).then_inc(fold_act, 1)
                act.wait_ge(fold_pe, 7)
                act.copy(ut_small[0:RANK_OUT, 0:P], bank[7][0:RANK_OUT, 0:P]).then_inc(fold_act, 1)
                act.copy(ut_small[0:RANK_MLP, P:2 * P], bank[7][0:RANK_MLP, P:2 * P]).then_inc(fold_act, 1)
                act.wait_ge(fold_pe, 8)
                act.copy(ut_fc2[:], bank[0][0:RANK_MLP, :]).then_inc(fold_act, 1)
                assert small[0] == 16 * N_SMALL
                act.wait_ge(small_loaded, 16 * N_SMALL)
                act.wait_ge(fold_pe, 9)
                for k in range(2):
                    act.copy(raw_qkv[:, k, :].rearrange("p (i e g) -> p g i e", i=LANES, e=DH),
                             bank[6][:, k * P:(k + 1) * P].rearrange("p (g i e) -> p g i e", i=LANES, e=DH)).then_inc(fold_act, 1)
                act.copy(raw_qkv[:, 2, :], bank[6][:, 2 * P:3 * P]).then_inc(fold_act, 1)
                act.mul(g_q[:], ln1_g[:], float(DH) ** -0.5).then_inc(fold_act, 1)

                def scale(c, first):
                    act.wait_ge(xn_ready, c.index + 1)
                    if not first:
                        act.wait_ge(xt_turned, c.index - 1)
                    for t in range(TPC):
                        last = act.activation(xnr[c.parity][:, t, :], xn[c.parity][:, t, :], ACT.Identity, scale=rstd2[:, ds(c.index * TPC + t, 1)])
                    last.then_inc(xnr_ready, 1)

                def copy_xt(c, first):
                    act.wait_ge(xt_turned, c.index + 1)
                    if not first:
                        act.wait_ge(xt_stored[c.parity], 16 * c.turn)
                    act.copy(xt[c.parity][:], bank[c.parity][:]).then_inc(xt_ready, 1)

                scale(at(0, 0), True)
                scale(at(0, 1), True)
                copy_xt(at(0, 0), True)
                scale(at(0, 2), False)
                copy_xt(at(0, 1), True)
                with act.Fori(1, chunks // 2 - 1) as q:
                    scale(at(q, 1), False)
                    copy_xt(at(q, 0), False)
                    scale(at(q, 2), False)
                    copy_xt(at(q, 1), False)
                q = chunks // 2 - 1
                scale(at(q, 1), False)
                copy_xt(at(q, 0), False)
                copy_xt(at(q, 1), False)
                act.wait_ge(fold_pe, 10)
                act.copy(wo[:], bank[1][:, 0:P]).then_inc(fold_act, 1)
                act.wait_ge(fold_pe, 11)
                act.copy(raw_w1[:], bank[2][:]).then_inc(fold_act, 1)
                act.wait_ge(fold_pe, 12)
                act.copy(w2[:].rearrange("p c d -> p (c d)"), bank[3][:]).then_inc(fold_act, 1)
                act.wait_ge(gap_ready, 1)
                act.activation(gap_exp[:], gap[:], ACT.Exp).then_inc(gap_exped, 1)
                act.wait_ge(fold_act, 16)
                act.activation(wq[:], raw_qkv[:, 0, :], ACT.Identity, scale=g_q[:]).then_inc(fold_act, 1)
                act.activation(wk[:], raw_qkv[:, 1, :], ACT.Identity, scale=ln1_g[:]).then_inc(fold_act, 1)
                act.activation(wv[:], raw_qkv[:, 2, :], ACT.Identity, scale=ln1_g[:]).then_inc(fold_act, 1)
                act.activation(w1[:], raw_w1[:], ACT.Identity, scale=ln2_g[:]).then_inc(fold_act, 1)
                act.wait_ge(const_ready, N_CONST)
                act.activation(b_rows[:], ones[:], ACT.Identity, scale=ln1_b[:]).then_inc(fold_act, 1)

            @block.tensor
            def _(pe):
                pe.wait_ge(const_ready, N_CONST)
                pe.wait_ge(small_loaded, 16 * N_SMALL)
                pe.wait_ge(diag_loaded, 16 * N_DIAG)
                for r in range(6):
                    for j in range(4):
                        pair = 4 * (r % 2) + j
                        last = pe.transpose(bank[r][0:PR, j * P:(j + 1) * P], u_in[r // 2][:, pair * PR:(pair + 1) * PR], ident[:])
                    last.then_inc(fold_pe, 1)
                pe.transpose(bank[7][0:RANK_OUT, 0:P], out_u[:], ident[:])
                pe.transpose(bank[7][0:RANK_MLP, P:2 * P], fc1_u[:], ident[:]).then_inc(fold_pe, 1)
                pe.wait_ge(fold_act, 1)
                for c in range(HCH):
                    last = pe.transpose(bank[0][0:RANK_MLP, c * P:(c + 1) * P], fc2_u[:, c, :], ident[:])
                last.then_inc(fold_pe, 1)
                for r in range(6):
                    pe.wait_ge(fold_act, r + 1)
                    for j in range(4):
                        pair = 4 * (r % 2) + j
                        col = (r // 2) * P + pair * 2 * DH
                        last = pe.matmul(bank[6][:, col:col + 2 * DH], ut[0:PR, r, j * P:(j + 1) * P],
                                         v_in[r // 2][:, pair, :], start=True, stop=True)
                last.then_inc(fold_pe, 1)
                pe.wait_ge(fold_act, 9)
                pe.wait_ge(router_loaded, 16)
                def turn(c, first):
                    pe.wait_ge(xnr_ready, c.index + 1)
                    if not first:
                        pe.wait_ge(xt_ready, c.index - 1)
                    for t in range(TPC):
                        last = pe.transpose(bank[c.parity][:, t * P:(t + 1) * P], xnr[c.parity][:, t, :], ident[:])
                    last.then_inc(xt_turned, 1)

                def score(c, of_four, first):
                    pe.wait_ge(xt_ready, c.index + 1)
                    if not first:
                        pe.wait_ge(logits_copied, c.index - 3)
                    for t in range(TPC):
                        last = pe.matmul(bank[2 + of_four][:, t * EXPERTS:(t + 1) * EXPERTS], xt[c.parity][:, t * P:(t + 1) * P],
                                         w_router[:], start=True, stop=True)
                    last.then_inc(logits_ready, 1)

                turn(at(0, 0), True)
                turn(at(0, 1), True)
                score(at(0, 0), 0, True)
                for i in range(3):
                    turn(at(0, i + 2), False)
                    score(at(0, i + 1), i + 1, True)
                quads = (chunks - 5) // 4
                with pe.Fori(0, quads) as quad:
                    for i in range(4):
                        turn(at(2 * quad, i + 5), False)
                        score(at(2 * quad, i + 4), i, False)
                for i in range(4 * quads + 3, chunks - 2):
                    turn(at(0, i + 2), False)
                    score(at(0, i + 1), (i + 1) % 4, False)
                score(at(0, chunks - 1), (chunks - 1) % 4, False)
                pe.wait_ge(xt_ready, chunks)
                pe.wait_ge(logits_copied, chunks)
                pe.matmul(bank[1][:, 0:P], ut_small[0:RANK_OUT, 0:P], out_v[:], start=True, stop=True).then_inc(fold_pe, 1)
                pe.matmul(bank[2][:], ut_small[0:RANK_MLP, P:2 * P], fc1_v[:], start=True, stop=True).then_inc(fold_pe, 1)
                pe.wait_ge(fold_act, 9)
                for c in range(HCH):
                    last = pe.matmul(bank[3][:, c * P:(c + 1) * P], ut_fc2[:, c * P:(c + 1) * P], fc2_v[:], start=True, stop=True)
                last.then_inc(fold_pe, 1)
                pe.wait_ge(gap_ready, 1)
                for e in range(EXPERTS):
                    last = pe.matmul(bank[7][0:tiles, e:e + 1], chosen[:, :, e], ones[:, 0:1], start=True, stop=True)
                last.then_inc(tile_counted, 1)
                pe.wait_ge(earlier_ready, 1)
                pe.matmul(bank[7][:, EXPERTS:2 * EXPERTS], ones[0:tiles, :], tile_count[:], start=True, stop=True)
                pe.wait_ge(earlier_ready, 2)
                for k in range(2):
                    part = slice(k * half, (k + 1) * half)
                    pe.matmul(bank[4 + k][:, 0:half], before[:], chosen[:].rearrange("p t e -> p (t e)")[:, part], start=True, stop=False)
                    last = pe.matmul(bank[4 + k][:, 0:half], ones[0:tiles, :], earlier[:].rearrange("k t e -> k (t e)")[:, part], start=False, stop=True)
                last.then_inc(counted, 1)
                pe.wait_ge(fold_act, 21)
                pe.matmul(bank[0][:, 0:1], raw_qkv[:, 0, :], ln1_b[:], start=True, stop=True)
                pe.matmul(bank[0][:, 1:2], raw_qkv[:, 1, :], ln1_b[:], start=True, stop=True)
                for c in range(HCH):
                    pe.matmul(bank[0][:, 2 + c:3 + c], raw_w1[:, c * P:(c + 1) * P], ln2_b[:], start=True, stop=True)
                pe.matmul(bank[0][:, P:2 * P], b_rows[:], raw_qkv[:, 2, :], start=True, stop=True).then_inc(fold_pe, 1)

            @block.vector
            def _(dve):
                n = tiles // XL
                for k in range(XL):
                    dve.wait_ge(x_loaded[k], 16)
                    with dve.Fori(k * n // 8, (k + 1) * n // 8) as c:
                        for t in range(8):
                            dve.bn_stats(stats[:].rearrange("p (c t) s -> p c t s", t=8)[:, ds(c, 1), t, :].rearrange("p o s -> p (o s)"),
                                         x_all[:].rearrange("p (c t) d -> p c t d", t=8)[:, ds(c, 1), t, :].rearrange("p o d -> p (o d)")).then_inc(stats_done, 1)
                dve.wait_ge(stats_done, tiles)
                steps = [0]

                def step(ins):
                    steps[0] += 1
                    ins.then_inc(ln_step, 1)
                    dve.wait_ge(ln_step, steps[0])

                step(dve.tensor_tensor(mean[:], stats[:, :, 1], stats[:, :, 4], ALU.add))
                step(dve.tensor_tensor(tmp[:], stats[:, :, 1], stats[:, :, 4], ALU.subtract))
                step(dve.tensor_tensor(var[:], stats[:, :, 2], stats[:, :, 5], ALU.add))
                step(dve.tensor_tensor(tmp[:], tmp[:], tmp[:], ALU.mult))
                step(dve.tensor_scalar(var[:], var[:], 1.0 / P, None, ALU.mult))
                step(dve.scalar_tensor_tensor(out=var[:], in0=tmp[:], scalar=0.25, in1=var[:], op0=ALU.mult, op1=ALU.add))
                step(dve.tensor_scalar(mean[:], mean[:], 0.5, None, ALU.mult))
                step(dve.tensor_scalar(std2[:], var[:], 1.0, None, ALU.mult))
                step(dve.tensor_scalar(var[:], var[:], LN_EPS, None, ALU.add))
                inverse_root(dve, step, var[:], rstd[:], root_bits[:], tmp[:])
                step(dve.tensor_tensor(var[:], rstd[:], rstd[:], ALU.mult))
                step(dve.tensor_tensor(var[:], var[:], std2[:], ALU.mult))
                step(dve.tensor_scalar(var[:], var[:], LN_EPS, None, ALU.add))
                inverse_root(dve, step, var[:], rstd2[:], root_bits[:], tmp[:])
                step(dve.tensor_tensor(std2[:], var[:], rstd2[:], ALU.mult))

                def normalise(c, first):
                    if not first:
                        dve.wait_ge(xn_stored[c.parity], 16 * c.turn)
                        dve.wait_ge(xnr_ready, c.index - 1)
                    for t in range(TPC):
                        col = ds(c.index * TPC + t, 1)
                        last = dve.tensor_scalar(xn[c.parity][:, t, :], x_all[:].rearrange("p t d -> p (t d)")[:, ds((c.index * TPC + t) * P, P)],
                                                 mean[:, col], rstd[:, col], ALU.subtract, ALU.mult)
                    last.then_inc(xn_ready, 1)

                def copy_logits(c, of_four):
                    dve.wait_ge(logits_ready, c.index + 1)
                    dve.tensor_tensor(logits[:].rearrange("p t e -> p (t e)")[:, ds(c.index * TPC * EXPERTS, TPC * EXPERTS)].rearrange("p (t e) -> p t e", e=EXPERTS),
                                      bank[2 + of_four][:, 0:TPC * EXPERTS].rearrange("p (t e) -> p t e", e=EXPERTS),
                                      std2[:, ds(c.index * TPC, TPC)].unsqueeze(2).to_broadcast([P, TPC, EXPERTS]), ALU.mult).then_inc(logits_copied, 1)

                normalise(at(0, 0), True)
                normalise(at(0, 1), True)
                normalise(at(0, 2), False)
                with dve.Fori(0, chunks // 4 - 1) as quad:
                    for d in range(4):
                        normalise(at(2 * quad, d + 3), False)
                        copy_logits(at(2 * quad, d), d)
                normalise(at(0, chunks - 1), False)
                for d in range(4):
                    copy_logits(at(0, chunks - 4 + d), d)
                dve.wait_ge(logits_copied, chunks)

                routed = [0]

                def link(ins):
                    routed[0] += 1
                    ins.then_inc(route, 1)
                    dve.wait_ge(route, routed[0])

                def over_experts(a):
                    return a.unsqueeze(2).to_broadcast([P, tiles, EXPERTS])

                for k, rest in enumerate((logits, left)):
                    link(dve.tensor_reduce(top[k][:], rest[:], AX.X, ALU.max))
                    link(dve.tensor_tensor(work[:], rest[:], over_experts(top[k][:]), ALU.is_equal))
                    link(dve.tensor_tensor(work[:], work[:], rev_e[:], ALU.mult))
                    link(dve.tensor_reduce(key[:], work[:], AX.X, ALU.max))
                    link(dve.tensor_tensor(pick[k][:], rev_e[:], over_experts(key[:]), ALU.is_equal))
                    if k == 0:
                        link(dve.scalar_tensor_tensor(out=left[:], in0=pick[0][:], scalar=LOWEST, in1=logits[:], op0=ALU.mult, op1=ALU.add))
                link(dve.tensor_tensor(chosen[:], pick[0][:], pick[1][:], ALU.add))
                dve.tensor_tensor(gap[:], top[1][:], top[0][:], ALU.subtract).then_inc(gap_ready, 1)
                dve.wait_ge(tile_counted, 1)
                dve.tensor_copy(tile_count[:], bank[7][0:tiles, 0:EXPERTS]).then_inc(earlier_ready, 1)
                dve.wait_ge(earlier_ready, 1)
                dve.tensor_tensor(earlier[:], tile_count[:].unsqueeze(1).to_broadcast([tiles, tiles, EXPERTS]),
                                  before[0:tiles, 0:tiles].unsqueeze(2).to_broadcast([tiles, tiles, EXPERTS]), ALU.mult).then_inc(earlier_ready, 1)
                dve.wait_ge(gap_exped, 1)
                link(dve.tensor_scalar(gap_sum[:], gap_exp[:], 1.0, None, ALU.add))
                link(dve.reciprocal(mix[:, :, 0], gap_sum[:]))
                link(dve.tensor_tensor(mix[:, :, 1], mix[:, :, 0], gap_exp[:], ALU.mult))
                link(dve.tensor_copy(tile_no[:], tile_no_i[:]))
                dve.wait_ge(counted, 1)
                link(dve.tensor_scalar(count_f[:], bank[7][:, EXPERTS:2 * EXPERTS], float(P - 1), None, ALU.add))
                link(dve.tensor_copy(count_i[:], count_f[:]))
                link(dve.tensor_scalar(count_i[:], count_i[:], 7, None, ALU.arith_shift_right))
                link(dve.tensor_copy(run_tiles[:], count_i[:]))
                e_src, e_dst, far = run_tiles, end_a, 1
                while far < EXPERTS:
                    dve.tensor_copy(e_dst[:, 0:far], e_src[:, 0:far])
                    link(dve.tensor_tensor(e_dst[:, far:], e_src[:, far:], e_src[:, 0:EXPERTS - far], ALU.add))
                    e_src, e_dst, far = e_dst, end_b if e_dst is end_a else end_a, 2 * far
                link(dve.tensor_tensor(base[:], e_src[:], run_tiles[:], ALU.subtract))
                link(dve.tensor_scalar(base[:], base[:], float(P), None, ALU.mult))
                for k in range(2):
                    part = slice(k * tiles // 2, (k + 1) * tiles // 2)
                    link(dve.tensor_tensor(work[:, part, :], bank[4 + k][:, 0:half].rearrange("p (t e) -> p t e", e=EXPERTS),
                                           base[:].unsqueeze(1).to_broadcast([P, tiles // 2, EXPERTS]), ALU.add))
                for k in range(2):
                    link(dve.tensor_tensor(pick[k][:], pick[k][:], work[:], ALU.mult))
                    link(dve.tensor_reduce(slot_f[:, :, k], pick[k][:], AX.X, ALU.add))
                dve.tensor_copy(slot_of[:], slot_f[:].rearrange("p t k -> p (t k)"))
                link(dve.tensor_tensor(past[:], tile_no[:].unsqueeze(2).to_broadcast([1, slot_tiles, EXPERTS]),
                                       e_src[0:1, :].unsqueeze(1).to_broadcast([1, slot_tiles, EXPERTS]), ALU.is_ge))
                link(dve.tensor_reduce(expert_f[:], past[:], AX.X, ALU.add))
                link(dve.tensor_scalar(expert_f[:], expert_f[:], float(EXPERTS - 1), None, ALU.min))
                link(dve.tensor_copy(tile_expert[:], expert_f[:]))
                dve.wait_ge(fold_pe, 13)
                dve.tensor_scalar(q_bias[:], bank[0][:, 0:1], q_b[:], float(DH) ** -0.5, ALU.add, ALU.mult)
                dve.tensor_tensor(k_bias[:], bank[0][:, 1:2], k_b[:], ALU.add)
                dve.tensor_tensor(mlp_bias[:], bank[0][:, 2:2 + HCH], fc1_b[:], ALU.add)
                dve.tensor_tensor(v_bias[:], bank[0][:, P:2 * P], v_b[:], ALU.add)


def attention(nc, env):
    chunks, slots = env["chunks"], env["slots"]
    ident, wq, wk, wv, wo = env["ident"], env["wq"], env["wk"], env["wv"], env["wo"]
    q_bias, k_bias, v_bias, out_bias = env["q_bias"], env["k_bias"], env["v_bias"], env["out_bias"]
    ln2_stats, slot_of, tiles = env["ln2_stats"], env["slot_of"], env["tiles"]
    w_gate_up, w_hi = env["w_gate_up"], env["w_hi"]
    UNITS = 12
    Q_STACKS, K_STACKS = PARTS * LANES, PARTS
    PT = 8

    with ExitStack() as stack:
        s = Scope(nc, stack, "att")
        ident_b = s.sb("ident_b", [P, P], BF16)
        mask_st = s.sb("mask_st", [P, SEQ])
        masked_st = s.two("masked_st", [P, CHUNK], BF16)
        mask_ts = s.sb("mask_ts", [P, LANES, P], BF16)
        xt = s.two("xt", [P, CHUNK])
        xn = s.two("xn", [P, TPC, P])
        slot_now = s.two("slot_now", [P, 2 * TPC], U32)
        row_of = s.sb("row_of", [P, tiles * 2], I32)
        row_now = s.two("row_now", [P, 2 * TPC])
        q_hi, q_lo, k_hi, k_lo = (s.sb(n, [P, CHUNK], F32R) for n in ("q_hi", "q_lo", "k_hi", "k_lo"))
        odd_stack = s.sb("odd_stack", [P, GROUPS * LANES * CHUNK], F32R)
        q_stack = [t[:].rearrange("p (g i s) -> p g i s", g=GROUPS, i=LANES) for t in (env["even_stack"], odd_stack)]
        k_stack = s.two("k_stack", [P, GROUPS, CHUNK], F32R)
        v_ones = s.two("v_ones", [P, TPC, HEADS, 32])
        row_max = s.two("row_max", [P, 2, HEADS])
        neg_max = [s.sb(f"neg_max{b}", [HEADS, SEQ], F32R) for b in range(2)]
        probs = s.sb("probs", [P, PT, CHUNK])
        ctx_t = s.sb("ctx_t", [P, GROUPS * SEQ])
        ctx_inv = s.sb("ctx_inv", [P, 2, HEADS])
        ctx = s.sb("ctx", [P, 2, P])
        ctx_turned = s.sb("ctx_turned", [P, SEQ])
        h = s.two("h", [P, SEQ])

        t_ps = [s.ps(f"t_ps{k}", [P, CHUNK]) for k in range(2)]
        m_ps = [s.ps(f"m_ps{k}", [P, CHUNK]) for k in range(2)]
        pv_ps = s.ps("pv_ps", [P, GROUPS * SEQ])
        free_ps = [s.ps(f"free_ps{k}", [P, CHUNK]) for k in range(2)]

        const_ready, cleared, ones_ready = s.sem("const_ready"), s.sem("cleared"), s.sem("ones_ready")
        v_cleared, other_cleared = s.sem("v_cleared"), s.sem("other_cleared")
        xt_loaded, xn_loaded = s.two_sems("xt_loaded"), s.two_sems("xn_loaded")
        q_done, k_done, v_done = s.sem("q_done"), s.sem("k_done"), s.sem("v_done")
        q_hi_ready, k_hi_ready = s.sem("q_hi_ready"), s.sem("k_hi_ready")
        q_split, k_split, v_ready = s.sem("q_split"), s.sem("k_split"), s.sem("v_ready")
        stack_free, q_stacked = s.sem("stack_free"), s.two_sems("q_stacked")
        k_stack_free, k_stack_started, k_stacked = s.sem("k_stack_free"), s.sem("k_stack_started"), s.two_sems("k_stacked")
        max_started = s.sem("max_started")
        max_scores, max_taken = s.sem("max_scores"), s.sem("max_taken")
        max_turned, max_copied = s.sem("max_turned"), s.sem("max_copied")
        max_stacked = s.two_sems("max_stacked")
        scores_done, exp_done = s.sem("scores_done"), s.sem("exp_done")
        pv_done, ctx_copied = s.sem("pv_done"), s.sem("ctx_copied")
        ctx_back, inv_ready, ctx_ready = s.sem("ctx_back"), s.sem("inv_ready"), s.sem("ctx_ready")
        ctx_again, ctx_turned_ready = s.sem("ctx_again"), s.sem("ctx_turned_ready")
        out_done, h_done, h_stored = s.sem("out_done"), s.sem("h_done"), s.two_sems("h_stored")
        x_out_ready, slot_ready = s.sem("x_out_ready"), s.sem("slot_ready")
        rows_ready, w_hi_ready = s.sem("rows_ready"), s.sem("w_hi_ready")
        scatter_started, scattered = s.sem("scatter_started"), s.two_sems("scattered")

        MAX_FROM = 8
        EARLY = 2 * UNITS - MAX_FROM
        MAX_SLOTS = {(MAX_FROM + m) % (2 * UNITS): [(int(m < EARLY), m)] for m in range(2 * UNITS)}
        SPLIT_SLOTS = range(2, 2 + 2 * EXPERTS, 2)
        HALVES = 2 * UNITS // 2

        def bank_of(turn, d):
            return (turn + d) % 2

        last_chunk = chunks - 1

        with nc.Block() as block:

            @block.sync
            def _(sp):
                def load_xt(c):
                    sp.dma_start(xt[c.parity][:], env["xt_dram"][ds(c.index * P, P), :]).then_inc(xt_loaded[c.parity], 16)

                def load_xn(c):
                    sp.dma_start(xn[c.parity][:], env["xn_tiles"][:, ds(c.index * TPC, TPC), :]).then_inc(xn_loaded[c.parity], 16)

                def stack_q(c):
                    sp.wait_ge(q_split, c.index + 1)
                    for part, q in enumerate((q_hi, q_hi, q_lo)):
                        for i in range(LANES):
                            to = 32 * part + DH * i
                            sp.dma_start(q_stack[c.parity][to:to + DH, :, i, :].bitcast(F32),
                                         q[32 * i:32 * i + 32, :].bitcast(F32)).then_inc(q_stacked[c.parity], 16)

                def stack_max(c, b):
                    sp.wait_ge(max_copied, 2 * c.index + b + 1)
                    sp.dma_start(q_stack[c.parity][ROWS:ROWS + 1, :, :, b * SEQ:(b + 1) * SEQ].bitcast(F32),
                                 neg_max[b][:].bitcast(F32)).then_inc(max_stacked[b], 16)

                def store_h(c, b):
                    seq = 2 * c.index + b
                    sp.wait_ge(h_done, seq + 1)
                    sp.dma_start(env["h_tiles"][:, ds(2 * seq, 2), :], h[b][:].rearrange("p (t d) -> p t d", d=P)).then_inc(h_stored[b], 16)

                def step(half, d):
                    p = at(half, d)
                    first, last = (isinstance(p.index, int) and p.index == k for k in (0, last_chunk))
                    three_ahead = not (isinstance(p.index, int) and p.index >= last_chunk - 2)
                    if not first and not last:
                        sp.wait_ge(scores_done, 2 * UNITS * p.index)
                        sp.sem_inc(stack_free, 1)
                        stack_q(at(half, d + 1))
                    if not first:
                        store_h(at(half, d - 1), 0)
                    if three_ahead:
                        sp.wait_ge(v_done, p.index + 2)
                        load_xt(at(half, d + 3))
                    stack_max(p, 1)
                    if not first:
                        store_h(at(half, d - 1), 1)
                        if not last:
                            load_xn(at(half, d + 1))
                    if not last:
                        stack_max(at(half, d + 1), 0)

                load_xt(at(0, 0))
                load_xt(at(0, 1))
                load_xn(at(0, 0))
                load_xn(at(0, 1))
                sp.wait_ge(cleared, 2)
                stack_q(at(0, 0))
                sp.wait_ge(v_done, 1)
                load_xt(at(0, 2))
                sp.wait_ge(other_cleared, 1)
                stack_q(at(0, 1))
                stack_max(at(0, 0), 0)
                step(0, 0)
                with sp.Fori(0, chunks // 2 - 2) as half:
                    step(half, 1)
                    step(half, 2)
                step(chunks // 2 - 2, 1)
                step(chunks // 2 - 1, 0)
                step(chunks // 2 - 1, 1)
                for b in range(2):
                    store_h(at(chunks // 2 - 1, 1), b)
                    sp.wait_ge(h_stored[b], 16 * (chunks + 1))

            @block.gpsimd
            def _(pool):
                pool.memset(q_stack[0][:, GROUPS // 2:].bitcast(F32), 0.0).then_inc(cleared, 1)
                pool.memset(v_ones[0][:], 1.0).then_inc(v_cleared, 1)
                pool.memset(mask_st[:], 0.0).then_inc(const_ready, 1)
                pool.memset(mask_ts[:], 0.0).then_inc(const_ready, 1)
                pool.tensor_copy(ident_b[:], ident[:]).then_inc(const_ready, 1)
                pool.wait_ge(const_ready, 2)
                pool.affine_select(out=mask_st[:], in_=mask_st[:], compare_op=ALU.is_ge, fill=MASKED, base=P,
                                   pattern=[[-1, SEQ]], channel_multiplier=1).then_inc(const_ready, 1)
                pool.affine_select(out=mask_ts[:], in_=mask_ts[:], compare_op=ALU.is_ge, fill=MASKED, base=0,
                                   pattern=[[0, LANES], [1, P]], channel_multiplier=-1).then_inc(const_ready, 1)
                pool.memset(v_ones[1][:], 1.0).then_inc(v_cleared, 1)
                pool.iota(row_of[:], pattern=[[2 * P, tiles], [1, 2]], base=0, channel_multiplier=2).then_inc(rows_ready, 1)
                def stack_k(c):
                    pool.wait_ge(k_split, c.index + 1)
                    pool.sem_inc(k_stack_started, 1)
                    for part, k in enumerate((k_hi, k_lo, k_hi)):
                        pool.dma_start(k_stack[c.parity][32 * part:32 * part + 32, :, :].bitcast(F32), k[:].bitcast(F32)).then_inc(k_stacked[c.parity], 16)

                def scatter(c, col):
                    t, k = divmod(col, 2)
                    pool.indirect_dma_start(env["slot_x"][:], bass.IndirectOffsetOnAxis(ap=slot_now[c.parity][:, col:col + 1], axis=0),
                                            xn[c.parity][:, t, :], None).then_inc(scattered[c.parity], 16)
                    pool.indirect_dma_start(env["slot_row"][:], bass.IndirectOffsetOnAxis(ap=slot_now[c.parity][:, col:col + 1], axis=0),
                                            row_now[c.parity][:, col:col + 1], None).then_inc(scattered[c.parity], 16)

                def step(half, d):
                    p = at(half, d)
                    first, last = (isinstance(p.index, int) and p.index == k for k in (0, last_chunk))
                    if not first and not last:
                        pool.wait_ge(scores_done, 2 * UNITS * p.index)
                        pool.sem_inc(k_stack_free, 1)
                        stack_k(at(half, d + 1))
                    pool.tensor_copy(slot_now[p.parity][:], slot_of[:, ds(p.index * 2 * TPC, 2 * TPC)]).then_inc(slot_ready, 1)
                    pool.tensor_copy(row_now[p.parity][:], row_of[:, ds(p.index * 2 * TPC, 2 * TPC)]).then_inc(slot_ready, 1)
                    pool.wait_ge(xn_loaded[p.parity], 16 * (p.turn + 1))
                    pool.wait_ge(slot_ready, 2 * (p.index + 1))
                    pool.sem_inc(scatter_started, 1)
                    for col in range(2 * TPC):
                        scatter(p, col)
                    pool.wait_ge(scattered[p.parity], 16 * 2 * 2 * TPC * (p.turn + 1))
                    pool.tensor_tensor(xn[p.parity][:], xn[p.parity][:], out_bias[:].unsqueeze(1).to_broadcast([P, TPC, P]), ALU.add).then_inc(x_out_ready, 1)

                stack_k(at(0, 0))
                pool.memset(q_stack[1].bitcast(F32), 0.0).then_inc(other_cleared, 1)
                stack_k(at(0, 1))
                pool.wait_ge(rows_ready, 1)
                step(0, 0)
                with pool.Fori(0, chunks // 2 - 2) as half:
                    step(half, 1)
                    step(half, 2)
                step(chunks // 2 - 2, 1)
                step(chunks // 2 - 1, 0)
                step(chunks // 2 - 1, 1)

            @block.tensor
            def _(pe):
                def project_q(c, bank, free, n):
                    pe.wait_ge(xt_loaded[c.parity], 16 * (c.turn + 1))
                    pe.wait_ge(free, n) if n is not None else None
                    pe.matmul(free_ps[bank][:], wq[:], xt[c.parity][:], start=True, stop=True).then_inc(q_done, 1)

                def project_k(c, bank, free, n):
                    pe.wait_ge(free, n) if n is not None else None
                    pe.matmul(free_ps[bank][:], wk[:], xt[c.parity][:], start=True, stop=True).then_inc(k_done, 1)

                def project_v(c, bank, free, n):
                    pe.wait_ge(free, n)
                    for t in range(TPC):
                        last = pe.matmul(free_ps[bank][:, t * P:(t + 1) * P], xt[c.parity][:, t * P:(t + 1) * P], wv[:], start=True, stop=True)
                    last.then_inc(v_done, 1)

                def max_unit(c, m):
                    b, u = divmod(m, UNITS)
                    wide, i = divmod(u, LANES)
                    ps, q, k = m_ps[m % 2], q_stack[c.parity], k_stack[c.parity]
                    lo, hi = b * SEQ, b * SEQ + P
                    if m == 0:
                        pe.wait_ge(q_stacked[c.parity], 16 * Q_STACKS * (c.turn + 1))
                        pe.wait_ge(k_stacked[c.parity], 16 * K_STACKS * (c.turn + 1))
                    if not (isinstance(c.index, int) and c.index == 0 and m < 2):
                        pe.wait_ge(max_taken, 2 * UNITS * c.index + m - 1)
                    if wide < 2:
                        for n in range(2):
                            g = 2 * wide + n
                            last = pe.matmul(ps[:, n * SEQ:(n + 1) * SEQ], q[0:ROWS, g, i, hi:hi + P], k[0:ROWS, g, lo:lo + SEQ], start=True, stop=True)
                    else:
                        for g in range(GROUPS):
                            last = pe.matmul(ps[:, g * P:(g + 1) * P], q[0:ROWS, g, i, lo:lo + P], k[0:ROWS, g, lo:lo + P], start=True, stop=True)
                    last.then_inc(max_scores, 1)

                def score_unit(c, m):
                    b, u = divmod(m, UNITS)
                    rows = slice(0, ROWS + 1)
                    ps, q, k = t_ps[m % 2], q_stack[c.parity], k_stack[c.parity]
                    lo, hi, end = b * SEQ, b * SEQ + P, (b + 1) * SEQ
                    if u == 0:
                        pe.wait_ge(max_stacked[b], 16 * (c.index + 1))
                    if not (isinstance(c.index, int) and c.index == 0 and m < 2):
                        pe.wait_ge(exp_done, 2 * UNITS * c.index + m - 1)
                    if u < 8:
                        g, pair = divmod(u, 2)
                        keys, queries, lanes = k[rows, g, lo:hi], slice(lo, end), slice(2 * pair, 2 * pair + 2)
                    else:
                        g = u - 8
                        keys, queries, lanes = k[rows, g, hi:end], slice(hi, end), slice(0, LANES)
                    by_lane = ps[:].rearrange("p (i s) -> p i s", s=queries.stop - queries.start)
                    pe.matmul(by_lane, keys, q[rows, g, lanes, queries], start=True, stop=False, skip_group_check=True)
                    pe.matmul(by_lane[:, :, 0:P], ident_b[:], mask_ts[:, lanes, :], start=False, stop=True, skip_group_check=True).then_inc(scores_done, 1)

                def probs_times_v(c, n):
                    b, u = divmod(n, HALVES // 2)
                    pe.wait_ge(exp_done, 2 * UNITS * c.index + 2 * (n + 1))
                    if n == 0:
                        pe.wait_ge(v_ready, c.index + 1)
                    if u in (0, 2) and not (isinstance(c.index, int) and c.index == 0 and b == 0):
                        pe.wait_ge(ctx_copied, 2 * (2 * c.index + b) - 1 + u // 2)
                    for i in range(LANES):
                        if u < GROUPS:
                            g = u
                            pt = probs[:, (2 * n + i // 2) % PT, i % 2 * SEQ:(i % 2 + 1) * SEQ]
                            last = pe.matmul(pv_ps[32 * i:32 * i + 32, g * SEQ:(g + 1) * SEQ], v_ones[c.parity][:, 2 * b, g * LANES + i, :],
                                             pt, start=(g % 2 == 0), stop=False, skip_group_check=True)
                    for j in range(0 if u < GROUPS else 2):
                        g = 2 * (u - GROUPS) + j
                        for i in range(LANES):
                            pt = probs[:, (2 * n + j) % PT, i * P:(i + 1) * P]
                            last = pe.matmul(pv_ps[32 * i:32 * i + 32, g * SEQ + P:(g + 1) * SEQ], v_ones[c.parity][:, 2 * b + 1, g * LANES + i, :],
                                             pt, start=False, stop=(j == 1), skip_group_check=True)
                    last.then_inc(pv_done, 1)

                def turn_max(c, b, bank, free, n):
                    pe.wait_ge(max_taken, UNITS * (2 * c.index + b + 1))
                    pe.wait_ge(free, n)
                    for t in range(2):
                        last = pe.transpose(free_ps[bank][0:HEADS, t * P:(t + 1) * P], row_max[b][:, t, :], ident[:])
                    last.then_inc(max_turned, 1)

                def context_back(seq, t, bank, free, n):
                    pe.wait_ge(ctx_copied, 2 * seq + 2)
                    pe.wait_ge(free, n)
                    for g in range(GROUPS):
                        last = pe.transpose(free_ps[bank][:, g * P:(g + 1) * P], ctx_t[:, g * SEQ + t * P:g * SEQ + (t + 1) * P], ident[:])
                    last.then_inc(ctx_back, 1)

                def context_again(seq, bank, free, n):
                    pe.wait_ge(ctx_ready, 2 * seq + 2)
                    pe.wait_ge(free, n)
                    for t in range(2):
                        last = pe.transpose(free_ps[bank][:, t * P:(t + 1) * P], ctx[:, t, :], ident[:])
                    last.then_inc(ctx_again, 1)

                def project_out(seq, bank, free, n):
                    pe.wait_ge(ctx_turned_ready, seq + 1)
                    pe.wait_ge(free, n)
                    for t in range(2):
                        last = pe.matmul(free_ps[bank][:, t * P:(t + 1) * P], ctx_turned[:, t * P:(t + 1) * P], wo[:], start=True, stop=True)
                    last.then_inc(out_done, 1)

                def step(half, d):
                    p, nxt, far = at(half, d), at(half, d + 1), at(half, d + 2)
                    x = p.index
                    first, last = (isinstance(x, int) and x == k for k in (0, last_chunk))
                    two_left = isinstance(x, int) and x >= last_chunk - 1
                    before, here = 2 * x - 1, 2 * x
                    for slot in range(2 * UNITS):
                        score_unit(p, slot)
                        if slot % 2 == 1 and slot >= 3:
                            probs_times_v(p, (slot - 3) // 2)
                        if slot == 1 and not first:
                            probs_times_v(at(half, d - 1), HALVES - 1)
                        if slot == 2 and not last:
                            project_v(nxt, bank_of(0, d), max_copied, 2 * x + 1)
                        if slot == 4 and not first:
                            context_back(before, 0, bank_of(1, d), h_done, before)
                        if slot == 6 and not first:
                            if last:
                                context_back(before, 1, bank_of(2, d), max_copied, 2 * x + 1)
                            else:
                                context_back(before, 1, bank_of(2, d), v_ready, x + 2)
                        if slot == 8 and not first:
                            context_again(before, bank_of(3, d), ctx_ready, 2 * before + 1)
                        if slot == 9:
                            if first:
                                turn_max(p, 1, bank_of(4, d), v_ready, 2)
                            else:
                                turn_max(p, 1, bank_of(4, d), ctx_ready, 2 * before + 2)
                        if slot == 10 and not first:
                            project_out(before, bank_of(5, d), ctx_turned_ready, before + 1)
                        if slot == 12 and not two_left:
                            project_q(far, bank_of(6, d), max_copied, 2 * x + 2)
                        if slot == 14 and not two_left:
                            if first:
                                project_k(far, bank_of(7, d), k_split, 2)
                            else:
                                project_k(far, bank_of(7, d), h_done, 2 * x)
                        if slot == 16:
                            if two_left:
                                context_back(here, 0, bank_of(8, d), max_copied, 2 * x + 2)
                            else:
                                context_back(here, 0, bank_of(8, d), q_split, x + 3)
                        if slot == 18:
                            if two_left:
                                context_back(here, 1, bank_of(9, d), h_done, 2 * x)
                            else:
                                context_back(here, 1, bank_of(9, d), k_split, x + 3)
                        if slot == 20:
                            context_again(here, bank_of(10, d), ctx_ready, 2 * here + 1)
                        if slot == 21 and not last:
                            turn_max(nxt, 0, bank_of(11, d), ctx_ready, 2 * here + 2)
                        if slot == 22:
                            project_out(here, bank_of(12, d), ctx_turned_ready, here + 1)
                        for ahead, m in MAX_SLOTS.get(slot, ()):
                            if not (ahead and last):
                                max_unit(at(half, d + ahead), m)

                project_q(at(0, 0), 1, None, None)
                project_k(at(0, 0), 0, None, None)
                project_v(at(0, 0), 1, q_split, 1)
                project_q(at(0, 1), 0, k_split, 1)
                project_k(at(0, 1), 1, v_ready, 1)
                pe.wait_ge(const_ready, 5)
                for m in range(EARLY):
                    max_unit(at(0, 0), m)
                    if m == UNITS:
                        turn_max(at(0, 0), 0, 0, q_split, 2)
                pe.wait_ge(ones_ready, 2)
                step(0, 0)
                with pe.Fori(0, chunks // 2 - 2) as half:
                    step(half, 1)
                    step(half, 2)
                step(chunks // 2 - 2, 1)
                step(chunks // 2 - 1, 0)
                step(chunks // 2 - 1, 1)
                probs_times_v(at(chunks // 2 - 1, 1), HALVES - 1)
                end = 2 * chunks - 1
                context_back(end, 0, bank_of(1, 2), h_done, end)
                context_back(end, 1, bank_of(2, 2), ctx_ready, 2 * end)
                context_again(end, bank_of(3, 2), ctx_ready, 2 * end + 1)
                project_out(end, bank_of(5, 2), ctx_turned_ready, end + 1)

            @block.scalar
            def _(act):
                def high_q(c, bank):
                    act.wait_ge(q_done, c.index + 1)
                    if not (isinstance(c.index, int) and c.index == 0):
                        prev = (1 - c.parity, c.turn if c.parity else c.turn - 1)
                        act.wait_ge(q_stacked[prev[0]], 16 * Q_STACKS * (prev[1] + 1))
                    act.activation(q_hi[:], free_ps[bank][:], ACT.Identity, bias=q_bias[:]).then_inc(q_hi_ready, 1)

                def high_k(c, bank):
                    act.wait_ge(k_done, c.index + 1)
                    if not (isinstance(c.index, int) and c.index == 0):
                        prev = (1 - c.parity, c.turn if c.parity else c.turn - 1)
                        act.wait_ge(k_stacked[prev[0]], 16 * K_STACKS * (prev[1] + 1))
                    act.activation(k_hi[:], free_ps[bank][:], ACT.Identity, bias=k_bias[:]).then_inc(k_hi_ready, 1)

                def copy_max(c, b, bank):
                    act.wait_ge(max_turned, 2 * c.index + b + 1)
                    if not (isinstance(c.index, int) and c.index == 0):
                        act.wait_ge(max_stacked[b], 16 * c.index)
                    act.mul(neg_max[b][:], free_ps[bank][0:HEADS, 0:SEQ], -1.0).then_inc(max_copied, 1)

                def exp_unit(c, m):
                    act.wait_ge(scores_done, 2 * UNITS * c.index + m + 1)
                    if m % 2 == 0 and not (isinstance(c.index, int) and c.index == 0 and m < PT):
                        act.wait_ge(pv_done, HALVES * c.index + (m - PT) // 2 + 1)
                    act.activation(probs[:, m % PT, :], t_ps[m % 2][:], ACT.Exp).then_inc(exp_done, 1)

                def copy_context(seq, k):
                    act.wait_ge(pv_done, HALVES // 2 * seq + GROUPS + 1 + k)
                    if k == 0 and not (isinstance(seq, int) and seq == 0):
                        act.wait_ge(ctx_back, 2 * seq)
                    act.copy(ctx_t[:, k * CHUNK:(k + 1) * CHUNK], pv_ps[:, k * CHUNK:(k + 1) * CHUNK]).then_inc(ctx_copied, 1)

                def copy_turned(seq, bank):
                    act.wait_ge(ctx_again, seq + 1)
                    if not (isinstance(seq, int) and seq == 0):
                        act.wait_ge(out_done, seq)
                    act.copy(ctx_turned[:], free_ps[bank][:, 0:SEQ]).then_inc(ctx_turned_ready, 1)

                def step(half, d):
                    p, far = at(half, d), at(half, d + 2)
                    x = p.index
                    first = isinstance(x, int) and x == 0
                    two_left = isinstance(x, int) and x >= last_chunk - 1
                    for slot in range(2 * UNITS):
                        exp_unit(p, slot)
                        if isinstance(x, int) and x == last_chunk and slot in SPLIT_SLOTS:
                            e = SPLIT_SLOTS.index(slot)
                            act.copy(w_hi[:, e, :], w_gate_up[:, e, :].bitcast(F32)).then_inc(w_hi_ready, 1)
                        if slot == 1 and not first:
                            copy_context(2 * x - 1, 1)
                        if slot == 8 and not first:
                            copy_turned(2 * x - 1, bank_of(3, d))
                        if slot == 9:
                            copy_max(p, 1, bank_of(4, d))
                        if slot == 11:
                            copy_context(2 * x, 0)
                        if slot == 12 and not two_left:
                            high_q(far, bank_of(6, d))
                        if slot == 13:
                            copy_context(2 * x, 1)
                        if slot == 14 and not two_left:
                            high_k(far, bank_of(7, d))
                        if slot == 20:
                            copy_turned(2 * x, bank_of(10, d))
                        if slot == 21 and not (isinstance(x, int) and x == last_chunk):
                            copy_max(at(half, d + 1), 0, bank_of(11, d))
                        if slot == 23:
                            copy_context(2 * x + 1, 0)

                high_q(at(0, 0), 1)
                high_k(at(0, 0), 0)
                high_q(at(0, 1), 0)
                high_k(at(0, 1), 1)
                for k in range(2):
                    act.activation(k_stack[k][ROWS:ROWS + 1, :, :].rearrange("o g (r s) -> o (g r) s", s=P),
                                   ident[ROWS:ROWS + 1, :].unsqueeze(1).to_broadcast([1, GROUPS * CHUNK // P, P]),
                                   ACT.Identity, scale=0.0, bias=1.0).then_inc(ones_ready, 1)
                copy_max(at(0, 0), 0, 0)
                step(0, 0)
                with act.Fori(0, chunks // 2 - 2) as half:
                    step(half, 1)
                    step(half, 2)
                step(chunks // 2 - 2, 1)
                step(chunks // 2 - 1, 0)
                step(chunks // 2 - 1, 1)
                copy_context(2 * chunks - 1, 1)
                copy_turned(2 * chunks - 1, bank_of(3, 2))

            @block.vector
            def _(dve):
                def low_q(c, bank):
                    dve.wait_ge(q_hi_ready, c.index + 1)
                    dve.scalar_tensor_tensor(out=q_lo[:], in0=free_ps[bank][:], scalar=q_bias[:], in1=q_hi[:].bitcast(F32),
                                             op0=ALU.add, op1=ALU.subtract).then_inc(q_split, 1)

                def low_k(c, bank):
                    dve.wait_ge(k_hi_ready, c.index + 1)
                    dve.scalar_tensor_tensor(out=k_lo[:], in0=free_ps[bank][:], scalar=k_bias[:], in1=k_hi[:].bitcast(F32),
                                             op0=ALU.add, op1=ALU.subtract).then_inc(k_split, 1)

                def copy_v(c, bank):
                    dve.wait_ge(v_done, c.index + 1)
                    dve.tensor_tensor(v_ones[c.parity][:, :, :, 0:DH], free_ps[bank][:].rearrange("p (t h e) -> p t h e", t=TPC, e=DH),
                                      v_bias[:].rearrange("p (h e) -> p h e", e=DH).unsqueeze(1).to_broadcast([P, TPC, HEADS, DH]), ALU.add).then_inc(v_ready, 1)

                def take_max(c, m):
                    b, u = divmod(m, UNITS)
                    wide, i = divmod(u, LANES)
                    dve.wait_ge(max_scores, 2 * UNITS * c.index + m + 1)
                    if u == 0 and not (isinstance(c.index, int) and c.index == 0):
                        dve.wait_ge(max_turned, 2 * c.index + b - 1)
                    dve.sem_inc(max_started, 1)
                    n, t, g, width = (2, 1, 2 * wide, SEQ) if wide < 2 else (GROUPS, 0, 0, P)
                    for k in range(n):
                        part, head = slice(k * width, (k + 1) * width), (g + k) * LANES + i
                        last = dve.tensor_tensor_reduce(out=masked_st[m % 2][:, part], in0=m_ps[m % 2][:, part], in1=mask_st[:, SEQ - width:],
                                                        scale=1.0, scalar=LOWEST, op0=ALU.add, op1=ALU.max,
                                                        accum_out=row_max[b][:, t, head:head + 1])
                    last.then_inc(max_taken, 1)

                def normalise(seq, t, bank):
                    n = 2 * seq + t
                    dve.wait_ge(ctx_back, n + 1)
                    if t == 0 and not (isinstance(seq, int) and seq == 0):
                        dve.wait_ge(ctx_again, seq)
                    rows = free_ps[bank][:].rearrange("p (h c) -> p h c", c=32)
                    dve.reciprocal(ctx_inv[:, t, :], rows[:, :, DH]).then_inc(inv_ready, 1)
                    dve.wait_ge(inv_ready, n + 1)
                    dve.tensor_tensor(ctx[:, t, :].rearrange("p (h e) -> p h e", e=DH), rows[:, :, 0:DH],
                                      ctx_inv[:, t, :].unsqueeze(2).to_broadcast([P, HEADS, DH]), ALU.mult).then_inc(ctx_ready, 1)

                def add_residual(seq, c, b, bank):
                    dve.wait_ge(out_done, seq + 1)
                    dve.wait_ge(x_out_ready, c.index + 1)
                    dve.wait_ge(h_stored[b], 16 * (c.index + 1))
                    dve.tensor_tensor(h[b][:], free_ps[bank][:, 0:SEQ], xn[c.parity][:, 2 * b:2 * b + 2, :].rearrange("p t d -> p (t d)"), ALU.add).then_inc(h_done, 1)
                    dve.wait_ge(h_done, seq + 1)
                    for t in range(2):
                        dve.bn_stats(ln2_stats[:, ds((seq * 2 + t) * 6, 6)], h[b][:, t * P:(t + 1) * P])

                def step(half, d):
                    p, prev, nxt, far = at(half, d), at(half, d - 1), at(half, d + 1), at(half, d + 2)
                    x = p.index
                    first, last = (isinstance(x, int) and x == k for k in (0, last_chunk))
                    two_left = isinstance(x, int) and x >= last_chunk - 1
                    for slot in range(2 * UNITS):
                        if slot == 2 and not last:
                            copy_v(nxt, bank_of(0, d))
                        if slot == 4 and not first:
                            normalise(2 * x - 1, 0, bank_of(1, d))
                        if slot == 6 and not first:
                            normalise(2 * x - 1, 1, bank_of(2, d))
                        if slot == 10 and not first:
                            add_residual(2 * x - 1, prev, 1, bank_of(5, d))
                        if slot == 13 and not two_left:
                            low_q(far, bank_of(6, d))
                        if slot == 15 and not two_left:
                            low_k(far, bank_of(7, d))
                        if slot == 16:
                            normalise(2 * x, 0, bank_of(8, d))
                        if slot == 18:
                            normalise(2 * x, 1, bank_of(9, d))
                        if slot == 22:
                            add_residual(2 * x, p, 0, bank_of(12, d))
                        if last and slot - 1 in SPLIT_SLOTS:
                            e = SPLIT_SLOTS.index(slot - 1)
                            dve.wait_ge(w_hi_ready, e + 1)
                            dve.tensor_tensor(w_gate_up[:, e, :], w_gate_up[:, e, :].bitcast(F32), w_hi[:, e, :].bitcast(F32), ALU.subtract)
                        for ahead, m in MAX_SLOTS.get(slot, ()):
                            if not (ahead and last):
                                take_max(at(half, d + ahead), m)

                for b in range(2):
                    dve.sem_inc(h_stored[b], 16)
                dve.memset(q_stack[0][:, 0:GROUPS // 2].bitcast(F32), 0.0).then_inc(cleared, 1)
                low_q(at(0, 0), 1)
                low_k(at(0, 0), 0)
                dve.wait_ge(v_cleared, 2)
                copy_v(at(0, 0), 1)
                low_q(at(0, 1), 0)
                low_k(at(0, 1), 1)
                for m in range(EARLY):
                    take_max(at(0, 0), m)

                step(0, 0)
                with dve.Fori(0, chunks // 2 - 2) as half:
                    step(half, 1)
                    step(half, 2)
                step(chunks // 2 - 2, 1)
                step(chunks // 2 - 1, 0)
                step(chunks // 2 - 1, 1)
                normalise(2 * chunks - 1, 0, bank_of(1, 2))
                normalise(2 * chunks - 1, 1, bank_of(2, 2))
                add_residual(2 * chunks - 1, at(chunks // 2 - 1, 1), 1, bank_of(5, 2))


def experts(nc, env):
    slot_tiles = env["slot_tiles"]
    ident, w_hi, w_lo, w_down, tile_expert = env["ident"], env["w_hi"], env["w_gate_up"], env["w_down"], env["tile_expert"]
    down_cols = w_down[:].rearrange("p e c d -> p (e c d)")
    NCH = len(FF_CHUNKS)
    STEPS = 8

    with ExitStack() as stack:
        s = Scope(nc, stack, "moe")
        x = s.two("x", [P, P])
        hi_cols, lo_cols = w_hi.rearrange("p e f -> p (e f)"), w_lo[:].rearrange("p e f -> p (e f)")
        x_hi, x_lo = s.two("x_hi", [P, P], F32R), s.two("x_lo", [P, P], F32R)
        gate = s.two("gate", [P, FF])
        hidden = s.two("hidden", [P, FF])
        hidden_t = s.two("hidden_t", [P, NCH * P])
        y = s.two("y", [P, P])
        row_tiles = [s.sb(f"row_tiles{k}", [n, P]) for k, n in enumerate((P, slot_tiles - P))]
        row_of = s.sb("row_of", [P, slot_tiles], U32)
        row_now = s.two("row_now", [P, 1], U32)
        x_ps = [s.ps(f"x_ps{k}", [P, 512]) for k in range(2)]
        gate_ps = [s.ps(f"gate_ps{k}", [P, 512]) for k in range(2)]
        up_ps = [s.ps(f"up_ps{k}", [P, 512]) for k in range(2)]
        hidden_ps, y_ps = s.ps("hidden_ps", [P, 512]), s.ps("y_ps", [P, 512])

        x_loaded, y_stored = s.two_sems("x_loaded"), s.two_sems("y_stored")
        rows_loaded, rows_turned, rows_ready = s.sem("rows_loaded"), s.sem("rows_turned"), s.sem("rows_ready")
        row_ready, scatter_started = s.sem("row_ready"), s.sem("scatter_started")
        x_turned, x_hi_ready, x_split = s.sem("x_turned"), s.sem("x_hi_ready"), s.sem("x_split")
        gate_up_done = s.sem("gate_up_done")
        gate_done, hidden_done, hidden_turned = s.sem("gate_done"), s.sem("hidden_done"), s.sem("hidden_turned")
        hidden_copied, down_done, y_copied = s.sem("hidden_copied"), s.sem("down_done"), s.sem("y_copied")

        def run(eng, first_step, step, prelude=lambda half: None):
            first_step()
            for d in range(1, STEPS + 1):
                step(0, d, 3)
            end = (slot_tiles - 3) // STEPS
            with eng.Fori(1, end) as turn:
                prelude(STEPS // 2 * turn)
                for d in range(1, STEPS + 1):
                    step(STEPS // 2 * turn, d, 3)
            prelude(STEPS // 2 * end)
            for d in range(1, slot_tiles - STEPS * end):
                step(STEPS // 2 * end, d, min(3, slot_tiles - STEPS * end - d))

        with nc.Block() as block:

            @block.sync
            def _(sp):
                def load(c, early=False):
                    if not early:
                        sp.wait_ge(x_turned, c.index - 1)
                    sp.dma_start(x[c.parity][:], env["slot_x"][ds(c.index * P, P), :]).then_inc(x_loaded[c.parity], 16)

                load(at(0, 0), True)
                load(at(0, 1), True)
                for k in range(2):
                    n = row_tiles[k].shape[0]
                    sp.dma_start(row_tiles[k][:], env["slot_row"][k * P * P:(k * P + n) * P, :].rearrange("(n s) o -> n (s o)", s=P)).then_inc(rows_loaded, 16)
                with sp.Fori(1, slot_tiles // 2) as half:
                    load(at(half, 0))
                    load(at(half, 1))

            @block.gpsimd
            def _(pool):
                def scatter(c, early=False):
                    if not early:
                        pool.wait_ge(y_stored[c.parity], 16 * c.turn)
                    pool.tensor_copy(row_now[c.parity][:], row_of[:, ds(c.index, 1)]).then_inc(row_ready, 1)
                    pool.wait_ge(y_copied, c.index + 1)
                    pool.wait_ge(row_ready, c.index + 1)
                    pool.sem_inc(scatter_started, 1)
                    pool.indirect_dma_start(env["y_dram"][:], bass.IndirectOffsetOnAxis(ap=row_now[c.parity][:], axis=0),
                                            y[c.parity][:], None).then_inc(y_stored[c.parity], 16)

                pool.wait_ge(rows_ready, 1)
                scatter(at(0, 0), True)
                scatter(at(0, 1), True)
                with pool.Fori(1, slot_tiles // 2) as half:
                    scatter(at(half, 0))
                    scatter(at(half, 1))
                for k in range(2):
                    pool.wait_ge(y_stored[k], 16 * (slot_tiles // 2))

            @block.tensor
            def _(pe):
                def turn_x(c, early=False):
                    pe.wait_ge(x_loaded[c.parity], 16 * (c.turn + 1))
                    if not early:
                        pe.wait_ge(x_split, c.index - 1)
                    pe.transpose(x_ps[c.parity][:, 0:P], x[c.parity][:], ident[:]).then_inc(x_turned, 1)

                numbers = []

                def load_numbers(half):
                    n = min(STEPS + 2, slot_tiles - 2 * half) if isinstance(half, int) else STEPS + 2
                    numbers[:] = nc.values_load_multi_w_load_instructions(tile_expert[0:1, ds(2 * half, n)], engines=(mybir.EngineType.PE,),
                                                                          min_val=0, max_val=EXPERTS - 1,
                                                                          skip_runtime_bounds_check_because="stage 1 clamps them")[1]

                def gate_up(c, e, early=False):
                    pe.wait_ge(x_split, c.index + 1)
                    if not early:
                        pe.wait_ge(hidden_done, c.index - 1)
                    for x_part, w_parts in ((x_lo, (hi_cols,)), (x_hi, (lo_cols, hi_cols))):
                        for at_col, ps in ((0, gate_ps), (FF, up_ps)):
                            for w_part in w_parts:
                                last = pe.matmul(ps[c.parity][:, 0:FF], x_part[c.parity][:], w_part[:, ds(e * (2 * FF) + at_col, FF)],
                                                 start=x_part is x_lo, stop=w_part is w_parts[-1] and x_part is x_hi)
                    last.then_inc(gate_up_done, 1)

                def turn_hidden(c, early=False):
                    pe.wait_ge(hidden_done, c.index + 1)
                    if not early:
                        pe.wait_ge(hidden_copied, c.index)
                    for k, (col, n) in enumerate(FF_CHUNKS):
                        last = pe.transpose(hidden_ps[0:n, k * P:(k + 1) * P], hidden[c.parity][:, col:col + n], ident[:])
                    last.then_inc(hidden_turned, 1)

                def down(c, e, early=False):
                    pe.wait_ge(hidden_copied, c.index + 1)
                    if early:
                        pe.wait_ge(rows_ready, 1)
                    if not early:
                        pe.wait_ge(y_copied, c.index)
                    for k, (col, n) in enumerate(FF_CHUNKS):
                        last = pe.matmul(y_ps[:, 0:P], hidden_t[c.parity][0:n, k * P:(k + 1) * P],
                                         down_cols[0:n, ds(e * (NCH * P) + k * P, P)], start=(k == 0), stop=(k == NCH - 1))
                    last.then_inc(down_done, 1)

                def first_step():
                    load_numbers(0)
                    turn_x(at(0, 0), True)
                    turn_x(at(0, 1), True)
                    gate_up(at(0, 0), numbers[0], True)
                    turn_x(at(0, 2))
                    gate_up(at(0, 1), numbers[1], True)
                    turn_hidden(at(0, 0), True)
                    pe.wait_ge(rows_loaded, 32)
                    for k, n in enumerate((P, slot_tiles - P)):
                        last = pe.transpose(y_ps[:, k * P:k * P + n], row_tiles[k][:], ident[0:n, 0:n])
                    last.then_inc(rows_turned, 1)

                def step(half, d, left):
                    if left > 2:
                        turn_x(at(half, d + 2))
                    if left > 1:
                        gate_up(at(half, d + 1), numbers[d + 1])
                    turn_hidden(at(half, d))
                    c = at(half, d - 1)
                    down(c, numbers[d - 1], isinstance(c.index, int) and c.index == 0)

                run(pe, first_step, step, load_numbers)
                down(at(slot_tiles // 2, -1), numbers[(slot_tiles - 1) % STEPS])

            @block.scalar
            def _(act):
                def high_x(c, early=False):
                    act.wait_ge(x_turned, c.index + 1)
                    if not early:
                        act.wait_ge(gate_up_done, c.index - 1)
                    act.copy(x_hi[c.parity][:], x_ps[c.parity][:, 0:P]).then_inc(x_hi_ready, 1)

                def silu(c, early=False):
                    act.wait_ge(gate_up_done, c.index + 1)
                    if not early:
                        act.wait_ge(hidden_done, c.index - 1)
                    act.activation(gate[c.parity][:], gate_ps[c.parity][:, 0:FF], ACT.Silu).then_inc(gate_done, 1)

                def copy_hidden(c, early=False):
                    act.wait_ge(hidden_turned, c.index + 1)
                    if not early and not (isinstance(c.index, int) and c.index == 1):
                        act.wait_ge(down_done, c.index - 1)
                    whole = FF_CHUNKS[-1][0]
                    rest = FF_CHUNKS[-1][1]
                    act.copy(hidden_t[c.parity][:, 0:whole], hidden_ps[:, 0:whole])
                    act.copy(hidden_t[c.parity][0:rest, whole:whole + P], hidden_ps[0:rest, whole:whole + P]).then_inc(hidden_copied, 1)

                def first_step():
                    high_x(at(0, 0), True)
                    high_x(at(0, 1), True)
                    silu(at(0, 0), True)
                    high_x(at(0, 2))
                    silu(at(0, 1), True)
                    copy_hidden(at(0, 0), True)

                def step(half, d, left):
                    if left > 2:
                        high_x(at(half, d + 2))
                    if left > 1:
                        silu(at(half, d + 1))
                    copy_hidden(at(half, d))

                run(act, first_step, step)

            @block.vector
            def _(dve):
                def low_x(c, early=False):
                    dve.wait_ge(x_hi_ready, c.index + 1)
                    if not early:
                        dve.wait_ge(gate_up_done, c.index - 1)
                    dve.tensor_tensor(x_lo[c.parity][:], x_ps[c.parity][:, 0:P], x_hi[c.parity][:].bitcast(F32), ALU.subtract).then_inc(x_split, 1)

                def gated(c, early=False):
                    dve.wait_ge(gate_done, c.index + 1)
                    if not early:
                        dve.wait_ge(hidden_turned, c.index - 1)
                    dve.tensor_tensor(hidden[c.parity][:], gate[c.parity][:], up_ps[c.parity][:, 0:FF], ALU.mult).then_inc(hidden_done, 1)

                def copy_y(c):
                    dve.wait_ge(down_done, c.index + 1)
                    if not (isinstance(c.turn, int) and c.turn == 0):
                        dve.wait_ge(y_stored[c.parity], 16 * c.turn)
                    dve.tensor_copy(y[c.parity][:], y_ps[:, 0:P]).then_inc(y_copied, 1)

                def first_step():
                    low_x(at(0, 0), True)
                    low_x(at(0, 1), True)
                    gated(at(0, 0), True)
                    low_x(at(0, 2))
                    gated(at(0, 1), True)
                    dve.wait_ge(rows_turned, 1)
                    dve.tensor_copy(row_of[:], y_ps[:, 0:slot_tiles]).then_inc(rows_ready, 1)

                def step(half, d, left):
                    if left > 2:
                        low_x(at(half, d + 2))
                    if left > 1:
                        gated(at(half, d + 1))
                    copy_y(at(half, d - 1))

                run(dve, first_step, step)
                copy_y(at(slot_tiles // 2, -1))


def mlp_and_combine(nc, env):
    chunks, tiles = env["chunks"], env["tiles"]
    ident, w1, w2, mlp_bias, fc2_bias = env["ident"], env["w1"], env["w2"], env["mlp_bias"], env["fc2_bias"]
    mix, ln2_stats = env["mix"], env["ln2_stats"]
    mix_cols = mix[:].rearrange("p t k -> p (t k)")

    with ExitStack() as stack:
        s = Scope(nc, stack, "mlp")
        mean, var, tmp, rstd = (s.sb(n, [P, tiles]) for n in ("mean", "var", "tmp", "rstd"))
        root_bits = s.sb("root_bits", [P, tiles], I32)
        hn = s.two("hn", [P, TPC, P])
        hn_hi, hn_lo = s.two("hn_hi", [P, CHUNK], F32R), s.two("hn_lo", [P, CHUNK], F32R)
        w1_hi, w1_lo = (s.sb(n, [P, HID], F32R) for n in ("w1_hi", "w1_lo"))
        mid = s.two("mid", [P, HCH, CHUNK])
        h = s.two("h", [P, TPC, P])
        x = s.two("x", [P, TPC, P])
        h_again = s.two("h_again", [P, TPC, P])
        total = s.two("total", [P, TPC, P])
        AHEAD = 4
        rows = [s.sb(f"rows{k}", [P, 2 * TPC, P]) for k in range(AHEAD)]
        t_ps = [s.ps(f"t_ps{k}", [P, CHUNK]) for k in range(2)]
        f_ps = [s.ps(f"f_ps{k}", [P, CHUNK]) for k in range(HCH)]
        o_ps = [s.ps(f"o_ps{k}", [P, CHUNK]) for k in range(2)]

        ln_step = s.sem("ln_step")
        w1_hi_ready, w1_split = s.sem("w1_hi_ready"), s.sem("w1_split")
        hn_ready, hn_turned = s.sem("hn_ready"), s.sem("hn_turned")
        hn_hi_ready, hn_split = s.sem("hn_hi_ready"), s.sem("hn_split")
        fc1_done, mid_ready, fc2_done = s.sem("fc1_done"), s.sem("mid_ready"), s.sem("fc2_done")
        h_loaded = s.two_sems("h_loaded")
        x_loaded, stored = s.two_sems("x_loaded"), s.two_sems("stored")
        y_loaded = [s.sem(f"y_loaded{k}") for k in range(AHEAD)]
        sum_step, total_ready = s.sem("sum_step"), s.sem("total_ready")
        SUMS = 3 + 2

        def run(eng, step):
            with eng.Fori(0, chunks // 2 - 1) as half:
                step(half, 0, 3)
                step(half, 1, 3)
            step(chunks // 2 - 1, 0, 2)
            step(chunks // 2 - 1, 1, 1)

        with nc.Block() as block:

            @block.sync
            def _(sp):
                def load_h(c):
                    sp.dma_start(h[c.parity][:], env["h_tiles"][:, ds(c.index * TPC, TPC), :]).then_inc(h_loaded[c.parity], 16)

                def load_residual(c):
                    sp.dma_start(x[c.parity][:], env["x_tiles"][:, ds(c.index * TPC, TPC), :]).then_inc(x_loaded[c.parity], 16)
                    sp.dma_start(h_again[c.parity][:], env["h_tiles"][:, ds(c.index * TPC, TPC), :]).then_inc(x_loaded[c.parity], 16)

                def step(half, d, left):
                    c = at(half, d)
                    if left > 4:
                        sp.wait_ge(hn_ready, c.index + 3)
                        load_h(at(half, d + 4))
                    sp.wait_ge(total_ready, c.index + 1)
                    sp.dma_start(env["out_tiles"][:, ds(c.index * TPC, TPC), :], total[c.parity][:]).then_inc(stored[c.parity], 16)
                    if left > 2:
                        load_residual(at(half, d + 2))

                for d in range(2):
                    load_h(at(0, d))
                for d in range(2):
                    load_residual(at(0, d))
                for d in range(2):
                    sp.wait_ge(hn_ready, d + 1)
                    load_h(at(0, d + 2))
                with sp.Fori(0, chunks // 2 - 2) as half:
                    step(half, 0, 5)
                    step(half, 1, 5)
                for j in range(chunks - 4, chunks):
                    step(j // 2, j % 2, chunks - j)
                for k in range(2):
                    sp.wait_ge(stored[k], 16 * (chunks // 2 + 1))

            @block.gpsimd
            def _(pool):
                y_tiles = env["y_dram"][0:2 * env["tokens"], :].rearrange("(n p k) d -> p n (k d)", p=P, k=2)

                pool.wait_ge(w1_hi_ready, 1)
                pool.tensor_tensor(w1_lo[:], w1[:], w1_hi[:].bitcast(F32), ALU.subtract).then_inc(w1_split, 1)

                def load_y(quad, k, again):
                    index = AHEAD * quad + k
                    if again:
                        pool.wait_ge(total_ready, index - (AHEAD - 1))
                    pool.dma_start(rows[k][:].rearrange("p (t k) d -> p t (k d)", k=2), y_tiles[:, ds(index * TPC, TPC), :]).then_inc(y_loaded[k], 16)

                for k in range(AHEAD):
                    load_y(0, k, False)
                with pool.Fori(1, chunks // AHEAD) as quad:
                    for k in range(AHEAD):
                        load_y(quad, k, True)

            @block.tensor
            def _(pe):
                def turn(c, early=False):
                    pe.wait_ge(hn_ready, c.index + 1)
                    if not early:
                        pe.wait_ge(hn_split, c.index - 1)
                    for t in range(TPC):
                        last = pe.transpose(t_ps[c.parity][:, t * P:(t + 1) * P], hn[c.parity][:, t, :], ident[:])
                    last.then_inc(hn_turned, 1)

                def fc1(c, k, early=False):
                    pe.wait_ge(hn_split, c.index + 1)
                    if not early:
                        pe.wait_ge(mid_ready, HCH * (c.index - 1) + k + 1)
                    part = slice(k * P, (k + 1) * P)
                    pe.matmul(f_ps[k][:], w1_lo[:, part], hn_hi[c.parity][:], start=True, stop=False)
                    pe.matmul(f_ps[k][:], w1_hi[:, part], hn_lo[c.parity][:], start=False, stop=False)
                    pe.matmul(f_ps[k][:], w1_hi[:, part], hn_hi[c.parity][:], start=False, stop=True).then_inc(fc1_done, 1)

                def fc2(c, t):
                    if t == 0:
                        pe.wait_ge(mid_ready, HCH * (c.index + 1))
                        if not (isinstance(c.index, int) and c.index < 2):
                            pe.wait_ge(total_ready, c.index - 1)
                    for k in range(HCH):
                        last = pe.matmul(o_ps[c.parity][:, t * P:(t + 1) * P], mid[c.parity][:, k, t * P:(t + 1) * P], w2[:, k, :],
                                         start=(k == 0), stop=(k == HCH - 1))
                    if t == TPC - 1:
                        last.then_inc(fc2_done, 1)

                def step(half, d, left):
                    if left > 2:
                        turn(at(half, d + 2))
                    for k in range(HCH):
                        if left > 1:
                            fc1(at(half, d + 1), k)
                        fc2(at(half, d), k)

                turn(at(0, 0), True)
                turn(at(0, 1), True)
                pe.wait_ge(w1_split, 1)
                for k in range(HCH):
                    fc1(at(0, 0), k, True)
                step(0, 0, 3)
                step(0, 1, 3)
                with pe.Fori(1, chunks // 2 - 1) as half:
                    step(half, 0, 3)
                    step(half, 1, 3)
                step(chunks // 2 - 1, 0, 2)
                step(chunks // 2 - 1, 1, 1)

            @block.scalar
            def _(act):
                act.copy(w1_hi[:], w1[:]).then_inc(w1_hi_ready, 1)

                def high(c, early=False):
                    act.wait_ge(hn_turned, c.index + 1)
                    if not early:
                        act.wait_ge(fc1_done, HCH * (c.index - 1))
                    act.copy(hn_hi[c.parity][:], t_ps[c.parity][:]).then_inc(hn_hi_ready, 1)

                def gelu(c, k, early=False):
                    act.wait_ge(fc1_done, HCH * c.index + k + 1)
                    if not early and k == 0:
                        act.wait_ge(fc2_done, c.index - 1)
                    act.activation(mid[c.parity][:, k, :], f_ps[k][:], ACT.Gelu_apprx_tanh, bias=mlp_bias[:, k:k + 1]).then_inc(mid_ready, 1)

                def step(half, d, left, early=False):
                    if left > 2:
                        high(at(half, d + 2))
                    if left > 1:
                        for k in range(HCH):
                            gelu(at(half, d + 1), k, early)

                high(at(0, 0), True)
                high(at(0, 1), True)
                for k in range(HCH):
                    gelu(at(0, 0), k, True)
                step(0, 0, 3, True)
                step(0, 1, 3)
                with act.Fori(1, chunks // 2 - 1) as half:
                    step(half, 0, 3)
                    step(half, 1, 3)
                step(chunks // 2 - 1, 0, 2)

            @block.vector
            def _(dve):
                steps = [0]

                def step_of(ins):
                    steps[0] += 1
                    ins.then_inc(ln_step, 1)
                    dve.wait_ge(ln_step, steps[0])

                parts = ln2_stats[:].rearrange("p (t c) -> p t c", c=6)
                step_of(dve.tensor_tensor(mean[:], parts[:, :, 1], parts[:, :, 4], ALU.add))
                step_of(dve.tensor_tensor(tmp[:], parts[:, :, 1], parts[:, :, 4], ALU.subtract))
                step_of(dve.tensor_tensor(var[:], parts[:, :, 2], parts[:, :, 5], ALU.add))
                step_of(dve.tensor_tensor(tmp[:], tmp[:], tmp[:], ALU.mult))
                step_of(dve.tensor_scalar(var[:], var[:], 1.0 / P, LN_EPS, ALU.mult, ALU.add))
                step_of(dve.tensor_scalar(mean[:], mean[:], 0.5, None, ALU.mult))
                step_of(dve.scalar_tensor_tensor(out=var[:], in0=tmp[:], scalar=0.25, in1=var[:], op0=ALU.mult, op1=ALU.add))
                inverse_root(dve, step_of, var[:], rstd[:], root_bits[:], tmp[:])

                def normalise(c, early=False):
                    dve.wait_ge(h_loaded[c.parity], 16 * (c.turn + 1))
                    if not early:
                        dve.wait_ge(hn_turned, c.index - 1)
                    for t in range(TPC):
                        tile = c.index * TPC + t
                        last = dve.tensor_scalar(hn[c.parity][:, t, :], h[c.parity][:, t, :], mean[:, ds(tile, 1)], rstd[:, ds(tile, 1)],
                                                 ALU.subtract, ALU.mult)
                    last.then_inc(hn_ready, 1)

                def low(c, early=False):
                    dve.wait_ge(hn_hi_ready, c.index + 1)
                    if not early:
                        dve.wait_ge(fc1_done, HCH * (c.index - 1))
                    dve.tensor_tensor(hn_lo[c.parity][:], t_ps[c.parity][:], hn_hi[c.parity][:].bitcast(F32), ALU.subtract).then_inc(hn_split, 1)

                def add_up(quad, d):
                    c = at(2 * quad, d)
                    sums = total[c.parity]
                    dve.wait_ge(x_loaded[c.parity], 32 * (c.turn + 1))
                    dve.wait_ge(stored[c.parity], 16 * (c.turn + 1))
                    done = SUMS * c.index
                    dve.tensor_tensor(sums[:], x[c.parity][:], h_again[c.parity][:], ALU.add).then_inc(sum_step, 1)
                    dve.wait_ge(sum_step, done + 1)
                    dve.tensor_tensor(sums[:], sums[:], fc2_bias[:].unsqueeze(1).to_broadcast([P, TPC, P]), ALU.add).then_inc(sum_step, 1)
                    dve.wait_ge(sum_step, done + 2)
                    dve.wait_ge(fc2_done, c.index + 1)
                    dve.tensor_tensor(sums[:], o_ps[c.parity][:].rearrange("p (t d) -> p t d", d=P), sums[:], ALU.add).then_inc(sum_step, 1)
                    dve.wait_ge(sum_step, done + 3)
                    dve.wait_ge(y_loaded[d % AHEAD], 16 * (quad + d // AHEAD + 1))
                    for k in range(2):
                        for t in range(TPC):
                            last = dve.scalar_tensor_tensor(out=sums[:, t, :], in0=rows[d % AHEAD][:, 2 * t + k, :], scalar=mix_cols[:, ds(c.index * 2 * TPC + 2 * t + k, 1)],
                                                            in1=sums[:, t, :], op0=ALU.mult, op1=ALU.add)
                        last.then_inc(sum_step, 1)
                        dve.wait_ge(sum_step, done + 4 + k)
                    dve.sem_inc(total_ready, 1)

                def step(quad, d, left):
                    if left > 3:
                        normalise(at(2 * quad, d + 3))
                    if left > 2:
                        low(at(2 * quad, d + 2))
                    add_up(quad, d)

                for k in range(2):
                    dve.sem_inc(stored[k], 16)
                normalise(at(0, 0), True)
                normalise(at(0, 1), True)
                low(at(0, 0), True)
                normalise(at(0, 2))
                low(at(0, 1), True)
                step(0, 0, 4)
                with dve.Fori(0, chunks // AHEAD - 1) as quad:
                    for d in range(1, 1 + AHEAD):
                        step(quad, d, 4)
                for d in range(1, AHEAD):
                    step(chunks // AHEAD - 1, d, AHEAD - d)


_ATTN = ("ln1_g", "ln1_b", "ln2_g", "ln2_b", "q_U", "q_V", "q_b", "k_U", "k_V", "k_b", "v_U", "v_V", "v_b",
         "out_U", "out_V", "out_b", "fc1_U", "fc1_V", "fc1_b", "fc2_U", "fc2_V", "fc2_b")
_FFN = ("Wr", "Wg", "Wu", "Wd")


def kernel(**inputs):
    import numpy as _np
    import concourse.bacc as _bacc
    from concourse import mybir as _mybir
    from concourse.bass_utils import run_bass_kernel_spmd as _run

    nc = _bacc.Bacc("TRN2", target_bir_lowering=False, num_devices=1)
    arrays = {}

    def given(name):
        a = _np.ascontiguousarray(inputs[name])
        arrays[f"in_{name}"] = a
        return nc.dram_tensor(f"in_{name}", a.shape, _mybir.dt.from_np(a.dtype), kind="ExternalInput").ap()

    x = given("L0_attn_hidden_states")
    w = {n: given(f"L0_attn_{n}") for n in _ATTN} | {n: given(f"L0_ffn_{n}") for n in _FFN}
    out = nc.dram_tensor("out", arrays["in_L0_attn_hidden_states"].shape, F32, kind="ExternalOutput").ap()
    layer_kernel(nc, x, w, out)
    r = _run(nc, [arrays], core_ids=[0])
    return r.results[0]["out"]
```
